# Optimizing a Trainium2 kernel written in Bass

```python
import numpy as np
import jax
import jax.numpy as jnp

def _softmax(x, axis=-1):
    return jax.nn.softmax(x, axis=axis)

def _gelu(x):
    return jax.nn.gelu(x, approximate=True)

def _silu(x):
    return jax.nn.silu(x)

def _sigmoid(x):
    return jax.nn.sigmoid(x)

def _layernorm(x, axis=-1, eps=1e-05):
    m = jnp.mean(x, axis=axis, keepdims=True)
    v = jnp.var(x, axis=axis, keepdims=True)
    return (x - m) / jnp.sqrt(v + eps)

def _scatter_add(tgt, idx, src, axis=0):
    return tgt.at[idx].add(src)

def _segment_sum(src, seg, n):
    return jax.ops.segment_sum(src, seg, n)
kernel_name = 'mk_flamingo_gated_d2_seqx_r8_ed5061'

def setup_inputs(seed: int=0):
    np.random.seed(seed)
    _w = jnp.asarray

    def _rec_inputs():
        import jax
        import jax.numpy as jnp
        _rk = jax.random.key(seed)
        x = 7.22e-05 + 1 * jax.random.normal(jax.random.fold_in(_rk, 1), (32, 128, 128), jnp.float32)
        _lenS = 128 - jax.random.randint(jax.random.fold_in(_rk, 7), (32,), 0, max(1, 128 // 4) + 1, jnp.int32)
        _lenS2 = 128 - jax.random.randint(jax.random.fold_in(_rk, 8), (32,), 0, max(1, 128 // 4) + 1, jnp.int32)
        _ctx_768P = jax.random.normal(jax.random.fold_in(_rk, 11), (32, 16, 96), jnp.float32)
        _ctx_768c = jax.random.dirichlet(jax.random.fold_in(_rk, 511), 0.3 * jnp.ones((16,), jnp.float32), (32, 128))
        _ctx_768t = jnp.einsum('bsk,bkd->bsd', _ctx_768c, _ctx_768P)
        _ctx_768t = _ctx_768t * jax.lax.rsqrt(jnp.mean(jnp.square(_ctx_768t)) + 1e-12) * 0.953939
        ctx_768 = -0.000191848 + 0.999787 * (_ctx_768t + 0.3 * jax.random.normal(jax.random.fold_in(_rk, 611), (32, 128, 96), jnp.float32))
        _g = jax.random.normal(jax.random.fold_in(_rk, 9001), (2, 2), jnp.float32)
        _g = jnp.sign(_g) * jnp.maximum(jnp.abs(_g), 1.0) + (_g == 0) * 1.0
        g_xattn = _g[0]
        g_ffn = _g[1]
        return (x, ctx_768, g_xattn, g_ffn)
    x, ctx_768, g_xattn, g_ffn = _rec_inputs()

    def _L0_xattn_setup():
        import jax, jax.numpy as jnp
        import numpy as np
        NUM_HEADS = 16
        CLAMP = 10000.0
        key = jax.random.key(seed)
        ks = jax.random.split(key, 8)
        B, Nq, Nkv, Cq, Ckv = (4, 256, 256, 128, 96)
        s_q = 1.0 / np.sqrt(Cq)
        s_kv = 1.0 / np.sqrt(Ckv)
        return {'query': jax.random.normal(ks[0], (B, Nq, Cq), jnp.float32), 'key_value': jax.random.normal(ks[1], (B, Nkv, Ckv), jnp.float32), 'Wq': jax.random.normal(ks[2], (Cq, Cq), jnp.float32) * s_q, 'bq': jnp.zeros((Cq,), jnp.float32), 'Wk': jax.random.normal(ks[3], (Ckv, Cq), jnp.float32) * s_kv, 'bk': jnp.zeros((Cq,), jnp.float32), 'Wv': jax.random.normal(ks[4], (Ckv, Cq), jnp.float32) * s_kv, 'bv': jnp.zeros((Cq,), jnp.float32), 'Wo': jax.random.normal(ks[5], (Cq, Cq), jnp.float32) * s_q, 'bo': jnp.zeros((Cq,), jnp.float32)}
    _L0_xattn_all = _L0_xattn_setup()
    _L0_xattn_in = {k: v for k, v in _L0_xattn_all.items() if k in ('Wq', 'bq', 'Wk', 'bk', 'Wv', 'bv', 'Wo', 'bo')}
    del _L0_xattn_all

    def _L0_ffn_setup():
        import jax, jax.numpy as jnp
        import numpy as np
        E, H, I = (8, 128, 512)
        B, S = (4, 512)
        TOP_K = 2
        key = jax.random.key(seed)
        ks = jax.random.split(key, 4)
        scale = 0.02
        return {'hidden_states': jax.random.normal(ks[0], (B, S, H), jnp.float32), 'gate_w': jax.random.normal(ks[1], (H, E), jnp.float32) * scale, 'gate_b': jnp.zeros((E,), jnp.float32), 'w1': jax.random.normal(ks[2], (E, H, I), jnp.float32) * scale, 'b1': jnp.zeros((E, I), jnp.float32), 'w2': jax.random.normal(ks[3], (E, I, H), jnp.float32) * scale, 'b2': jnp.zeros((E, H), jnp.float32), 'alpha': jnp.ones((E,), jnp.float32)}
    _L0_ffn_all = _L0_ffn_setup()
    _L0_ffn_in = {k: v for k, v in _L0_ffn_all.items() if k in ('gate_w', 'gate_b', 'w1', 'b1', 'w2', 'b2', 'alpha')}
    del _L0_ffn_all

    def _L1_xattn_setup():
        import jax, jax.numpy as jnp
        import numpy as np
        import math
        E = 128
        EV = 128
        FFN = 512
        DINO = 96
        B, S, P = (64, 64, 32)

        def bitnet_linear(x, W, b):
            w_scale = jnp.maximum(jnp.mean(jnp.abs(W)), 1e-05)
            qW = jnp.sign(W) * (jnp.abs(W) > 0.5 * w_scale).astype(W.dtype)
            i_scale = jnp.maximum(jnp.max(jnp.abs(x)), 1e-08) / 127.0
            qx = jnp.clip(jnp.round(x / i_scale), -128.0, 127.0)
            out = jnp.einsum('...i,oi->...o', qx, qW) * (w_scale * i_scale)
            return out + b
        key = jax.random.key(seed)
        ks = iter(jax.random.split(key, 32))

        def lin_w(fin, fout):
            return jax.random.normal(next(ks), (fout, fin), jnp.float32) * math.sqrt(2.0 / fin)
        return {'text_embeddings': jax.random.normal(next(ks), (B, S, E), jnp.float32), 'dinov2_features': jax.random.normal(next(ks), (B, P, DINO), jnp.float32), 'W_d2v': lin_w(DINO, EV), 'b_d2v': jnp.zeros((EV,), jnp.float32), 'W_img': lin_w(EV, E), 'b_img': jnp.zeros((E,), jnp.float32), 'W_txt': lin_w(E, E), 'b_txt': jnp.zeros((E,), jnp.float32), 'W_att0': lin_w(E, E // 2), 'b_att0': jnp.zeros((E // 2,), jnp.float32), 'W_att1': lin_w(E, E // 2), 'b_att1': jnp.zeros((E // 2,), jnp.float32), 'W_f1': lin_w(2 * E, FFN), 'b_f1': jnp.zeros((FFN,), jnp.float32), 'W_f2': lin_w(FFN, E), 'b_f2': jnp.zeros((E,), jnp.float32)}
    _L1_xattn_all = _L1_xattn_setup()
    _L1_xattn_in = {k: v for k, v in _L1_xattn_all.items() if k in ('W_d2v', 'b_d2v', 'W_img', 'b_img', 'W_txt', 'b_txt', 'W_att0', 'b_att0', 'W_att1', 'b_att1', 'W_f1', 'b_f1', 'W_f2', 'b_f2')}
    del _L1_xattn_all

    def _L1_ffn_setup():
        import jax, jax.numpy as jnp
        import numpy as np
        E = 8
        TOP_K = 2
        ROUTE_SCALE = 1.0
        ALPHA = 1.702
        LIMIT = 7.0
        D = 128
        F = 128
        B, S = (2, 128)

        def swiglu(h):
            g = jnp.minimum(h[..., ::2], LIMIT)
            l = jnp.clip(h[..., 1::2], -LIMIT, LIMIT)
            return g * jax.nn.sigmoid(ALPHA * g) * (l + 1.0)
        if __name__ == '__main__':
            out = reference(**setup_inputs())
            print(out.shape, out.dtype)
        key = jax.random.key(seed)
        ks = jax.random.split(key, 16)
        sd = 1.0 / np.sqrt(D)
        sf = 1.0 / np.sqrt(F)
        return {'x': jax.random.normal(ks[0], (B, S, D), jnp.float32), 'gate_w': jax.random.normal(ks[1], (E, D), jnp.float32) * sd, 'gate_b': jax.random.normal(ks[2], (E,), jnp.float32) * 0.01, 'w1': jax.random.normal(ks[3], (E, 2 * F, D), jnp.float32) * sd, 'b1': jax.random.normal(ks[4], (E, 2 * F), jnp.float32) * 0.01, 'w3': jax.random.normal(ks[5], (E, 2 * F, D), jnp.float32) * sd, 'b3': jax.random.normal(ks[6], (E, 2 * F), jnp.float32) * 0.01, 'w2': jax.random.normal(ks[7], (E, D, F), jnp.float32) * sf, 'b2': jax.random.normal(ks[8], (E, D), jnp.float32) * 0.01, 'sw1': jax.random.normal(ks[9], (2 * F, D), jnp.float32) * sd, 'sb1': jax.random.normal(ks[10], (2 * F,), jnp.float32) * 0.01, 'sw3': jax.random.normal(ks[11], (2 * F, D), jnp.float32) * sd, 'sb3': jax.random.normal(ks[12], (2 * F,), jnp.float32) * 0.01, 'sw2': jax.random.normal(ks[13], (D, F), jnp.float32) * sf, 'sb2': jax.random.normal(ks[14], (D,), jnp.float32) * 0.01}
    _L1_ffn_all = _L1_ffn_setup()
    _L1_ffn_in = {k: v for k, v in _L1_ffn_all.items() if k in ('gate_w', 'gate_b', 'w1', 'b1', 'w3', 'b3', 'w2', 'b2', 'sw1', 'sb1', 'sw3', 'sb3', 'sw2', 'sb2')}
    del _L1_ffn_all
    return {'x': x, 'ctx_768': ctx_768, 'g_xattn': g_xattn, 'g_ffn': g_ffn, 'L0_xattn_Wq': _L0_xattn_in['Wq'], 'L0_xattn_bq': _L0_xattn_in['bq'], 'L0_xattn_Wk': _L0_xattn_in['Wk'], 'L0_xattn_bk': _L0_xattn_in['bk'], 'L0_xattn_Wv': _L0_xattn_in['Wv'], 'L0_xattn_bv': _L0_xattn_in['bv'], 'L0_xattn_Wo': _L0_xattn_in['Wo'], 'L0_xattn_bo': _L0_xattn_in['bo'], 'L0_ffn_gate_w': _L0_ffn_in['gate_w'], 'L0_ffn_gate_b': _L0_ffn_in['gate_b'], 'L0_ffn_w1': _L0_ffn_in['w1'], 'L0_ffn_b1': _L0_ffn_in['b1'], 'L0_ffn_w2': _L0_ffn_in['w2'], 'L0_ffn_b2': _L0_ffn_in['b2'], 'L0_ffn_alpha': _L0_ffn_in['alpha'], 'L1_xattn_W_d2v': _L1_xattn_in['W_d2v'], 'L1_xattn_b_d2v': _L1_xattn_in['b_d2v'], 'L1_xattn_W_img': _L1_xattn_in['W_img'], 'L1_xattn_b_img': _L1_xattn_in['b_img'], 'L1_xattn_W_txt': _L1_xattn_in['W_txt'], 'L1_xattn_b_txt': _L1_xattn_in['b_txt'], 'L1_xattn_W_att0': _L1_xattn_in['W_att0'], 'L1_xattn_b_att0': _L1_xattn_in['b_att0'], 'L1_xattn_W_att1': _L1_xattn_in['W_att1'], 'L1_xattn_b_att1': _L1_xattn_in['b_att1'], 'L1_xattn_W_f1': _L1_xattn_in['W_f1'], 'L1_xattn_b_f1': _L1_xattn_in['b_f1'], 'L1_xattn_W_f2': _L1_xattn_in['W_f2'], 'L1_xattn_b_f2': _L1_xattn_in['b_f2'], 'L1_ffn_gate_w': _L1_ffn_in['gate_w'], 'L1_ffn_gate_b': _L1_ffn_in['gate_b'], 'L1_ffn_w1': _L1_ffn_in['w1'], 'L1_ffn_b1': _L1_ffn_in['b1'], 'L1_ffn_w3': _L1_ffn_in['w3'], 'L1_ffn_b3': _L1_ffn_in['b3'], 'L1_ffn_w2': _L1_ffn_in['w2'], 'L1_ffn_b2': _L1_ffn_in['b2'], 'L1_ffn_sw1': _L1_ffn_in['sw1'], 'L1_ffn_sb1': _L1_ffn_in['sb1'], 'L1_ffn_sw3': _L1_ffn_in['sw3'], 'L1_ffn_sb3': _L1_ffn_in['sb3'], 'L1_ffn_sw2': _L1_ffn_in['sw2'], 'L1_ffn_sb2': _L1_ffn_in['sb2']}

def reference(x, ctx_768, g_xattn, g_ffn, L0_xattn_Wq, L0_xattn_bq, L0_xattn_Wk, L0_xattn_bk, L0_xattn_Wv, L0_xattn_bv, L0_xattn_Wo, L0_xattn_bo, L0_ffn_gate_w, L0_ffn_gate_b, L0_ffn_w1, L0_ffn_b1, L0_ffn_w2, L0_ffn_b2, L0_ffn_alpha, L1_xattn_W_d2v, L1_xattn_b_d2v, L1_xattn_W_img, L1_xattn_b_img, L1_xattn_W_txt, L1_xattn_b_txt, L1_xattn_W_att0, L1_xattn_b_att0, L1_xattn_W_att1, L1_xattn_b_att1, L1_xattn_W_f1, L1_xattn_b_f1, L1_xattn_W_f2, L1_xattn_b_f2, L1_ffn_gate_w, L1_ffn_gate_b, L1_ffn_w1, L1_ffn_b1, L1_ffn_w3, L1_ffn_b3, L1_ffn_w2, L1_ffn_b2, L1_ffn_sw1, L1_ffn_sb1, L1_ffn_sw3, L1_ffn_sb3, L1_ffn_sw2, L1_ffn_sb2):
    import jax
    import jax.numpy as jnp

    def _L0_xattn_ref(query, key_value, Wq, bq, Wk, bk, Wv, bv, Wo, bo):
        import jax, jax.numpy as jnp
        import numpy as np
        NUM_HEADS = 16
        CLAMP = 10000.0
        B, Nq, Cq = query.shape
        Nkv = key_value.shape[1]
        H = NUM_HEADS
        D = Cq // H
        scale = D ** (-0.5)
        q = (query @ Wq + bq).reshape(B, Nq, H, D).transpose(0, 2, 1, 3)
        k = (key_value @ Wk + bk).reshape(B, Nkv, H, D).transpose(0, 2, 1, 3)
        v = (key_value @ Wv + bv).reshape(B, Nkv, H, D).transpose(0, 2, 1, 3)
        attn = jnp.einsum('bhqd,bhkd->bhqk', q, k) * scale
        attn = jnp.clip(attn, -CLAMP, CLAMP)
        attn = jax.nn.softmax(attn, axis=-1)
        attn = jnp.where(jnp.any(jnp.isnan(attn)), jnp.asarray(1.0 / Nkv, attn.dtype), attn)
        x = jnp.einsum('bhqk,bhkd->bqhd', attn, v).reshape(B, Nq, Cq)
        return x @ Wo + bo

    def _L0_ffn_ref(hidden_states, gate_w, gate_b, w1, b1, w2, b2, alpha):
        import jax, jax.numpy as jnp
        import numpy as np
        E, H, I = (8, 128, 512)
        B, S = (4, 512)
        TOP_K = 2
        b, s, h = hidden_states.shape
        x = hidden_states.reshape(-1, h)
        logits = x @ gate_w + gate_b
        probs = jax.nn.softmax(logits, axis=-1)
        vals, idx = jax.lax.top_k(probs, TOP_K)
        scores = vals / jnp.sum(vals, axis=-1, keepdims=True)
        onehot = jax.nn.one_hot(idx, E, dtype=x.dtype)
        w_te = jnp.einsum('tk,tke->te', scores, onehot) * alpha
        out = jnp.zeros_like(x)
        for e in range(E):
            hmid = jax.nn.gelu(x @ w1[e] + b1[e], approximate=False)
            y = hmid @ w2[e] + b2[e]
            out = out + w_te[:, e:e + 1] * y
        return out.reshape(b, s, h)

    def _L1_xattn_ref(text_embeddings, dinov2_features, W_d2v, b_d2v, W_img, b_img, W_txt, b_txt, W_att0, b_att0, W_att1, b_att1, W_f1, b_f1, W_f2, b_f2):
        import jax, jax.numpy as jnp
        import numpy as np
        import math
        E = 128
        EV = 128
        FFN = 512
        DINO = 96
        B, S, P = (64, 64, 32)

        def bitnet_linear(x, W, b):
            w_scale = jnp.maximum(jnp.mean(jnp.abs(W)), 1e-05)
            qW = jnp.sign(W) * (jnp.abs(W) > 0.5 * w_scale).astype(W.dtype)
            i_scale = jnp.maximum(jnp.max(jnp.abs(x)), 1e-08) / 127.0
            qx = jnp.clip(jnp.round(x / i_scale), -128.0, 127.0)
            out = jnp.einsum('...i,oi->...o', qx, qW) * (w_scale * i_scale)
            return out + b
        b, s, e = text_embeddings.shape
        vis = bitnet_linear(dinov2_features, W_d2v, b_d2v)
        image_embeds = bitnet_linear(vis, W_img, b_img)
        fused = bitnet_linear(text_embeddings, W_txt, b_txt)
        inv_sqrt_e = 1.0 / math.sqrt(e)
        for Wa, ba in ((W_att0, b_att0), (W_att1, b_att1)):
            kv = bitnet_linear(image_embeds, Wa, ba)
            k = jnp.concatenate([kv, kv], axis=-1)
            scores = jnp.einsum('bse,bpe->bsp', fused, k) * inv_sqrt_e
            attn = jax.nn.softmax(scores, axis=-1)
            fused = fused + 0.1 * jnp.einsum('bsp,bpe->bse', attn, k)
        avg_img = jnp.mean(image_embeds, axis=1, keepdims=True)
        concatenated = jnp.concatenate([fused, jnp.broadcast_to(avg_img, (b, s, e))], axis=-1)
        h = jax.nn.relu(bitnet_linear(concatenated, W_f1, b_f1))
        return bitnet_linear(h, W_f2, b_f2)

    def _L1_ffn_ref(x, gate_w, gate_b, w1, b1, w3, b3, w2, b2, sw1, sb1, sw3, sb3, sw2, sb2):
        import jax, jax.numpy as jnp
        import numpy as np
        E = 8
        TOP_K = 2
        ROUTE_SCALE = 1.0
        ALPHA = 1.702
        LIMIT = 7.0
        D = 128
        F = 128
        B, S = (2, 128)

        def swiglu(h):
            g = jnp.minimum(h[..., ::2], LIMIT)
            l = jnp.clip(h[..., 1::2], -LIMIT, LIMIT)
            return g * jax.nn.sigmoid(ALPHA * g) * (l + 1.0)
        if __name__ == '__main__':
            out = reference(**setup_inputs())
            print(out.shape, out.dtype)
        inp_shape = x.shape
        xt = x.reshape(-1, D)
        logits = xt @ gate_w.T
        scores = jax.nn.softmax(logits.astype(jnp.float32), axis=-1)
        biased = scores + gate_b.astype(jnp.float32)
        idx = jax.lax.top_k(biased, TOP_K)[1]
        weights = (jnp.take_along_axis(scores, idx, axis=-1) * ROUTE_SCALE).astype(x.dtype)
        cw = jnp.sum(jax.nn.one_hot(idx, E, dtype=x.dtype) * weights[..., None], axis=1)
        h1 = jnp.einsum('td,efd->etf', xt, w1) + b1[:, None, :]
        h3 = jnp.einsum('td,efd->etf', xt, w3) + b3[:, None, :]
        a = swiglu(h1 * h3)
        y = jnp.einsum('etf,edf->etd', a, w2) + b2[:, None, :]
        routed = jnp.einsum('te,etd->td', cw, y)
        sh = swiglu((xt @ sw1.T + sb1) * (xt @ sw3.T + sb3))
        shared = sh @ sw2.T + sb2
        return (routed + shared).reshape(inp_shape)
    x = x + jnp.tanh(g_xattn[0]) * _L0_xattn_ref(_layernorm(x, axis=-1), ctx_768, L0_xattn_Wq, L0_xattn_bq, L0_xattn_Wk, L0_xattn_bk, L0_xattn_Wv, L0_xattn_bv, L0_xattn_Wo, L0_xattn_bo)
    x = x + jnp.tanh(g_ffn[0]) * _L0_ffn_ref(_layernorm(x, axis=-1), L0_ffn_gate_w, L0_ffn_gate_b, L0_ffn_w1, L0_ffn_b1, L0_ffn_w2, L0_ffn_b2, L0_ffn_alpha)
    x = x + jnp.tanh(g_xattn[1]) * _L1_xattn_ref(_layernorm(x, axis=-1), ctx_768, L1_xattn_W_d2v, L1_xattn_b_d2v, L1_xattn_W_img, L1_xattn_b_img, L1_xattn_W_txt, L1_xattn_b_txt, L1_xattn_W_att0, L1_xattn_b_att0, L1_xattn_W_att1, L1_xattn_b_att1, L1_xattn_W_f1, L1_xattn_b_f1, L1_xattn_W_f2, L1_xattn_b_f2)
    x = x + jnp.tanh(g_ffn[1]) * _L1_ffn_ref(_layernorm(x, axis=-1), L1_ffn_gate_w, L1_ffn_gate_b, L1_ffn_w1, L1_ffn_b1, L1_ffn_w3, L1_ffn_b3, L1_ffn_w2, L1_ffn_b2, L1_ffn_sw1, L1_ffn_sb1, L1_ffn_sw3, L1_ffn_sb3, L1_ffn_sw2, L1_ffn_sb2)
    return x

_drawn_inputs = setup_inputs


def setup_inputs(seed=0):
    import zlib

    import numpy as np

    out = dict(_drawn_inputs(seed))
    spreads = {'g_ffn': (-1.0, 0.2),
     'L0_xattn_bq': (0.0, 0.1),
     'L0_xattn_bk': (0.0, 2.0),
     'L0_xattn_bv': (0.0, 0.1),
     'L0_xattn_bo': (0.0, 0.1),
     'L0_ffn_gate_b': (0.0, 0.1),
     'L0_ffn_b1': (0.0, 0.309),
     'L0_ffn_b2': (0.0, 0.1),
     'L0_ffn_alpha': (1.0, 0.6),
     'L1_xattn_b_d2v': (0.0, 0.1),
     'L1_xattn_b_img': (0.0, 0.1),
     'L1_xattn_b_txt': (0.0, 0.1),
     'L1_xattn_b_att0': (0.0, 1.058),
     'L1_xattn_b_att1': (0.0, 1.27),
     'L1_xattn_b_f1': (0.0, 0.1),
     'L1_xattn_b_f2': (0.0, 0.1)}
    factors = {'L1_ffn_b1': 8.0,
     'L1_ffn_b3': 8.0,
     'L1_ffn_b2': 23.732,
     'L1_ffn_sb1': 8.0,
     'L1_ffn_sb3': 8.0,
     'L1_ffn_sb2': 8.0}
    for name, (base, spread) in spreads.items():
        noise = np.random.default_rng([zlib.crc32(name.encode()), seed]).standard_normal(out[name].shape)
        drawn = base * np.exp(spread * noise) if base else spread * noise
        out[name] = jnp.asarray(drawn.astype(out[name].dtype))
    for name, factor in factors.items():
        out[name] = (out[name] * factor).astype(out[name].dtype)
    return out
```

```python
from contextlib import ExitStack

import concourse.bass as bass
from concourse import mybir

F32 = mybir.dt.float32
BF16 = mybir.dt.bfloat16
I32 = mybir.dt.int32
U32 = mybir.dt.uint32
ALU = mybir.AluOpType
ACT = mybir.ActivationFunctionType
AX = mybir.AxisListType
RED = bass.bass_isa.ReduceOp

P = 128
NB = 32
CC = 96
NH = 16
DH = P // NH
VW = 32
CLAMP = 10000.0
LN_EPS = 1e-5
SCALE = DH ** -0.5
NE = 8
TOPK = 2
FF = 512
TILES = 72
ROW = P + 1
ROUND = 1.5 * 2.0 ** 23


class Chain:

    def __init__(self, eng, sem, start=0):
        self.eng, self.sem, self.start, self.n = eng, sem, start, 0

    def mark(self, ins):
        self.n += 1
        ins.then_inc(self.sem, 1)
        return self.n

    def need(self, n):
        self.eng.wait_ge(self.sem, self.start + n)

    def link(self, ins):
        self.need(self.mark(ins))


def semaphores(nc, stack, names):
    handles = [nc.alloc_semaphore(name=n) for n in names]
    stack.callback(nc.all_engine_barrier)
    stack.callback(nc.clear_and_free_semaphores, handles)
    return handles


def spread(ap, shape, dim):
    return ap.unsqueeze(dim).broadcast_to(shape)


def ln_statistics(dve, link, st, mean, rstd, work, var_ready, std_ready, done):
    me, mo, ve, vo = st[:, :, 1], st[:, :, 4], st[:, :, 2], st[:, :, 5]
    link(dve.tensor_tensor(mean[:, :], me, mo, ALU.add))
    link(dve.tensor_tensor(work[:, 0, :], me, mo, ALU.subtract))
    link(dve.tensor_scalar(mean[:, :], mean[:, :], 0.5, None, ALU.mult))
    link(dve.tensor_tensor(work[:, 1, :], ve, vo, ALU.add))
    link(dve.tensor_tensor(work[:, 0, :], work[:, 0, :], work[:, 0, :], ALU.mult))
    dve.scalar_tensor_tensor(work[:, 2, :], work[:, 0, :], P / 4.0, work[:, 1, :], ALU.mult, ALU.add)\
       .then_inc(var_ready, 1)
    dve.wait_ge(std_ready, 1)
    dve.reciprocal(rstd[:, :], work[:, 3, :]).then_inc(done, 1)


def build(nc, A, out):
    with ExitStack() as ctx:
        def sb(stack, name, shape, dt=F32):
            return stack.enter_context(nc.sbuf_tensor(name, shape, dt))

        def sems(stack, names):
            return semaphores(nc, stack, names.split())

        score_banks = [ctx.enter_context(nc.psum_tensor(f"banks{i}", [P, 1024], F32)) for i in (0, 2)]
        ps = [b[:, j * 512:j * 512 + 512] for b in score_banks for j in (0, 1)]
        ps += [ctx.enter_context(nc.psum_tensor(f"bank{i}", [P, 512], F32)) for i in range(4, 8)]
        X = sb(ctx, "X", [P, NB, P])
        ident = sb(ctx, "ident", [P, P])
        stats = sb(ctx, "stats", [P, NB, 6])
        mean = sb(ctx, "mean", [P, NB])
        rstd = sb(ctx, "rstd", [P, NB])
        lnwork = sb(ctx, "lnwork", [P, 4, NB])
        gates = sb(ctx, "gates", [P, 4])
        epsc = sb(ctx, "epsc", [P, 1])
        CT = sb(ctx, "CT", [CC, NB, P])
        expsum = sb(ctx, "expsum", [P, 2 * NB])

        xg = [nc.dram_tensor(f"xg{n}", ((TILES + n * NB) * P, ROW), F32).ap() for n in (0, 1)]
        yg = [nc.dram_tensor(f"yg{n}", ((TOPK + n) * NB * P, P), F32).ap() for n in (0, 1)]
        vacant = sb(ctx, "vacant", [P, ROW])

        with ExitStack() as a:
            wq = sb(a, "wq", [P, P]); wk = sb(a, "wk", [CC, P]); wv = sb(a, "wv", [CC, P])
            bq = sb(a, "bq", [P, 1]); bk = sb(a, "bk", [P, 1]); bqs = sb(a, "bqs", [P, 1])
            bv = sb(a, "bv", [P, P])
            headmask = sb(a, "headmask", [P, NH])
            graw = sb(a, "graw", [P, 4])
            cv = sb(a, "cv", [CC, 2, P])
            xn = sb(a, "xn", [P, 2, P])
            xT = sb(a, "xT", [P, 2, P])
            qT = sb(a, "qT", [P, 2, P])
            kT = sb(a, "kT", [P, 2, P])
            kx = sb(a, "kx", [P, 2, NH, P])
            V = sb(a, "V", [P, 2, NH, VW])
            mx = sb(a, "mx", [P, 2, 8])
            D = sb(a, "D", [P, 2, 8, P])
            E = sb(a, "E", [P, 4, 8, P])
            PT = sb(a, "PT", [P, 4, 4 * P])
            oT = sb(a, "oT", [P, 2, 4, P])
            rl = sb(a, "rl", [P, 2, NH])
            O = sb(a, "O", [P, 2, P])
            OF = sb(a, "OF", [P, 2, P])
            wo = sb(a, "wo", [P, P]); bo = sb(a, "bo", [P, P])
            bog = sb(a, "bog", [P, P])
            y = sb(a, "y", [P, P])

            (loaded, ctx_loaded, vacant_set, vacated, gload, zeroed, made, chain_p, chain_v, var_r, std_r, stat_done, prep, bq_r) = sems(
                a, "loaded ctx_loaded vacant_set vacated gload zeroed made chain_p chain_v var_r std_r stat_done prep bq_r")
            with nc.Block() as blk:
                @blk.sync
                def _(sp):
                    sp.dma_start(X[:, :, :], A["x"].rearrange("b p f -> p b f")).then_inc(loaded, 16)
                    sp.dma_start(CT[:, :, :], A["ctx_T"]).then_inc(ctx_loaded, 16)
                    sp.wait_ge(loaded, 16)
                    sp.wait_ge(ctx_loaded, 16)
                    sp.wait_ge(vacant_set, 2)
                    for x in xg:
                        sp.dma_start(x[0:TILES * P, :].rearrange("(j p) c -> p j c", p=P),
                                     spread(vacant[:, :], [P, TILES, ROW], 1)).then_inc(vacated, 16)
                    sp.wait_ge(vacated, 32)
                    sp.wait_ge(gload, 16 * 10)

                @blk.scalar
                def _(act):
                    for dst, src in ((wq[:, :], A["L0_xattn_Wq"]), (wk[:, :], A["L0_xattn_Wk"]),
                                     (wv[:, :], A["L0_xattn_Wv"]),
                                     (bq[:, :], A["L0_xattn_bq"].unsqueeze(1)),
                                     (bk[:, :], A["L0_xattn_bk"].unsqueeze(1)),
                                     (bv[:, :], A["L0_xattn_bv"].partition_broadcast(P)),
                                     (wo[:, :], A["L0_xattn_Wo"]),
                                     (bo[:, :], A["L0_xattn_bo"].partition_broadcast(P)),
                                     (graw[:, 0:2], A["g_xattn"].partition_broadcast(P)),
                                     (graw[:, 2:4], A["g_ffn"].partition_broadcast(P))):
                        act.dma_start(dst, src).then_inc(gload, 16)
                    act.wait_ge(gload, 16 * 10)
                    act.activation(gates[:, :], graw[:, :], ACT.Tanh).then_inc(prep, 1)
                    act.activation(bqs[:, :], bq[:, :], ACT.Copy, scale=SCALE).then_inc(prep, 1)
                    act.wait_ge(var_r, 1)
                    act.wait_ge(zeroed, 1)
                    act.activation(lnwork[:, 3, :], lnwork[:, 2, :], ACT.Sqrt, bias=epsc[:, :], scale=1.0 / P)\
                       .then_inc(std_r, 1)

                @blk.gpsimd
                def _(pool):
                    c = Chain(pool, chain_p)
                    pool.memset(epsc[:, :], LN_EPS).then_inc(zeroed, 1)
                    pool.memset(vacant[:, 0:P], 0.0).then_inc(vacant_set, 1)
                    pool.memset(vacant[:, P:ROW], 2.0 * TOPK * NB * P).then_inc(vacant_set, 1)
                    c.link(pool.memset(ident[:, :], 0.0))
                    c.link(pool.memset(headmask[:, :], 1.0))
                    c.link(pool.affine_select(out=ident[:, :], in_=ident[:, :], compare_op=ALU.not_equal,
                                              fill=1.0, base=0, pattern=[[-1, P]], channel_multiplier=1))
                    c.link(pool.affine_select(out=headmask[:, :], in_=headmask[:, :], compare_op=ALU.is_ge,
                                              fill=0.0, base=0, pattern=[[-DH, NH]], channel_multiplier=1))
                    c.link(pool.affine_select(out=headmask[:, :], in_=headmask[:, :], compare_op=ALU.is_ge,
                                              fill=0.0, base=DH - 1, pattern=[[DH, NH]], channel_multiplier=-1))
                    c.link(pool.memset(V[:, :, :, :], 0.0))
                    c.link(pool.memset(V[:, :, :, DH:DH + 1], 1.0))

                @blk.vector
                def _(dve):
                    dve.wait_ge(loaded, 16)
                    with dve.Fori(0, NB) as b:
                        dve.bn_stats(stats[:, b, :], X[:, b, :]).then_inc(made, 1)
                    dve.wait_ge(made, NB)
                    c = Chain(dve, chain_v)
                    ln_statistics(dve, c.link, stats, mean, rstd, lnwork, var_r, std_r, stat_done)

            (cv_in0, cv_in1, xn_made, inputs_ps, xT_sb, qk_ps, v_ps, q_sb, k_sb, kx_made0, kx_made1, v_sb, scored,
             chain_s, shifted, expd, capped, pT_ps, pT_sb, pv_ps, o_sb, back_ps, normed, of_ps, of_sb, y_ps, y_sb, bog_made, capping) = sems(
                a, "cv_in0 cv_in1 xn_made inputs_ps xT_sb qk_ps v_ps q_sb k_sb kx_made0 kx_made1 v_sb scored "
                   "chain_s shifted expd capped pT_ps pT_sb pv_ps o_sb back_ps normed of_ps of_sb y_ps y_sb bog_made capping")
            cv_in = (cv_in0, cv_in1)
            kx_made = (kx_made0, kx_made1)
            S = ((ps[0], ps[1]), (ps[2], ps[3]))
            BACK_BANK, IN_BANK = ps[4], ps[5]
            GROUP_BANK = (IN_BANK, BACK_BANK, IN_BANK, BACK_BANK)
            OPS, QKV = ps[6], ps[7]

            def links_before(t, k):
                scores, backs, sums = min(k, NB) * 4, max(k - 3, 0), max(k - 4, 0) * 2
                return t * 7 - 11 if k == INNER else scores + backs + sums

            INNER = 4

            def steps(eng, step):
                for t in range(INNER):
                    step(t, t % 2, t)
                with eng.Fori(0, (NB - 8) // 2) as i:
                    for n in (0, 1):
                        step(i * 2 + (INNER + n), n, INNER)
                for t in range(INNER + NB - 8, NB + 4):
                    step(t, t % 2, t)

            def spread_keys(eng, b, u, h, k):
                eng.wait_ge(k_sb, b + 1)
                if k >= 1:
                    eng.wait_ge(scored, b * 2 - 2)
                eng.tensor_tensor(kx[:, u, 8 * h:8 * h + 8, :], spread(kT[:, u, :], [P, 8, P], 1),
                                  spread(headmask[:, 8 * h:8 * h + 8], [P, 8, P], 2), ALU.mult)\
                   .then_inc(kx_made[h], 1)

            def has_scores(k): return k < NB
            def has_values(k): return 2 <= k <= NB + 1
            def has_back(k): return 3 <= k <= NB + 2
            def has_sum(k): return k >= 4
            def has_v(k): return 1 <= k <= NB
            def has_project(k): return k < NB - 2

            with nc.Block() as blk:
                @blk.sync
                def _(sp):
                    sp.dma_start(cv[:, 0, :], A["ctx_T"][:, 0, :]).then_inc(cv_in[0], 16)
                    sp.dma_start(cv[:, 1, :], A["ctx_T"][:, 1, :]).then_inc(cv_in[1], 16)
                    with sp.Fori(1, NB // 2) as i:
                        for u in (0, 1):
                            sp.wait_ge(v_ps, i * 2 + (u - 1))
                            sp.dma_start(cv[:, u, :], A["ctx_T"][:, i * 2 + u, :]).then_inc(cv_in[u], 16)

                @blk.tensor
                def _(pe):
                    def turn_inputs(b, u):
                        pe.wait_ge(xn_made, b + 1)
                        pe.transpose(IN_BANK[:, 0:P], xn[:, u, :], ident[:, :]).then_inc(inputs_ps, 1)

                    def project(b, u):
                        pe.wait_ge(xT_sb, b + 1)
                        pe.matmul(QKV[:, 0:P], wq[:, :], xT[:, u, :], start=True, stop=True)
                        pe.matmul(QKV[:, P:2 * P], wk[:, :], CT[:, b, :], start=True, stop=True).then_inc(qk_ps, 1)

                    def score(b, u, h, k):
                        pe.wait_ge(kx_made[h], b + 1)
                        pe.wait_ge(q_sb, b + 1)
                        if k >= 1:
                            pe.wait_ge(shifted, b * 2 + (h - 1))
                        for j in (0, 1):
                            mm = pe.matmul(S[h][j][:, :], qT[:, u, :],
                                           kx[:, u, 8 * h + 4 * j:8 * h + 4 * j + 4, :], start=True, stop=True)
                        mm.then_inc(scored, 1)

                    def turn_exps(b, u, g):
                        for r in range(4):
                            mm = pe.transpose(GROUP_BANK[g][:, r * P:(r + 1) * P],
                                              E[:, 2 * u + g // 2, 4 * (g % 2) + r, :], ident[:, :])
                        mm.then_inc(pT_ps, 1)

                    def apply_values(b, u, g):
                        pe.wait_ge(pT_sb, b * 4 + (g + 1))
                        for r in range(4):
                            mm = pe.matmul(OPS[VW * r:VW * (r + 1), g * P:(g + 1) * P], V[:, u, 4 * g + r, :],
                                           PT[:, g, r * P:(r + 1) * P], start=True, stop=True)
                        mm.then_inc(pv_ps, 1)

                    def turn_back(b, u):
                        pe.wait_ge(o_sb, b + 1)
                        for g in range(4):
                            mm = pe.transpose(BACK_BANK[:, g * P:(g + 1) * P], oT[:, u, g, :], ident[:, :])
                        mm.then_inc(back_ps, 1)

                    turn_inputs(0, 0)
                    project(0, 0)
                    turn_inputs(1, 1)
                    pe.wait_ge(q_sb, 1)
                    pe.wait_ge(k_sb, 1)
                    project(1, 1)

                    def step(t, u, k):
                        b, w = t - 2, 1 - u
                        if has_scores(k):
                            score(t, u, 0, k)
                            score(t, u, 1, k)
                        if has_values(k):
                            pe.wait_ge(capped, b * 2 + 1)
                            if k >= 3:
                                pe.wait_ge(pT_sb, b * 4)
                            else:
                                pe.wait_ge(xT_sb, 4)
                            turn_exps(b, u, 0)
                        if has_back(k):
                            if k == NB + 2:
                                pe.wait_ge(pT_sb, NB * 4)
                            turn_back(t - 3, w)
                        if has_v(k):
                            pe.wait_ge(q_sb, t + 2 if k < NB - 1 else NB)
                            pe.wait_ge(k_sb, t + 2 if k < NB - 1 else NB)
                        if has_sum(k):
                            pe.wait_ge(y_sb, t - 4)
                        if has_v(k):
                            pe.wait_ge(cv_in[w], (t - 1) * 8 + (16 - 8 * w))
                            pe.matmul(QKV[:, 2 * P:3 * P], cv[:, w, :], wv[:, :], start=True, stop=True)\
                              .then_inc(v_ps, 1)
                        if has_sum(k):
                            pe.wait_ge(normed, t - 3)
                            pe.transpose(QKV[:, 3 * P:4 * P], O[:, u, :], ident[:, :]).then_inc(of_ps, 1)
                        if has_project(k):
                            if has_values(k):
                                pe.wait_ge(pT_sb, b * 4 + 1)
                            else:
                                pe.wait_ge(xT_sb, t + 2)
                            turn_inputs(t + 2, u)
                        if has_values(k):
                            if k >= 3:
                                pe.wait_ge(normed, b)
                            turn_exps(b, u, 1)
                            if k >= 3:
                                pe.wait_ge(o_sb, b)
                            pe.wait_ge(v_sb, b + 1)
                            apply_values(b, u, 0)
                            pe.wait_ge(capped, b * 2 + 2)
                            if has_project(k):
                                pe.wait_ge(xT_sb, b + 5)
                            else:
                                pe.wait_ge(pT_sb, b * 4 + 1)
                            turn_exps(b, u, 2)
                        if has_sum(k):
                            pe.wait_ge(v_sb, t if k <= NB else NB)
                            pe.wait_ge(of_sb, t - 3)
                            pe.matmul(QKV[:, 3 * P:4 * P], OF[:, u, :], wo[:, :], start=True, stop=True)\
                              .then_inc(y_ps, 1)
                        if has_project(k):
                            if k >= 1:
                                pe.wait_ge(v_sb, t)
                            else:
                                pe.wait_ge(q_sb, 2)
                                pe.wait_ge(k_sb, 2)
                            project(t + 2, u)
                        if has_values(k):
                            apply_values(b, u, 1)
                        if has_values(k):
                            turn_exps(b, u, 3)
                            apply_values(b, u, 2)
                            apply_values(b, u, 3)
                    steps(pe, step)

                @blk.scalar
                def _(act):
                    def inputs(b, u, fresh=False):
                        act.wait_ge(inputs_ps, b + 1)
                        if not fresh:
                            act.wait_ge(qk_ps, b - 1)
                        act.activation(xT[:, u, :], IN_BANK[:, 0:P], ACT.Copy).then_inc(xT_sb, 1)

                    def queries_keys(b, u, fresh=False):
                        act.wait_ge(qk_ps, b + 1)
                        if not fresh:
                            act.wait_ge(scored, b * 2 - 2)
                            act.wait_ge(kx_made[0], b - 1)
                            act.wait_ge(kx_made[1], b - 1)
                        act.activation(qT[:, u, :], QKV[:, 0:P], ACT.Identity, bias=bqs[:, :], scale=SCALE)\
                           .then_inc(q_sb, 1)
                        act.activation(kT[:, u, :], QKV[:, P:2 * P], ACT.Identity, bias=bk[:, :])\
                           .then_inc(k_sb, 1)

                    def exponentials(b, u, h, k):
                        act.wait_ge(shifted, b * 2 + (h + 1))
                        if k >= 2:
                            act.wait_ge(pT_ps, b * 4 + (2 * h - 6))
                        act.activation(E[:, 2 * u + h, :, :], D[:, h, :, :], ACT.Exp,
                                       accum_out=expsum[:, bass.ds(b * 2 + h, 1)]).then_inc(expd, 1)

                    def copy_exps(b, g, k):
                        act.wait_ge(pT_ps, b * 4 + (g + 1))
                        if k >= 3:
                            act.wait_ge(pv_ps, b * 4 + (g - 3))
                        act.activation(PT[:, g, :], GROUP_BANK[g][:, :], ACT.Copy).then_inc(pT_sb, 1)

                    def copy_result(b, u, k):
                        act.wait_ge(pv_ps, b * 4 + 4)
                        if k >= 3:
                            act.wait_ge(back_ps, b - 1)
                        act.activation(oT[:, u, :, :], OPS[:, :].rearrange("p (g q) -> p g q", g=4), ACT.Copy)\
                           .then_inc(o_sb, 1)

                    def copy_attention(b, u, k):
                        act.wait_ge(of_ps, b + 1)
                        act.wait_ge(v_sb, b + 4 if k <= NB else NB)
                        act.activation(OF[:, u, :], QKV[:, 3 * P:4 * P], ACT.Copy).then_inc(of_sb, 1)

                    for b in (0, 1):
                        inputs(b, b, fresh=True)
                        queries_keys(b, b, fresh=True)

                    def step(t, u, k):
                        b, w = t - 2, 1 - u
                        if has_values(k):
                            copy_exps(b, 0, k)
                        if has_project(k):
                            inputs(t + 2, u)
                        if has_values(k):
                            copy_exps(b, 1, k)
                        if has_sum(k):
                            copy_attention(t - 4, u, k)
                        if has_values(k):
                            copy_exps(b, 2, k)
                        if has_project(k):
                            queries_keys(t + 2, u)
                        if has_values(k):
                            copy_exps(b, 3, k)
                            copy_result(b, u, k)
                        if has_scores(k):
                            exponentials(t, u, 0, k)
                        if has_scores(k):
                            exponentials(t, u, 1, k)
                    steps(act, step)

                @blk.gpsimd
                def _(pool):
                    def cap(b, u, h):
                        pool.wait_ge(expd, b * 2 + (h + 1))
                        e = E[:, 2 * u + h, :, :]
                        pool.sem_inc(capping, 1)
                        pool.tensor_scalar(e, e, 1.0, None, ALU.min).then_inc(capped, 1)

                    spread_keys(pool, 0, 0, 1, 0)

                    def step(t, u, k):
                        if k < NB - 1:
                            spread_keys(pool, t + 1, 1 - u, 1, k)
                        if has_scores(k):
                            cap(t, u, 0)
                            cap(t, u, 1)
                    steps(pool, step)

                @blk.vector
                def _(dve):
                    def normalise(b, u, fresh=False):
                        if not fresh:
                            dve.wait_ge(inputs_ps, b - 1)
                        dve.tensor_scalar(xn[:, u, :], X[:, b, :], mean[:, bass.ds(b, 1)],
                                          rstd[:, bass.ds(b, 1)], ALU.subtract, ALU.mult).then_inc(xn_made, 1)

                    def maxima(c, b):
                        by_head = [banks[:, :].rearrange("p (h k) -> p h k", h=8) for banks in score_banks]
                        maxed, clipped = [], []
                        for h in (0, 1):
                            dve.wait_ge(scored, b * 2 + (h + 1))
                            maxed.append(c.mark(dve.tensor_reduce(mx[:, h, :], by_head[h], AX.X, ALU.max)))
                        return by_head, maxed

                    def clip_maxima(c, maxed):
                        clipped = []
                        for h in (0, 1):
                            c.need(maxed[h])
                            clipped.append(c.mark(dve.tensor_scalar(mx[:, h, :], mx[:, h, :], CLAMP, -CLAMP,
                                                                    ALU.min, ALU.max)))
                        return clipped

                    def shift(c, b, k, by_head, clipped):
                        for h in (0, 1):
                            if k >= 1:
                                dve.wait_ge(expd, b * 2 + (h - 1))
                            c.need(clipped[h])
                            dve.scalar_tensor_tensor(D[:, h, :, :], by_head[h], -CLAMP,
                                                     spread(mx[:, h, :], [P, 8, P], 2), ALU.max, ALU.subtract)\
                               .then_inc(shifted, 1)

                    def values(b, u, k):
                        dve.wait_ge(v_ps, b + 1)
                        if has_sum(k):
                            dve.wait_ge(of_ps, b - 2)
                        if k >= 3:
                            dve.wait_ge(pv_ps, b * 4 - 4)
                        dve.tensor_tensor(V[:, u, :, 0:DH], QKV[:, 2 * P:3 * P].rearrange("p (h d) -> p h d", h=NH),
                                          bv[:, :].rearrange("p (h d) -> p h d", h=NH), ALU.add).then_inc(v_sb, 1)

                    def invert(c, b, u):
                        dve.wait_ge(back_ps, b + 1)
                        return c.mark(dve.reciprocal(
                            rl[:, u, :], BACK_BANK[:, :].rearrange("p (h d) -> p h d", d=VW)[:, :, DH]))

                    def divide(c, b, u, k, inverted):
                        if k >= 5 or k == INNER:
                            dve.wait_ge(of_ps, b - 1)
                        c.need(inverted)
                        dve.tensor_tensor(O[:, u, :].rearrange("p (h d) -> p h d", h=NH),
                                          BACK_BANK[:, :].rearrange("p (h d) -> p h d", d=VW)[:, :, 0:DH],
                                          spread(rl[:, u, :], [P, NH, DH], 2), ALU.mult).then_inc(normed, 1)

                    def project(b, k):
                        dve.wait_ge(y_ps, b + 1)
                        dve.wait_ge(k_sb, b + 7 if k < NB - 2 else NB)
                        dve.scalar_tensor_tensor(y[:, :], QKV[:, 3 * P:4 * P], gates[:, 0:1], bog[:, :],
                                                 ALU.mult, ALU.add).then_inc(y_sb, 1)

                    def add(c, b):
                        dve.wait_ge(y_sb, b + 1)
                        xb = X[:, b, :]
                        c.link(dve.tensor_tensor(xb, xb, y[:, :], ALU.add))
                        c.link(dve.bn_stats(stats[:, b, :], xb))

                    dve.tensor_scalar(bog[:, :], bo[:, :], gates[:, 0:1], None, ALU.mult).then_inc(bog_made, 1)
                    dve.wait_ge(bog_made, 1)
                    normalise(0, 0, fresh=True)
                    normalise(1, 1, fresh=True)
                    spread_keys(dve, 0, 0, 0, 0)
                    normalise(2, 0)

                    def step(t, u, k):
                        c = Chain(dve, chain_s, links_before(t, k))
                        if k < NB - 1:
                            spread_keys(dve, t + 1, 1 - u, 0, k)
                        if has_scores(k):
                            by_head, maxed = maxima(c, t)
                        if has_back(k):
                            inverted = invert(c, t - 3, 1 - u)
                        if has_scores(k):
                            clipped = clip_maxima(c, maxed)
                        if has_v(k):
                            values(t - 1, 1 - u, k)
                        if has_back(k):
                            divide(c, t - 3, 1 - u, k, inverted)
                        if has_scores(k):
                            shift(c, t, k, by_head, clipped)
                        if has_sum(k):
                            project(t - 4, k)
                        if k < NB - 3:
                            normalise(t + 3, 1 - u)
                        if has_sum(k):
                            add(c, t - 4)
                    steps(dve, step)

        nan_guard(nc, A, X, CT, expsum, stats, gates, ps)

        t = dict(nc=nc, A=A, X=X, ident=ident, stats=stats, mean=mean, rstd=rstd, lnwork=lnwork, epsc=epsc,
                 gates=gates, ps=ps)
        with ExitStack() as a:
            r = Routing(nc, a, "e0", shared=False)
            normalise_and_gate(r, first=True, **t)
            route(r, first=True, **t)
            scatter_rows(r, xg[0], **t)
            gelu_experts(r, xg[0], yg[0], **t)
            combine(r, yg[0], gates[:, 2:3], **t)
        ternary_attention(nc, A, X, CT, ident, stats, mean, rstd, lnwork, epsc, gates, ps)
        with ExitStack() as a:
            r = Routing(nc, a, "e1", shared=True)
            normalise_and_gate(r, first=False, **t)
            route(r, first=False, **t)
            scatter_rows(r, xg[1], **t)
            swiglu_experts(r, xg[1], yg[1], **t)
            combine(r, yg[1], gates[:, 3:4], **t)
        store(nc, X, out)


def store(nc, src, out):
    with nc.semaphore("stored") as stored, nc.Block() as blk:
        @blk.sync
        def _(sp):
            sp.dma_start(out.rearrange("b p f -> p b f"), src[:, :, :]).then_inc(stored, 16)
            sp.wait_ge(stored, 16)


def nan_guard(nc, A, X, CT, expsum, stats, gates, ps):
    with ExitStack() as a:
        sb = lambda name, shape, dt=F32: a.enter_context(nc.sbuf_tensor(name, shape, dt))
        sems = lambda names: semaphores(nc, a, names.split())
        nans = sb("nans", [P, 4])
        flag = sb("flag", [P, 1], I32)
        wo = sb("g_wo", [P, P]); wv = sb("g_wv", [CC, P]); bv = sb("g_bv", [P, 1]); bo = sb("g_bo", [P, P])
        ctxsum = sb("ctxsum", [CC, NB])
        vbar = sb("vbar", [P, NB])
        vrep = sb("vrep", [P, P])
        (chain, row_flag, all_flag, flagged, loaded, vbar_ps, vrep_made, y_ps, added, summed) = sems(
            "g_chain row_flag all_flag flagged g_loaded vbar_ps vrep_made g_y_ps added g_summed")

        with nc.Block() as blk:
            @blk.gpsimd
            def _(pool):
                pool.wait_ge(row_flag, 1)
                pool.partition_all_reduce(nans[:, 3:4], nans[:, 2:3], P, RED.max).then_inc(all_flag, 1)

            @blk.sync
            def _(sp):
                sp.wait_ge(flagged, 1)
                with sp.If(sp.value_load(flag[0:1, 0:1], min_val=0, max_val=1) > 0):
                    for dst, src in ((X[:, :, :], A["x"].rearrange("b p f -> p b f")),
                                     (wo[:, :], A["L0_xattn_Wo"]), (wv[:, :], A["L0_xattn_Wv"]),
                                     (bv[:, :], A["L0_xattn_bv"].unsqueeze(1)),
                                     (bo[:, :], A["L0_xattn_bo"].partition_broadcast(P))):
                        sp.dma_start(dst, src).then_inc(loaded, 16)
                sp.end_ifs()

            @blk.tensor
            def _(pe):
                pe.wait_ge(flagged, 1)
                with pe.If(pe.value_load(flag[0:1, 0:1], min_val=0, max_val=1) > 0):
                    pe.wait_ge(loaded, 16 * 5)
                    pe.wait_ge(summed, 1)
                    pe.matmul(ps[0][:, 0:NB], wv[:, :], ctxsum[:, :], start=True, stop=True).then_inc(vbar_ps, 1)
                    with pe.Fori(0, NB) as b:
                        pe.wait_ge(vrep_made, b + 1)
                        pe.wait_ge(added, b)
                        pe.matmul(ps[1][:, 0:P], vrep[:, :], wo[:, :], start=True, stop=True).then_inc(y_ps, 1)
                pe.end_ifs()

            @blk.vector
            def _(dve):
                c = Chain(dve, chain)
                c.link(dve.tensor_reduce(nans[:, 0:1], expsum[:, :], AX.X, ALU.add))
                c.link(dve.tensor_tensor(nans[:, 1:2], nans[:, 0:1], nans[:, 0:1], ALU.is_equal))
                dve.tensor_scalar(nans[:, 2:3], nans[:, 1:2], -1.0, 1.0, ALU.mult, ALU.add).then_inc(row_flag, 1)
                dve.wait_ge(all_flag, 1)
                dve.tensor_copy(flag[:, :], nans[:, 3:4]).then_inc(flagged, 1)
                dve.wait_ge(flagged, 1)
                with dve.If(dve.value_load(flag[0:1, 0:1], min_val=0, max_val=1) > 0):
                    dve.tensor_reduce(ctxsum[:, :], CT[:, :, :], AX.X, ALU.add).then_inc(summed, 1)
                    dve.wait_ge(vbar_ps, 1)
                    c.link(dve.tensor_scalar(vbar[:, :], ps[0][:, 0:NB], 1.0 / P, bv[:, :], ALU.mult, ALU.add))
                    c.link(dve.tensor_scalar(bo[:, :], bo[:, :], gates[:, 0:1], None, ALU.mult))
                    with dve.Fori(0, NB) as b:
                        dve.tensor_copy(vrep[:, :], vbar[:, bass.ds(b, 1)].broadcast_to([P, P])).then_inc(vrep_made, 1)
                        l = Chain(dve, chain, b * 3 + 5)
                        dve.wait_ge(y_ps, b + 1)
                        xb = X[:, b, :]
                        l.link(dve.scalar_tensor_tensor(xb, ps[1][:, 0:P], gates[:, 0:1], xb, ALU.mult, ALU.add))
                        l.link(dve.tensor_tensor(xb, xb, bo[:, :], ALU.add))
                        l.link(dve.bn_stats(stats[:, b, :], xb))
                        dve.sem_inc(added, 1)
                dve.end_ifs()


class Routing:

    def __init__(self, nc, stack, name, shared):
        sb = lambda n, shape, dt=F32: stack.enter_context(nc.sbuf_tensor(f"{name}_{n}", shape, dt))
        self.name = name
        self.shared = shared
        self.choices = TOPK + int(shared)
        self.logits = sb("logits", [P, NB, NE])
        self.slots = sb("slots", [P, TOPK, NB], U32)
        self.weights = sb("weights", [P, self.choices, NB])
        self.tile_expert = sb("tile_expert", [P, TILES + (NB if shared else 0)], I32)


def named(nc, stack, name):
    sb = lambda n, shape, dt=F32: stack.enter_context(nc.sbuf_tensor(f"{name}_{n}", shape, dt))
    sems = lambda names: semaphores(nc, stack, [f"{name}_{n}" for n in names.split()])
    return sb, sems


def normalise_and_gate(r, nc, A, X, ident, stats, mean, rstd, lnwork, epsc, gates, ps, first):
    with ExitStack() as a:
        sb, sems = named(nc, a, r.name + "g")
        gw = sb("gw", [P, NE]); gb = sb("gb", [P, NE])
        xn = sb("xn", [P, 2, P]); xT = sb("xT", [P, 2, P])
        chain, loaded, var_r, std_r, stat_done, xn_made, xT_ps, xT_sb, gated = sems(
            "chain loaded var_r std_r stat_done xn_made xT_ps xT_sb gated")
        with nc.Block() as blk:
            @blk.sync
            def _(sp):
                sp.dma_start(gw[:, :], A["L0_ffn_gate_w"] if first else A["gate_w_T"]).then_inc(loaded, 16)
                if first:
                    sp.dma_start(gb[:, :], A["L0_ffn_gate_b"].partition_broadcast(P)).then_inc(loaded, 16)

            @blk.vector
            def _(dve):
                c = Chain(dve, chain)
                ln_statistics(dve, c.link, stats, mean, rstd, lnwork, var_r, std_r, stat_done)
                dve.wait_ge(stat_done, 1)
                with dve.Fori(0, NB // 2) as i:
                    for u in (0, 1):
                        b = i * 2 + u
                        dve.wait_ge(xT_ps, b + 1)
                        dve.tensor_scalar(xn[:, u, :], X[:, b, :], mean[:, bass.ds(b, 1)],
                                          rstd[:, bass.ds(b, 1)], ALU.subtract, ALU.mult).then_inc(xn_made, 1)
                dve.wait_ge(loaded, 32 if first else 16)
                dve.wait_ge(gated, NB)
                lg = ps[7][:, 0:NB * NE].rearrange("p (b e) -> p b e", e=NE)
                if first:
                    c.link(dve.tensor_tensor(r.logits[:, :, :], lg, spread(gb[:, :], [P, NB, NE], 1), ALU.add))
                else:
                    c.link(dve.tensor_copy(r.logits[:, :, :], lg))

            @blk.scalar
            def _(act):
                act.wait_ge(var_r, 1)
                act.activation(lnwork[:, 3, :], lnwork[:, 2, :], ACT.Sqrt, bias=epsc[:, :], scale=1.0 / P)\
                   .then_inc(std_r, 1)
                with act.Fori(0, NB // 2) as i:
                    for u in (0, 1):
                        act.wait_ge(xT_ps, i * 2 + (u + 3))
                        act.activation(xT[:, u, :], ps[5 + u][:, 0:P], ACT.Copy).then_inc(xT_sb, 1)

            @blk.tensor
            def _(pe):
                pe.sem_inc(xT_ps, 2)
                def turn(b, u):
                    pe.wait_ge(xn_made, b + 1)
                    pe.transpose(ps[5 + u][:, 0:P], xn[:, u, :], ident[:, :]).then_inc(xT_ps, 1)

                def gate(b, u):
                    pe.wait_ge(xT_sb, b + 1)
                    pe.matmul(ps[7][:, bass.ds(b * NE, NE)], xT[:, u, :], gw[:, :], start=True, stop=True)\
                      .then_inc(gated, 1)
                pe.wait_ge(loaded, 32 if first else 16)
                turn(0, 0)
                turn(1, 1)
                with pe.Fori(0, NB // 2 - 1) as i:
                    for u in (0, 1):
                        gate(i * 2 + u, u)
                        turn(i * 2 + (u + 2), u)
                gate(NB - 2, 0)
                gate(NB - 1, 1)


def route(r, nc, A, X, ident, stats, mean, rstd, lnwork, epsc, gates, ps, first):
    with ExitStack() as a:
        sb, sems = named(nc, a, r.name + "r")
        rev = sb("rev", [P, NE])
        jota = sb("jota", [P, TILES])
        before = sb("before", [P, P], BF16)
        ones = sb("ones", [P, P], BF16)
        extra = sb("extra", [P, NE])
        probs = sb("probs", [P, NB, NE]); choice = sb("choice", [P, NB, NE]); w3 = sb("w3", [P, NB, NE])
        hot = sb("hot", [P, TOPK, NB, NE])
        best = sb("best", [P, 4, NB])
        chosen = sb("chosen", [P, NB, NE], BF16)
        cum = sb("cum", [P, 2, NE, NB])
        each = sb("each", [P, NE, NB])
        small = sb("small", [P, 6, NE])
        cmp = sb("cmp", [P, TILES, NE])
        slotf = sb("slotf", [P, TOPK, NB])
        loaded, made, chain, shifted, expd, chosen_r, counted, pool_chain = sems(
            "loaded made chain shifted expd chosen_r counted pool_chain")
        B3 = [P, NB, NE]
        with nc.Block() as blk:
            @blk.sync
            def _(sp):
                src = A["L0_ffn_alpha"] if first else A["L1_ffn_gate_b"]
                sp.dma_start(extra[:, :], src.partition_broadcast(P)).then_inc(loaded, 16)

            @blk.gpsimd
            def _(pool):
                c = Chain(pool, pool_chain)
                c.link(pool.iota(rev[:, :], pattern=[[-1, NE]], base=NE, channel_multiplier=0,
                                 allow_small_or_imprecise_dtypes=True))
                c.link(pool.iota(jota[:, :], pattern=[[1, TILES]], base=0, channel_multiplier=0,
                                 allow_small_or_imprecise_dtypes=True))
                c.link(pool.memset(ones[:, :], 1.0))
                c.link(pool.memset(before[:, :], 1.0))
                c.link(pool.affine_select(out=before[:, :], in_=before[:, :], compare_op=ALU.is_ge, fill=0.0,
                                          base=-1, pattern=[[1, P]], channel_multiplier=-1))
                pool.sem_inc(made, 1)

            @blk.scalar
            def _(act):
                act.wait_ge(shifted, 1)
                act.activation(probs[:, :, :], probs[:, :, :], ACT.Exp).then_inc(expd, 1)

            @blk.tensor
            def _(pe):
                pe.wait_ge(made, 1)
                pe.wait_ge(chosen_r, 1)
                m = chosen[:, :, :]
                pe.matmul(ps[0][:, 0:NB * NE], before[:, :], m, start=True, stop=True)
                pe.matmul(ps[1][:, 0:NB * NE], ones[:, :], m, start=True, stop=True).then_inc(counted, 1)

            @blk.vector
            def _(dve):
                c = Chain(dve, chain)
                tt, ts = dve.tensor_tensor, dve.tensor_scalar
                L = c.link
                m = best[:, 0, :]
                L(dve.tensor_reduce(m, r.logits[:, :, :], AX.X, ALU.max))
                tt(probs[:, :, :], r.logits[:, :, :], spread(m, B3, 2), ALU.subtract).then_inc(shifted, 1)
                dve.wait_ge(expd, 1)
                L(dve.tensor_reduce(m, probs[:, :, :], AX.X, ALU.add))
                L(dve.reciprocal(m, m))
                L(tt(probs[:, :, :], probs[:, :, :], spread(m, B3, 2), ALU.mult))
                dve.wait_ge(loaded, 16)
                dve.wait_ge(made, 1)
                if first:
                    L(dve.tensor_copy(choice[:, :, :], probs[:, :, :]))
                else:
                    L(tt(choice[:, :, :], probs[:, :, :], spread(extra[:, :], B3, 1), ALU.add))
                for k in range(TOPK):
                    h = hot[:, k, :, :]
                    if k:
                        L(ts(w3[:, :, :], hot[:, 0, :, :], -1.0, 1.0, ALU.mult, ALU.add))
                        L(tt(choice[:, :, :], choice[:, :, :], w3[:, :, :], ALU.mult))
                        L(dve.scalar_tensor_tensor(choice[:, :, :], hot[:, 0, :, :], -3.0e38, choice[:, :, :],
                                                   ALU.mult, ALU.add))
                    L(dve.tensor_reduce(m, choice[:, :, :], AX.X, ALU.max))
                    L(tt(w3[:, :, :], choice[:, :, :], spread(m, B3, 2), ALU.is_equal))
                    L(tt(w3[:, :, :], w3[:, :, :], spread(rev[:, :], B3, 1), ALU.mult))
                    L(dve.tensor_reduce(best[:, 1, :], w3[:, :, :], AX.X, ALU.max))
                    L(tt(h, spread(rev[:, :], B3, 1), spread(best[:, 1, :], B3, 2), ALU.is_equal))
                tt(chosen[:, :, :], hot[:, 0, :, :], hot[:, 1, :, :], ALU.add).then_inc(chosen_r, 1)
                for k in range(TOPK):
                    L(tt(w3[:, :, :], hot[:, k, :, :], probs[:, :, :], ALU.mult))
                    L(dve.tensor_reduce(r.weights[:, k, :], w3[:, :, :], AX.X, ALU.add))
                if first:
                    L(tt(best[:, 2, :], r.weights[:, 0, :], r.weights[:, 1, :], ALU.add))
                    L(dve.reciprocal(best[:, 2, :], best[:, 2, :]))
                    for k in range(TOPK):
                        L(tt(r.weights[:, k, :], r.weights[:, k, :], best[:, 2, :], ALU.mult))
                        L(tt(w3[:, :, :], hot[:, k, :, :], spread(extra[:, :], B3, 1), ALU.mult))
                        L(dve.tensor_reduce(best[:, 3, :], w3[:, :, :], AX.X, ALU.add))
                        L(tt(r.weights[:, k, :], r.weights[:, k, :], best[:, 3, :], ALU.mult))
                dve.wait_ge(counted, 1)
                L(dve.tensor_copy(each[:, :, :], ps[1][:, 0:NB * NE].rearrange("p (b e) -> p e b", e=NE)))
                L(dve.tensor_copy(cum[:, 0, :, :], each[:, :, :]))
                src, dst, d = 0, 1, 1
                while d < NB:
                    L(dve.tensor_copy(cum[:, dst, :, 0:d], cum[:, src, :, 0:d]))
                    L(tt(cum[:, dst, :, d:NB], cum[:, src, :, d:NB], cum[:, src, :, 0:NB - d], ALU.add))
                    src, dst, d = dst, src, 2 * d
                ntile, end, start = small[:, 0, :], small[:, 1, :], small[:, 2, :]
                L(ts(ntile, cum[:, src, :, NB - 1], (P - 1) / 2.0, 1.0 / P, ALU.add, ALU.mult))
                L(ts(ntile, ntile, ROUND, -ROUND, ALU.add, ALU.add))
                L(dve.tensor_copy(end, ntile))
                for d in (1, 2, 4):
                    L(dve.tensor_copy(small[:, 3, :], end))
                    L(tt(small[:, 1, d:NE], small[:, 3, d:NE], small[:, 3, 0:NE - d], ALU.add))
                L(tt(start, end, ntile, ALU.subtract))
                L(tt(cum[:, dst, :, :], cum[:, src, :, :], each[:, :, :], ALU.subtract))
                L(dve.scalar_tensor_tensor(cum[:, dst, :, :], spread(start, [P, NE, NB], 2), float(P),
                                           cum[:, dst, :, :], ALU.mult, ALU.add))
                L(tt(w3[:, :, :], ps[0][:, 0:NB * NE].rearrange("p (b e) -> p b e", e=NE),
                     cum[:, dst, :, :].rearrange("p e b -> p b e"), ALU.add))
                for k in range(TOPK):
                    L(tt(choice[:, :, :], hot[:, k, :, :], w3[:, :, :], ALU.mult))
                    L(dve.tensor_reduce(slotf[:, k, :], choice[:, :, :], AX.X, ALU.add))
                L(dve.tensor_copy(r.slots[:, :, :], slotf[:, :, :]))
                C3 = [P, TILES, NE]
                L(tt(cmp[:, :, :], spread(jota[:, :], C3, 2), spread(end, C3, 1), ALU.is_ge))
                L(dve.tensor_reduce(jota[:, :], cmp[:, :, :], AX.X, ALU.add))
                L(ts(r.tile_expert[:, 0:TILES], jota[:, :], float(NE - 1), None, ALU.min))
                if r.shared:
                    L(dve.memset(r.weights[:, TOPK, :], 1.0))
                    L(dve.memset(r.tile_expert[:, TILES:TILES + NB], NE))


def scatter_rows(r, xg, nc, A, X, ident, stats, mean, rstd, lnwork, epsc, gates, ps):
    with ExitStack() as a:
        sb, sems = named(nc, a, r.name + "s")
        rows = sb("rows", [P, 2, r.choices, ROW])
        index = sb("index", [P, 2, TOPK], U32)
        nmr = sb("nmr", [P, NB])
        token = sb("token", [P, 1])
        base = sb("base", [P, NB])
        prep, chain, row0, row1, row2, begun = sems("prep chain row0 row1 row2 begun")
        sent = [sems("sent00 sent01 sent02"), sems("sent10 sent11 sent12")]
        with nc.Block() as blk:
            @blk.vector
            def _(dve):
                c = Chain(dve, chain)
                c.link(dve.scalar_tensor_tensor(nmr[:, :], mean[:, :], -1.0, rstd[:, :], ALU.mult, ALU.mult))
                dve.wait_ge(prep, 2)
                c.link(dve.tensor_scalar(base[:, :], base[:, :], token[:, :], None, ALU.add))
                dve.sem_inc(prep, 1)
                with dve.Fori(0, NB // 2) as i:
                    for u in (0, 1):
                        b = i * 2 + u
                        for k in range(r.choices):
                            dve.wait_ge(sent[u][k], i * 16)
                        dve.tensor_copy(rows[:, u, 0, P:ROW], base[:, bass.ds(b, 1)])
                        for k in range(1, r.choices):
                            dve.tensor_scalar(rows[:, u, k, P:ROW], base[:, bass.ds(b, 1)], float(k * NB * P), None,
                                              ALU.add)
                        dve.tensor_copy(index[:, u, :], r.slots[:, :, bass.ds(b, 1)])
                        dve.tensor_scalar(rows[:, u, 0, 0:P], X[:, b, :], mean[:, bass.ds(b, 1)],
                                          rstd[:, bass.ds(b, 1)], ALU.subtract, ALU.mult).then_inc(row0, 1)

            @blk.scalar
            def _(act):
                with act.Fori(0, NB // 2) as i:
                    for u in (0, 1):
                        act.wait_ge(row0, i * 2 + (u + 1))
                        act.activation(rows[:, u, 1, 0:P], rows[:, u, 0, 0:P], ACT.Copy).then_inc(row1, 1)
                        if r.shared:
                            act.activation(rows[:, u, 2, 0:P], rows[:, u, 0, 0:P], ACT.Copy).then_inc(row2, 1)

            if r.shared:
                @blk.sync
                def _(sp):
                    with sp.Fori(0, NB // 2) as i:
                        for u in (0, 1):
                            sp.wait_ge(row2, i * 2 + (u + 1))
                            sp.dma_start(xg[bass.ds(i * (2 * P) + (TILES + u) * P, P), :], rows[:, u, 2, :])\
                              .then_inc(sent[u][2], 16)
                    for u in (0, 1):
                        sp.wait_ge(sent[u][2], NB // 2 * 16)

            @blk.gpsimd
            def _(pool):
                pool.iota(token[:, :], pattern=[[0, 1]], base=0, channel_multiplier=1,
                          allow_small_or_imprecise_dtypes=True).then_inc(prep, 1)
                pool.iota(base[:, :], pattern=[[P, NB]], base=0, channel_multiplier=0,
                          allow_small_or_imprecise_dtypes=True).then_inc(prep, 1)
                with pool.Fori(0, NB // 2) as i:
                    for u in (0, 1):
                        for k, ready in enumerate((row0, row1)):
                            pool.wait_ge(ready, i * 2 + (u + 1))
                            pool.sem_inc(begun, 1)
                            pool.indirect_dma_start(xg, bass.IndirectOffsetOnAxis(index[:, u, k:k + 1], 0),
                                                    rows[:, u, k, :], None, bounds_check=TILES * P - 1)\
                                .then_inc(sent[u][k], 16)
                for u in (0, 1):
                    for k in range(TOPK):
                        pool.wait_ge(sent[u][k], NB // 2 * 16)


def rows_in(j, q):
    return (j - q) * 4 + 16


def gelu_experts(r, xg, yg, nc, A, X, ident, stats, mean, rstd, lnwork, epsc, gates, ps):
    with ExitStack() as a:
        sb, sems = named(nc, a, r.name + "x")
        NC = FF // P
        w1 = sb("w1", [P, NE, FF])
        w2 = sb("w2", [P, NE, NC, P])
        b1 = sb("b1", [P, NE, FF])
        b2 = sb("b2", [P, NE, P])
        rows = sb("rows", [P, 4, ROW])
        xT = sb("xT", [P, 2, P])
        h = sb("h", [P, 2, FF]); g = sb("g", [P, 2, FF]); gT = sb("gT", [P, 2, FF])
        y = sb("y", [P, 2, P]); yrow = sb("yrow", [P, 2], U32)
        wload, xT_ps, xT_sb, h_ps, h_sb, g_sb, gT_ps, gT_sb, y_ps, y_sb, id_sb, begun = sems(
            "wload xT_ps xT_sb h_ps h_sb g_sb gT_ps gT_sb y_ps y_sb id_sb begun")
        row_in = sems("row_in0 row_in1 row_in2 row_in3")
        sent = sems("sent0 sent1")
        X_BANK, H_BANK, GT_BANK, Y_BANK = (ps[0], ps[1]), (ps[2], ps[3]), (ps[4], ps[5]), (ps[6], ps[7])
        with nc.Block() as blk:
            @blk.sync
            def _(sp):
                sp.dma_start(w1[:, :, :], A["L0_ffn_w1"].rearrange("e d f -> d e f")).then_inc(wload, 16)
                sp.dma_start(w2[:, :, :, :], A["L0_ffn_w2"].rearrange("e (c i) d -> i e c d", i=P)).then_inc(wload, 16)
                for q in range(4):
                    sp.dma_start(rows[:, q, :], xg[q * P:(q + 1) * P, :]).then_inc(row_in[q], 16)
                with sp.Fori(1, TILES // 4) as i:
                    for q in range(4):
                        sp.wait_ge(xT_ps, i * 4 + (q - 3))
                        sp.wait_ge(id_sb, i * 4 + (q - 3))
                        sp.dma_start(rows[:, q, :], xg[bass.ds(i * (4 * P) + q * P, P), :]).then_inc(row_in[q], 16)

            @blk.scalar
            def _(act):
                act.dma_start(b1[:, :, :], A["L0_ffn_b1"].partition_broadcast(P)).then_inc(wload, 16)
                act.dma_start(b2[:, :, :], A["L0_ffn_b2"].partition_broadcast(P)).then_inc(wload, 16)

                def turned(j, u):
                    act.wait_ge(xT_ps, j + 1)
                    act.activation(xT[:, u, :], X_BANK[u][:, 0:P], ACT.Copy).then_inc(xT_sb, 1)

                def gelu(j, u):
                    act.wait_ge(h_sb, j + 1)
                    act.activation(g[:, u, :], h[:, u, :], ACT.Gelu).then_inc(g_sb, 1)

                def hidden(j, u):
                    act.wait_ge(gT_ps, j + 1)
                    act.activation(gT[:, u, :], GT_BANK[u][:, :], ACT.Copy).then_inc(gT_sb, 1)

                turned(0, 0)
                turned(1, 1)
                gelu(0, 0)
                with act.Fori(0, (TILES - 2) // 2) as i:
                    for n in (0, 1):
                        j, u = i * 2 + (n + 1), (n + 1) % 2
                        hidden(j - 1, 1 - u)
                        act.wait_ge(h_ps, j)
                        turned(j + 1, 1 - u)
                        gelu(j, u)
                hidden(TILES - 2, 0)
                gelu(TILES - 1, 1)
                hidden(TILES - 1, 1)

            @blk.tensor
            def _(pe):
                def turn(j, u, q):
                    pe.wait_ge(row_in[q], rows_in(j, q))
                    pe.transpose(X_BANK[u][:, 0:P], rows[:, q, 0:P], ident[:, :]).then_inc(xT_ps, 1)

                def first_product(j, u):
                    e = pe.value_load(r.tile_expert[0:1, bass.ds(j, 1)], min_val=0, max_val=NE - 1)
                    pe.wait_ge(xT_sb, j + 1)
                    pe.matmul(H_BANK[u][:, :], xT[:, u, :], w1[:, e, :], start=True, stop=True).then_inc(h_ps, 1)

                def turn_hidden(j, u):
                    pe.wait_ge(g_sb, j + 1)
                    for c in range(NC):
                        mm = pe.transpose(GT_BANK[u][:, c * P:(c + 1) * P], g[:, u, c * P:(c + 1) * P], ident[:, :])
                    mm.then_inc(gT_ps, 1)

                def second_product(j, u):
                    e = pe.value_load(r.tile_expert[0:1, bass.ds(j, 1)], min_val=0, max_val=NE - 1)
                    pe.wait_ge(gT_sb, j + 1)
                    for c in range(NC):
                        mm = pe.matmul(Y_BANK[u][:, 0:P], gT[:, u, c * P:(c + 1) * P], w2[:, e, c, :],
                                       start=(c == 0), stop=(c == NC - 1))
                    mm.then_inc(y_ps, 1)

                pe.wait_ge(wload, 64)
                turn(0, 0, 0)
                turn(1, 1, 1)
                first_product(0, 0)
                with pe.Fori(0, (TILES - 4) // 4) as i:
                    for n in range(4):
                        j, u = i * 4 + (n + 1), (n + 1) % 2
                        turn_hidden(j - 1, 1 - u)
                        turn(j + 1, 1 - u, (n + 2) % 4)
                        first_product(j, u)
                        second_product(j - 1, 1 - u)
                for j in range(TILES - 3, TILES):
                    u = j % 2
                    turn_hidden(j - 1, 1 - u)
                    if j + 1 < TILES:
                        turn(j + 1, 1 - u, (j + 1) % 4)
                    first_product(j, u)
                    second_product(j - 1, 1 - u)
                turn_hidden(TILES - 1, 1)
                second_product(TILES - 1, 1)

            @blk.vector
            def _(dve):
                def hidden(j, u, fresh=False):
                    e = dve.value_load(r.tile_expert[0:1, bass.ds(j, 1)], min_val=0, max_val=NE - 1)
                    dve.wait_ge(h_ps, j + 1)
                    if not fresh:
                        dve.wait_ge(g_sb, j - 1)
                    dve.tensor_tensor(h[:, u, :], H_BANK[u][:, :], b1[:, e, :], ALU.add).then_inc(h_sb, 1)

                def output(j, u, q, fresh=False):
                    e = dve.value_load(r.tile_expert[0:1, bass.ds(j, 1)], min_val=0, max_val=NE - 1)
                    if not fresh:
                        dve.wait_ge(sent[u], (j - u) * 8)
                    dve.wait_ge(row_in[q], rows_in(j, q))
                    dve.tensor_copy(yrow[:, u:u + 1], rows[:, q, P:ROW]).then_inc(id_sb, 1)
                    dve.wait_ge(y_ps, j + 1)
                    dve.tensor_tensor(y[:, u, :], Y_BANK[u][:, 0:P], b2[:, e, :], ALU.add).then_inc(y_sb, 1)

                dve.wait_ge(wload, 64)
                hidden(0, 0, fresh=True)
                hidden(1, 1, fresh=True)
                output(0, 0, 0, fresh=True)
                hidden(2, 0)
                output(1, 1, 1, fresh=True)
                with dve.Fori(0, (TILES - 4) // 4) as i:
                    for n in range(4):
                        j, u = i * 4 + (n + 3), (n + 3) % 2
                        hidden(j, u)
                        output(j - 1, 1 - u, (n + 2) % 4)
                hidden(TILES - 1, 1)
                output(TILES - 2, 0, (TILES - 2) % 4)
                output(TILES - 1, 1, (TILES - 1) % 4)

            @blk.gpsimd
            def _(pool):
                with pool.Fori(0, TILES // 2) as i:
                    for u in (0, 1):
                        pool.wait_ge(id_sb, i * 2 + (u + 1))
                        pool.wait_ge(y_sb, i * 2 + (u + 1))
                        pool.sem_inc(begun, 1)
                        pool.indirect_dma_start(yg, bass.IndirectOffsetOnAxis(yrow[:, u:u + 1], 0), y[:, u, :], None,
                                                bounds_check=TOPK * NB * P - 1, oob_is_err=False)\
                            .then_inc(sent[u], 16)
                for u in (0, 1):
                    pool.wait_ge(sent[u], TILES // 2 * 16)


def combine(r, yg, gate, nc, A, X, ident, stats, mean, rstd, lnwork, epsc, gates, ps):
    W = 8
    with ExitStack() as a:
        sb, sems = named(nc, a, r.name + "c")
        y = sb("y", [P, NB // W, r.choices, W, P])
        chain, wdone = sems("chain wdone")
        y_in = sems(" ".join(f"y_in{n}" for n in range(NB // W)))
        with nc.Block() as blk:
            @blk.sync
            def _(sp):
                for n in range(NB // W):
                    for k in range(r.choices):
                        t0 = (k * NB + n * W) * P
                        sp.dma_start(y[:, n, k, :, :], yg[t0:t0 + W * P, :].rearrange("(b p) f -> p b f", p=P))\
                          .then_inc(y_in[n], 16)

            @blk.vector
            def _(dve):
                dve.tensor_scalar(r.weights[:, :, :], r.weights[:, :, :], gate, None, ALU.mult).then_inc(wdone, 1)
                dve.wait_ge(wdone, 1)
                for n in range(NB // W):
                    dve.wait_ge(y_in[n], 16 * r.choices)
                    with dve.Fori(0, W) as i:
                        b = i + n * W
                        c = Chain(dve, chain, (i + n * W) * (r.choices + 1))
                        for k in range(r.choices):
                            c.link(dve.scalar_tensor_tensor(X[:, b, :], y[:, n, k, i, :],
                                                            r.weights[:, k, bass.ds(b, 1)], X[:, b, :],
                                                            ALU.mult, ALU.add))
                        c.link(dve.bn_stats(stats[:, b, :], X[:, b, :]))


BIT_WEIGHTS = (("d2v", CC * P, 0, P), ("img", P * P, P, 2 * P), ("txt", P * P, 2 * P, 3 * P),
               ("att0", P * P // 2, 3 * P, 7 * P // 2), ("att1", P * P // 2, 7 * P // 2, 4 * P),
               ("f1", 2 * P * FF, 4 * P, 12 * P), ("f2", FF * P, 12 * P, 16 * P))
D2V, IMG_W, TXT, ATT0, ATT1, F1, F2 = range(7)
CTX_A, VIS_A, IMG_A, XN_A, CAT_A, HID_A = range(6)
QMAX = 127.0
GB = 4
G = NB // GB
GW = GB * P


def ternary_attention(nc, A, X, CT, ident, stats, mean, rstd, lnwork, epsc, gates, ps):
    with ExitStack() as a:
        sb, sems = named(nc, a, "t")
        W = sb("W", [P, 16 * P])
        neg = sb("neg", [P, 8 * P])
        qW = sb("qW", [P, 16 * P], BF16)
        katt = sb("katt", [P, 2, 2, P // 2], BF16)
        bias = sb("bias", [P, 9])
        rowbias = sb("rowbias", [P, 3, P])
        wsum = sb("wsum", [P, 7]); wsc = sb("wsc", [P, 7]); thr = sb("thr", [P, 2, 7])
        counts = sb("counts", [P, 7])
        amax = sb("amax", [P, 6]); gmax = sb("gmax", [P, 6])
        isc = sb("isc", [P, 6]); inv = sb("inv", [P, 6])
        osc = sb("osc", [P, 7])
        partmax = sb("partmax", [P, 4 * G])
        hsc = sb("hsc", [P, 1]); hbias = sb("hbias", [P, 4])
        hraw = sb("hraw", [P, 4])
        gf2 = sb("gf2", [P, 1]); gb2 = sb("gb2", [P, P])
        identb = sb("identb", [P, P], BF16)
        scaled = sb("scaled", [P, 2, GW])
        qin = sb("qin", [P, NB, P], BF16)
        vis = sb("vis", [P, NB, P]); img = sb("img", [P, NB, P])
        imgq = sb("imgq", [P, NB, P], BF16)
        K = [sb("K0", [P, NB, P]), sb("K1", [P, NB, P])]
        avg = sb("avg", [P, NB]); avgq = sb("avgq", [P, NB], BF16)
        fused = vis
        xn = img

        (wload, chain, wsum_r, wtot_r, amax_r, gmax_r, scale_r, var_r, std_r, stat_done, q_ready, identb_made,
         pool_chain) = sems("wload chain wsum_r wtot_r amax_r gmax_r scale_r var_r std_r stat_done q_ready "
                            "identb_made pool_chain")

        def scale_inputs(dve, L, k, layers, n):
            dve.wait_ge(gmax_r, n)
            L(dve.tensor_scalar(isc[:, k:k + 1], gmax[:, k:k + 1], 1e-8, 1.0 / QMAX, ALU.max, ALU.mult))
            L(dve.reciprocal(inv[:, k:k + 1], isc[:, k:k + 1]))
            for w in layers:
                L(dve.tensor_tensor(osc[:, w:w + 1], isc[:, k:k + 1], wsc[:, w:w + 1], ALU.mult))
            dve.sem_inc(scale_r, 1)

        def all_max(pool, k, n):
            pool.wait_ge(amax_r, n)
            pool.partition_all_reduce(gmax[:, k:k + 1], amax[:, k:k + 1], P, RED.max).then_inc(gmax_r, 1)

        with nc.Block() as blk:
            @blk.sync
            def _(sp):
                sp.dma_start(W[:, :], A["bit_weights"]).then_inc(wload, 16)
                sp.dma_start(bias[:, :], A["bit_bias"]).then_inc(wload, 16)
                sp.dma_start(rowbias[:, :, :], A["bit_rowbias"].partition_broadcast(P)).then_inc(wload, 16)

            @blk.gpsimd
            def _(pool):
                c = Chain(pool, pool_chain)
                for k, (_, count, _, _) in enumerate(BIT_WEIGHTS):
                    m = pool.memset(counts[:, k:k + 1], 1.0 / count)
                    c.mark(m)
                c.link(pool.memset(identb[:, :], 0.0))
                pool.affine_select(out=identb[:, :], in_=identb[:, :], compare_op=ALU.not_equal, fill=1.0,
                                   base=0, pattern=[[-1, P]], channel_multiplier=1).then_inc(identb_made, 1)
                all_max(pool, CTX_A, 1)
                pool.wait_ge(wsum_r, 1)
                pool.partition_all_reduce(wsc[:, :], wsum[:, :], P, RED.add).then_inc(wtot_r, 1)

            @blk.scalar
            def _(act):
                act.wait_ge(var_r, 1)
                act.activation(lnwork[:, 3, :], lnwork[:, 2, :], ACT.Sqrt, bias=epsc[:, :], scale=1.0 / P)\
                   .then_inc(std_r, 1)

            @blk.vector
            def _(dve):
                c = Chain(dve, chain)
                L = c.link
                L(dve.memset(amax[:, :], 0.0))
                dve.tensor_reduce(amax[0:CC, CTX_A:CTX_A + 1], CT[:, :, :], AX.XY, ALU.max,
                                  apply_absolute_value=True).then_inc(amax_r, 1)
                dve.wait_ge(wload, 48)
                for k, (_, _, c0, c1) in enumerate(BIT_WEIGHTS):
                    n = c.mark(dve.tensor_reduce(wsum[:, k:k + 1], W[:, c0:c1], AX.X, ALU.add,
                                                 apply_absolute_value=True))
                c.need(n)
                dve.sem_inc(wsum_r, 1)
                ln_statistics(dve, L, stats, mean, rstd, lnwork, var_r, std_r, stat_done)
                dve.wait_ge(wtot_r, 1)
                dve.wait_ge(identb_made, 1)
                L(dve.tensor_tensor(wsc[:, :], wsc[:, :], counts[:, :], ALU.mult))
                L(dve.tensor_scalar(wsc[:, :], wsc[:, :], 1e-5, None, ALU.max))
                L(dve.tensor_scalar(thr[:, 0, :], wsc[:, :], 0.5, None, ALU.mult))
                L(dve.tensor_scalar(thr[:, 1, :], wsc[:, :], -0.5, None, ALU.mult))
                for k, (_, _, c0, c1) in enumerate(BIT_WEIGHTS):
                    L(dve.tensor_scalar(neg[:, 0:c1 - c0], W[:, c0:c1], thr[:, 1, k:k + 1], None, ALU.is_lt))
                    L(dve.scalar_tensor_tensor(qW[:, c0:c1], W[:, c0:c1], thr[:, 0, k:k + 1], neg[:, 0:c1 - c0],
                                               ALU.is_gt, ALU.subtract))
                L(dve.tensor_copy(katt[:, :, :, :], spread(
                    qW[:, 3 * P:4 * P].rearrange("p (a f) -> p a f", a=2), [P, 2, 2, P // 2], 2)))
                scale_inputs(dve, L, CTX_A, (D2V,), 1)

        r = {}
        stages = ((CT, CTX_A, D2V, vis, VIS_A, qin), (vis, VIS_A, IMG_W, img, IMG_A, qin),
                  (img, IMG_A, ATT0, K[0], None, imgq), (None, IMG_A, ATT1, K[1], None, imgq))
        with ExitStack() as s:
            _, ssems = named(nc, s, "tc")
            scaled_r, q_r, out_ps, out_r, chunk_max, avg_c, lchain = ssems(
                "scaled_r q_r out_ps out_r chunk_max avg_c lchain")
            with nc.Block() as blk:
                @blk.gpsimd
                def _(pool):
                    all_max(pool, VIS_A, 2)
                    all_max(pool, IMG_A, 3)

                @blk.scalar
                def _(act):
                    nq = 0
                    for n, (src, ain, w, dst, aout, q) in enumerate(stages):
                        act.wait_ge(scale_r, min(n, 2) + 1)
                        K0 = CC if n == 0 else P

                        def scale(g, u, wait, base):
                            if wait:
                                act.wait_ge(q_r, base + (g - 1))
                            act.activation(scaled[0:K0, u, :], src[:, bass.ds(g * GB, GB), :], ACT.Copy,
                                           scale=inv[0:K0, ain:ain + 1]).then_inc(scaled_r, 1)

                        def output(g, u, n=n, dst=dst, w=w):
                            act.wait_ge(out_ps, g + (n * G + 1))
                            act.activation(dst[:, bass.ds(g * GB, GB), :], ps[u][:, :], ACT.Identity,
                                           bias=bias[:, w:w + 1], scale=osc[:, w:w + 1]).then_inc(out_r, 1)

                        if src is not None:
                            base = n * G
                            scale(0, 0, False, base)
                            scale(1, 1, False, base)
                            with act.Fori(0, (G - 2) // 2) as i:
                                for u in (0, 1):
                                    output(i * 2 + u, u)
                                    scale(i * 2 + (u + 2), u, True, base)
                            output(G - 2, 0)
                            output(G - 1, 1)
                        else:
                            with act.Fori(0, G // 2) as i:
                                for u in (0, 1):
                                    output(i * 2 + u, u)

                @blk.tensor
                def _(pe):
                    for n, (src, ain, w, dst, aout, q) in enumerate(stages):
                        K0 = CC if n == 0 else P
                        lhs = katt[:, n - 2, :, :] if n >= 2 else qW[0:K0, BIT_WEIGHTS[w][2]:BIT_WEIGHTS[w][3]]
                        with pe.Fori(0, G // 2) as i:
                            for u in (0, 1):
                                g = i * 2 + u
                                if n < 3:
                                    pe.wait_ge(q_r, g + (n * G + 1))
                                if n:
                                    pe.wait_ge(out_r, g + (n * G - 1))
                                pe.matmul(ps[u][:, :], lhs, q[0:K0, bass.ds(g * GB, GB), :], start=True, stop=True)\
                                  .then_inc(out_ps, 1)

                @blk.vector
                def _(dve):
                    c = Chain(dve, lchain)
                    for n, (src, ain, w, dst, aout, q) in enumerate(stages):
                        K0 = CC if n == 0 else P

                        def rounded(g, u, n=n, q=q, K0=K0):
                            dve.wait_ge(scaled_r, g + (n * G + 1))
                            dve.tensor_scalar(q[0:K0, bass.ds(g * GB, GB), :],
                                              scaled[0:K0, u, :].rearrange("p (b q) -> p b q", q=P), ROUND, -ROUND,
                                              ALU.add, ALU.add).then_inc(q_r, 1)

                        def largest(g, n=n, dst=dst):
                            dve.wait_ge(out_r, g + (n * G + 1))
                            dve.tensor_reduce(partmax[:, bass.ds(g, 1)], dst[:, bass.ds(g * GB, GB), :], AX.XY,
                                              ALU.max, apply_absolute_value=True).then_inc(chunk_max, 1)

                        if src is None:
                            continue
                        rounded(0, 0)
                        rounded(1, 1)
                        with dve.Fori(0, (G - 2) // 2) as i:
                            for u in (0, 1):
                                if aout is not None:
                                    largest(i * 2 + u)
                                rounded(i * 2 + (u + 2), u)
                        if aout is not None:
                            largest(G - 2)
                            largest(G - 1)
                            dve.wait_ge(chunk_max, (n + 1) * G)
                            dve.tensor_reduce(amax[:, aout:aout + 1], partmax[:, 0:G], AX.X, ALU.max)\
                               .then_inc(amax_r, 1)
                            scale_inputs(dve, c.link, aout, (IMG_W,) if aout == VIS_A else (ATT0, ATT1), n + 2)
                    c.link(dve.tensor_reduce(avg[:, :], img[:, :, :], AX.X, ALU.add))
                    c.link(dve.tensor_scalar(avg[:, :], avg[:, :], 1.0 / P, None, ALU.mult))

        with ExitStack() as s:
            ssb, ssems = named(nc, s, "tx")
            scaled_r, q_r, xn_r, turned, qT_r, out_ps, out_r, chunk_max = ssems(
                "scaled_r q_r xn_r turned qT_r out_ps out_r chunk_max")
            xq = ssb("xq", [P, 2, GW], BF16)
            with nc.Block() as blk:
                @blk.gpsimd
                def _(pool):
                    all_max(pool, XN_A, 4)

                @blk.scalar
                def _(act):
                    act.wait_ge(scale_r, 4)

                    def scale(g, u, fresh=False):
                        if not fresh:
                            act.wait_ge(q_r, g - 1)
                        act.activation(scaled[:, u, :], xn[:, bass.ds(g * GB, GB), :], ACT.Copy,
                                       scale=inv[:, XN_A:XN_A + 1]).then_inc(scaled_r, 1)

                    def output(g, u):
                        act.wait_ge(out_ps, g + 1)
                        act.activation(fused[:, bass.ds(g * GB, GB), :], ps[4 + u][:, :], ACT.Identity,
                                       bias=bias[:, TXT:TXT + 1], scale=osc[:, TXT:TXT + 1]).then_inc(out_r, 1)
                    scale(0, 0, fresh=True)
                    scale(1, 1, fresh=True)
                    with act.Fori(0, (G - 2) // 2) as i:
                        for u in (0, 1):
                            output(i * 2 + u, u)
                            scale(i * 2 + (u + 2), u)
                    output(G - 2, 0)
                    output(G - 1, 1)

                @blk.tensor
                def _(pe):
                    pe.sem_inc(turned, 2)
                    pe.sem_inc(qT_r, 2)
                    pe.sem_inc(out_r, 2)
                    with pe.Fori(0, G // 2) as i:
                        for u in (0, 1):
                            g = i * 2 + u
                            pe.wait_ge(q_r, g + 1)
                            pe.wait_ge(qT_r, g + 2)
                            for j in range(GB):
                                mm = pe.matmul(ps[u][:, j * P:(j + 1) * P], xq[:, u, j * P:(j + 1) * P],
                                               identb[:, :], start=True, stop=True)
                            mm.then_inc(turned, 1)
                            pe.wait_ge(qT_r, g + 3)
                            pe.wait_ge(out_r, g + 1)
                            pe.matmul(ps[4 + u][:, :], qW[:, 2 * P:3 * P], qin[:, bass.ds(g * GB, GB), :],
                                      start=True, stop=True).then_inc(out_ps, 1)

                @blk.vector
                def _(dve):
                    c = Chain(dve, chain, 0)
                    with dve.Fori(0, NB) as b:
                        dve.tensor_scalar(xn[:, b, :], X[:, b, :], mean[:, bass.ds(b, 1)],
                                          rstd[:, bass.ds(b, 1)], ALU.subtract, ALU.mult).then_inc(xn_r, 1)
                    dve.wait_ge(xn_r, NB)
                    dve.tensor_reduce(amax[:, XN_A:XN_A + 1], xn[:, :, :], AX.XY, ALU.max,
                                      apply_absolute_value=True).then_inc(amax_r, 1)
                    lc = Chain(dve, chunk_max)
                    scale_inputs(dve, lc.link, XN_A, (TXT,), 4)
                    with dve.Fori(0, G // 2) as i:
                        for u in (0, 1):
                            g = i * 2 + u
                            dve.wait_ge(scaled_r, g + 1)
                            dve.wait_ge(turned, g + 1)
                            dve.tensor_scalar(xq[:, u, :], scaled[:, u, :], ROUND, -ROUND, ALU.add, ALU.add)\
                               .then_inc(q_r, 1)
                            dve.wait_ge(turned, g + 3)
                            dve.tensor_copy(qin[:, bass.ds(g * GB, GB), :],
                                            ps[u][:, :].rearrange("p (b q) -> p b q", q=P)).then_inc(qT_r, 1)

        with ExitStack() as s:
            ssb, ssems = named(nc, s, "ta")
            fg = ssb("fg", [P, 2, GW])
            ktok = ssb("ktok", [P, 2, 2, GW])
            mx = ssb("mx", [P, 2, GB]); nm = ssb("nm", [P, 2, GB])
            E = ssb("E", [P, 2, GW]); esum = ssb("esum", [P, 2, GB]); rl = ssb("rl", [P, 2, GB])
            PT = ssb("PT", [P, 2, GW])
            names = "f_in kt_ps kt_r s_ps m_r e_r n_r t_ps t_r o_ps f_r x_r"
            (f_in, kt_ps, kt_r) = ssems("f_in kt_ps kt_r")
            s_ps, m_r, e_r, n_r, t_ps, t_r, o_ps, f_r, ach = [ssems(f"{n}0 {n}1") for n in
                                                     "s_ps m_r e_r n_r t_ps t_r o_ps f_r ach".split()]
            ISQ = P ** -0.5
            KT_BANK = (ps[0], ps[1])
            S_BANK, T_BANK, O_BANK = (ps[2], ps[3]), (ps[4], ps[5]), (ps[6], ps[7])

            def rounds(eng, start, stages_of):
                def step(g, u, first=False, last=False):
                    for st in stages_of:
                        st(0, g, u)
                        if not first:
                            st(1, g - 1, 1 - u)
                    if not last:
                        start(g + 1, 1 - u)
                step(0, 0, first=True)
                step(1, 1)
                with eng.Fori(0, (G - 4) // 2) as i:
                    for n in (0, 1):
                        step(i * 2 + (2 + n), n)
                step(G - 2, 0)
                step(G - 1, 1, last=True)
                for st in stages_of:
                    st(1, G - 1, (G - 1) % 2)

            with nc.Block() as blk:
                @blk.tensor
                def _(pe):
                    def keys(g, u):
                        if not isinstance(g, int) or g > 0:
                            pe.wait_ge(kt_r, g * 2)
                        for o in (0, 1):
                            for j in range(GB):
                                pe.matmul(KT_BANK[o][:, j * P:(j + 1) * P],
                                          imgq[:, bass.ds(g * GB + j, 1), :], katt[:, o, :, :],
                                          start=True, stop=True).then_inc(kt_ps, 1)

                    def score(o, g, u):
                        if o == 0:
                            pe.wait_ge(f_in, g + 1)
                            if not isinstance(g, int) or g > 0:
                                pe.wait_ge(e_r[0], g * GB)
                        else:
                            pe.wait_ge(f_r[0], g + 1)
                            if not isinstance(g, int) or g > 0:
                                pe.wait_ge(e_r[1], g * GB)
                        for j in range(GB):
                            mm = pe.matmul(S_BANK[o][:, j * P:(j + 1) * P], fg[:, u, j * P:(j + 1) * P],
                                           K[o][:, bass.ds(g * GB + j, 1), :], start=True, stop=True)
                        mm.then_inc(s_ps[o], 1)

                    def turn(o, g, u):
                        pe.wait_ge(n_r[o], g + 1)
                        if not isinstance(g, int) or g > 0:
                            pe.wait_ge(t_r[o], g)
                        for j in range(GB):
                            mm = pe.transpose(T_BANK[o][:, j * P:(j + 1) * P], E[:, o, j * P:(j + 1) * P], ident[:, :])
                        mm.then_inc(t_ps[o], 1)

                    def apply(o, g, u):
                        pe.wait_ge(t_r[o], g + 1)
                        if o == 0:
                            pe.wait_ge(kt_r, g * 2 + 2)
                        if not isinstance(g, int) or g > 0:
                            pe.wait_ge(f_r[o], g)
                        for j in range(GB):
                            mm = pe.matmul(O_BANK[o][:, j * P:(j + 1) * P], ktok[:, u, o, j * P:(j + 1) * P],
                                           PT[:, o, j * P:(j + 1) * P], start=True, stop=True)
                        mm.then_inc(o_ps[o], 1)

                    keys(0, 0)
                    rounds(pe, keys, (score, turn, apply))

                @blk.scalar
                def _(act):
                    def exps(o, g, u):
                        act.wait_ge(m_r[o], g + 1)
                        if not isinstance(g, int) or g > 0:
                            act.wait_ge(t_ps[o], g)
                        for j in range(GB):
                            act.activation(E[:, o, j * P:(j + 1) * P], S_BANK[o][:, j * P:(j + 1) * P], ACT.Exp,
                                           bias=nm[:, o, j:j + 1], scale=ISQ,
                                           accum_out=esum[:, o, j:j + 1]).then_inc(e_r[o], 1)

                    def copy(o, g, u):
                        act.wait_ge(t_ps[o], g + 1)
                        if not isinstance(g, int) or g > 0:
                            act.wait_ge(o_ps[o], g)
                        act.activation(PT[:, o, :], T_BANK[o][:, :], ACT.Copy).then_inc(t_r[o], 1)
                    rounds(act, lambda g, u: None, (exps, copy))

                @blk.vector
                def _(dve):
                    def fetch(g, u):
                        if not isinstance(g, int) or g > 1:
                            dve.wait_ge(f_r[1], g - 1)
                        dve.tensor_copy(fg[:, u, :].rearrange("p (b q) -> p b q", q=P),
                                        fused[:, bass.ds(g * GB, GB), :]).then_inc(f_in, 1)
                        dve.wait_ge(kt_ps, g * (2 * GB) + 2 * GB)
                        for o in (0, 1):
                            dve.scalar_tensor_tensor(
                                ktok[:, u, o, :].rearrange("p (b f) -> p b f", f=P),
                                KT_BANK[o][:, :].rearrange("p (b f) -> p b f", f=P), osc[:, ATT0 + o:ATT0 + o + 1],
                                spread(rowbias[:, o, :], [P, GB, P], 1), ALU.mult, ALU.add).then_inc(kt_r, 1)

                    def maximum(o, g, u):
                        dve.wait_ge(s_ps[o], g + 1)
                        c = Chain(dve, ach[o], g * 2)
                        c.link(dve.tensor_reduce(mx[:, o, :], S_BANK[o][:, :].rearrange("p (b k) -> p b k", k=P),
                                                 AX.X, ALU.max))
                        dve.tensor_scalar(nm[:, o, :], mx[:, o, :], -ISQ, None, ALU.mult).then_inc(m_r[o], 1)

                    def normalise(o, g, u):
                        dve.wait_ge(e_r[o], g * GB + GB)
                        c = Chain(dve, ach[o], g * 2 + 1)
                        c.link(dve.reciprocal(rl[:, o, :], esum[:, o, :]))
                        e = E[:, o, :].rearrange("p (b k) -> p b k", k=P)
                        dve.scalar_tensor_tensor(e, e, 0.1, spread(rl[:, o, :], [P, GB, P], 2),
                                                 ALU.mult, ALU.mult).then_inc(n_r[o], 1)

                    def add(o, g, u):
                        dve.wait_ge(o_ps[o], g + 1)
                        f = fg[:, u, :].rearrange("p (b q) -> p b q", q=P)
                        dve.tensor_tensor(f if o == 0 else fused[:, bass.ds(g * GB, GB), :], f,
                                          O_BANK[o][:, :].rearrange("p (b q) -> p b q", q=P), ALU.add)\
                           .then_inc(f_r[o], 1)
                    fetch(0, 0)
                    rounds(dve, fetch, (maximum, normalise, add))

        with ExitStack() as s:
            ssb, ssems = named(nc, s, "tf")
            hin = ssb("hin", [P, 2, 2, GW])
            hq = ssb("hq", [P, 2, 4, GW], BF16)
            (chain2, chunk_max, scaled_r, q_r, avg_r, h_ps, h_max, hs_r, h2_ps, h2_r, hq_r, y_ps, y_r, xb_r) = ssems(
                "chain2 chunk_max scaled_r q_r avg_r h_ps h_max hs_r h2_ps h2_r hq_r y_ps y_r xb_r")

            def hidden_product(pe, bank, c, g):
                pe.matmul(bank[:, :], qW[:, 4 * P + c * P:5 * P + c * P], qin[:, bass.ds(g * GB, GB), :],
                          start=True, stop=False)
                return pe.matmul(bank[:, :], qW[:, 8 * P + c * P:9 * P + c * P],
                                 spread(avgq[:, bass.ds(g * GB, GB)], [P, GB, P], 2), start=False, stop=True)

            with nc.Block() as blk:
                @blk.gpsimd
                def _(pool):
                    all_max(pool, CAT_A, 5)
                    all_max(pool, HID_A, 6)

                @blk.tensor
                def _(pe):
                    pe.sem_inc(h_max, 8)
                    with pe.Fori(0, G // 2) as i:
                        for n in (0, 1):
                            g = i * 2 + n
                            pe.wait_ge(q_r, g + 1)
                            pe.wait_ge(avg_r, 1)
                            for c in range(4):
                                pe.wait_ge(h_max, g * 4 + (c + 1))
                                hidden_product(pe, ps[4 * n + c], c, g).then_inc(h_ps, 1)
                    pe.wait_ge(h_max, 8 + 4 * G)
                    pe.wait_ge(hs_r, 1)
                    def hidden(g, u):
                        for c in range(4):
                            pe.wait_ge(h2_r, g * 4 + (c + 1))
                            hidden_product(pe, ps[c], c, g).then_inc(h2_ps, 1)

                    def output(g, u):
                        pe.wait_ge(hq_r, g * 4 + 4)
                        pe.wait_ge(y_r, g * 4 + 1)
                        for j in range(GB):
                            for c in range(4):
                                mm = pe.matmul(ps[6 + u][:, j * P:(j + 1) * P], hq[:, u, c, j * P:(j + 1) * P],
                                               qW[:, (12 + c) * P:(13 + c) * P], start=(c == 0), stop=(c == 3))
                        mm.then_inc(y_ps, 1)
                    pe.sem_inc(h2_r, 4)
                    pe.sem_inc(y_r, 8)
                    hidden(0, 0)
                    hidden(1, 1)
                    with pe.Fori(0, (G - 2) // 2) as i:
                        for n in (0, 1):
                            output(i * 2 + n, n)
                            hidden(i * 2 + (n + 2), n)
                    output(G - 2, 0)
                    output(G - 1, 1)

                @blk.scalar
                def _(act):
                    act.wait_ge(scale_r, 5)
                    with act.Fori(0, G // 2) as i:
                        for u in (0, 1):
                            g = i * 2 + u
                            act.wait_ge(q_r, g)
                            act.activation(scaled[:, u, :], fused[:, bass.ds(g * GB, GB), :], ACT.Copy,
                                           scale=inv[:, CAT_A:CAT_A + 1]).then_inc(scaled_r, 1)
                    act.wait_ge(hs_r, 1)
                    with act.Fori(0, G) as g:
                        for c in range(4):
                            act.wait_ge(h2_ps, g * 4 + (c + 1))
                            act.wait_ge(hq_r, g * 4 + c)
                            act.activation(hin[:, c % 2, 0, :], ps[c][:, :], ACT.Relu, bias=hbias[:, c:c + 1],
                                           scale=hsc[:, :]).then_inc(h2_r, 1)

                @blk.vector
                def _(dve):
                    c = Chain(dve, chain2)
                    L = c.link
                    L(dve.tensor_reduce(partmax[:, 0:1], fused[:, :, :], AX.XY, ALU.max, apply_absolute_value=True))
                    L(dve.tensor_reduce(partmax[:, 1:2], avg[:, :], AX.X, ALU.max, apply_absolute_value=True))
                    dve.tensor_reduce(amax[:, CAT_A:CAT_A + 1], partmax[:, 0:2], AX.X, ALU.max).then_inc(amax_r, 1)
                    scale_inputs(dve, L, CAT_A, (F1,), 5)
                    L(dve.tensor_scalar(avg[:, :], avg[:, :], inv[:, CAT_A:CAT_A + 1], None, ALU.mult))
                    dve.tensor_scalar(avgq[:, :], avg[:, :], ROUND, -ROUND, ALU.add, ALU.add).then_inc(avg_r, 1)
                    L(dve.tensor_scalar(gb2[:, :], rowbias[:, 2, :], gates[:, 1:2], None, ALU.mult))
                    with dve.Fori(0, G // 2) as i:
                        for u in (0, 1):
                            g = i * 2 + u
                            dve.wait_ge(scaled_r, g + 1)
                            dve.tensor_scalar(qin[:, bass.ds(g * GB, GB), :],
                                              scaled[:, u, :].rearrange("p (b q) -> p b q", q=P), ROUND, -ROUND,
                                              ALU.add, ALU.add).then_inc(q_r, 1)
                            for k in range(4):
                                dve.wait_ge(h_ps, g * 4 + (k + 1))
                                dve.tensor_reduce(partmax[:, bass.ds(g + k * G, 1)], ps[4 * u + k][:, :], AX.X,
                                                  ALU.max).then_inc(h_max, 1)
                    dve.wait_ge(h_max, 8 + 4 * G)
                    L(dve.tensor_reduce(hraw[:, :], partmax[:, :].rearrange("p (c g) -> p c g", c=4), AX.X, ALU.max))
                    L(dve.scalar_tensor_tensor(hraw[:, :], hraw[:, :], osc[:, F1:F1 + 1], bias[:, 5:9],
                                               ALU.mult, ALU.add))
                    L(dve.tensor_scalar(hraw[:, :], hraw[:, :], 0.0, None, ALU.max))
                    dve.tensor_reduce(amax[:, HID_A:HID_A + 1], hraw[:, :], AX.X, ALU.max).then_inc(amax_r, 1)
                    scale_inputs(dve, L, HID_A, (F2,), 6)
                    L(dve.tensor_tensor(hsc[:, :], osc[:, F1:F1 + 1], inv[:, HID_A:HID_A + 1], ALU.mult))
                    L(dve.tensor_scalar(hbias[:, :], bias[:, 5:9], inv[:, HID_A:HID_A + 1], None, ALU.mult))
                    L(dve.tensor_tensor(gf2[:, :], osc[:, F2:F2 + 1], gates[:, 1:2], ALU.mult))
                    dve.sem_inc(hs_r, 1)

                    def rounded(g, u):
                        for k in range(4):
                            dve.wait_ge(h2_r, g * 4 + (k + 5))
                            if k == 0 and (not isinstance(g, int) or g > 1):
                                dve.wait_ge(y_ps, g - 1)
                            dve.tensor_scalar(hq[:, u, k, :], hin[:, k % 2, 0, :], ROUND, -ROUND, ALU.add, ALU.add)\
                               .then_inc(hq_r, 1)

                    def add(g, u):
                        dve.wait_ge(y_ps, g + 1)
                        xb = X[:, bass.ds(g * GB, GB), :]
                        l = Chain(dve, xb_r, g * 2)
                        l.link(dve.tensor_tensor(xb, xb, spread(gb2[:, :], [P, GB, P], 1), ALU.add))
                        l.link(dve.scalar_tensor_tensor(xb, ps[6 + u][:, :].rearrange("p (b f) -> p b f", f=P),
                                                        gf2[:, :], xb, ALU.mult, ALU.add))
                        for j in range(GB):
                            dve.bn_stats(stats[:, bass.ds(g * GB + j, 1), :], X[:, bass.ds(g * GB + j, 1), :])\
                               .then_inc(y_r, 1)
                    rounded(0, 0)
                    rounded(1, 1)
                    with dve.Fori(0, (G - 2) // 2) as i:
                        for n in (0, 1):
                            add(i * 2 + n, n)
                            rounded(i * 2 + (n + 2), n)
                    add(G - 2, 0)
                    add(G - 1, 1)
                    dve.wait_ge(y_r, 8 + NB)


ALPHA = 1.702
LIMIT = 7.0


def swiglu_experts(r, xg, yg, nc, A, X, ident, stats, mean, rstd, lnwork, epsc, gates, ps):
    N = TILES + NB
    with ExitStack() as a:
        sb, sems = named(nc, a, r.name + "x")
        w13 = sb("w13", [P, NE + 1, FF])
        w2 = sb("w2", [P, NE + 1, P])
        b13 = sb("b13", [P, NE + 1, FF])
        b2 = sb("b2", [P, NE + 1, P])
        rows = sb("rows", [P, 4, ROW])
        xT = sb("xT", [P, 2, P])
        h = sb("h", [P, 2, FF])
        prod = sb("prod", [P, 2, 2 * P]); sig = sb("sig", [P, 2, P])
        act_t = sb("act", [P, 2, P]); aT = sb("aT", [P, 2, P])
        y = sb("y", [P, 2, P]); yrow = sb("yrow", [P, 2], U32)
        wload, xT_ps, xT_sb, h_ps, g_r, sig_r, a_r, aT_ps, aT_sb, y_ps, y_sb, id_sb, chain, tchain, begun = sems(
            "wload xT_ps xT_sb h_ps g_r sig_r a_r aT_ps aT_sb y_ps y_sb id_sb chain tchain begun")
        row_in = sems("row_in0 row_in1 row_in2 row_in3")
        sent = sems("sent0 sent1")
        X_BANK, H_BANK, AT_BANK, Y_BANK = (ps[0], ps[1]), (ps[2], ps[3]), (ps[4], ps[5]), (ps[6], ps[7])
        with nc.Block() as blk:
            @blk.sync
            def _(sp):
                sp.dma_start(w13[:, :, :], A["w13"]).then_inc(wload, 16)
                sp.dma_start(w2[:, :, :], A["w2s"]).then_inc(wload, 16)
                for q in range(4):
                    sp.dma_start(rows[:, q, :], xg[q * P:(q + 1) * P, :]).then_inc(row_in[q], 16)
                with sp.Fori(1, N // 4) as i:
                    for q in range(4):
                        sp.wait_ge(xT_ps, i * 4 + (q - 3))
                        sp.wait_ge(id_sb, i * 4 + (q - 3))
                        sp.dma_start(rows[:, q, :], xg[bass.ds(i * (4 * P) + q * P, P), :]).then_inc(row_in[q], 16)

            @blk.scalar
            def _(act):
                act.dma_start(b13[:, :, :], A["b13"].partition_broadcast(P)).then_inc(wload, 16)
                act.dma_start(b2[:, :, :], A["b2s"].partition_broadcast(P)).then_inc(wload, 16)

                def turned(j, u):
                    act.wait_ge(xT_ps, j + 1)
                    act.activation(xT[:, u, :], X_BANK[u][:, 0:P], ACT.Copy).then_inc(xT_sb, 1)

                def sigmoid(j, u):
                    act.wait_ge(g_r, j + 1)
                    act.activation(sig[:, u, :], prod[:, u, 0:P], ACT.Sigmoid, scale=ALPHA).then_inc(sig_r, 1)

                def hidden(j, u):
                    act.wait_ge(aT_ps, j + 1)
                    act.activation(aT[:, u, :], AT_BANK[u][:, 0:P], ACT.Copy).then_inc(aT_sb, 1)

                turned(0, 0)
                turned(1, 1)
                sigmoid(0, 0)
                with act.Fori(0, (N - 2) // 2) as i:
                    for n in (0, 1):
                        j, u = i * 2 + (n + 1), (n + 1) % 2
                        hidden(j - 1, 1 - u)
                        act.wait_ge(h_ps, j)
                        turned(j + 1, 1 - u)
                        sigmoid(j, u)
                hidden(N - 2, 0)
                sigmoid(N - 1, 1)
                hidden(N - 1, 1)

            @blk.tensor
            def _(pe):
                def turn(j, u, q):
                    pe.wait_ge(row_in[q], rows_in(j, q))
                    pe.transpose(X_BANK[u][:, 0:P], rows[:, q, 0:P], ident[:, :]).then_inc(xT_ps, 1)

                def first_product(j, u):
                    e = pe.value_load(r.tile_expert[0:1, bass.ds(j, 1)], min_val=0, max_val=NE)
                    pe.wait_ge(xT_sb, j + 1)
                    pe.matmul(H_BANK[u][:, :], xT[:, u, :], w13[:, e, :], start=True, stop=True).then_inc(h_ps, 1)

                def turn_hidden(j, u):
                    pe.wait_ge(a_r, j + 1)
                    pe.transpose(AT_BANK[u][:, 0:P], act_t[:, u, :], ident[:, :]).then_inc(aT_ps, 1)

                def second_product(j, u):
                    e = pe.value_load(r.tile_expert[0:1, bass.ds(j, 1)], min_val=0, max_val=NE)
                    pe.wait_ge(aT_sb, j + 1)
                    pe.matmul(Y_BANK[u][:, 0:P], aT[:, u, :], w2[:, e, :], start=True, stop=True).then_inc(y_ps, 1)

                pe.wait_ge(wload, 64)
                turn(0, 0, 0)
                turn(1, 1, 1)
                first_product(0, 0)
                with pe.Fori(0, (N - 4) // 4) as i:
                    for n in range(4):
                        j, u = i * 4 + (n + 1), (n + 1) % 2
                        turn_hidden(j - 1, 1 - u)
                        turn(j + 1, 1 - u, (n + 2) % 4)
                        first_product(j, u)
                        second_product(j - 1, 1 - u)
                for j in range(N - 3, N):
                    u = j % 2
                    turn_hidden(j - 1, 1 - u)
                    if j + 1 < N:
                        turn(j + 1, 1 - u, (j + 1) % 4)
                    first_product(j, u)
                    second_product(j - 1, 1 - u)
                turn_hidden(N - 1, 1)
                second_product(N - 1, 1)

            @blk.vector
            def _(dve):
                def gate_part(j, u):
                    c = Chain(dve, chain, j * 2)
                    e = dve.value_load(r.tile_expert[0:1, bass.ds(j, 1)], min_val=0, max_val=NE)
                    dve.wait_ge(h_ps, j + 1)
                    c.link(dve.tensor_tensor(h[:, u, :], H_BANK[u][:, :], b13[:, e, :], ALU.add))
                    c.link(dve.tensor_tensor(prod[:, u, :], h[:, u, 0:2 * P], h[:, u, 2 * P:4 * P], ALU.mult))
                    dve.tensor_scalar(prod[:, u, 0:P], prod[:, u, 0:P], LIMIT, None, ALU.min).then_inc(g_r, 1)

                def value_part(j, u, fresh=False):
                    c = Chain(dve, tchain, j * 2)
                    l, g = prod[:, u, P:2 * P], prod[:, u, 0:P]
                    c.link(dve.tensor_scalar(l, l, LIMIT, -LIMIT, ALU.min, ALU.max))
                    dve.wait_ge(g_r, j + 1)
                    c.link(dve.scalar_tensor_tensor(l, l, 1.0, g, ALU.add, ALU.mult))
                    dve.wait_ge(sig_r, j + 1)
                    if not fresh:
                        dve.wait_ge(aT_ps, j - 1)
                    dve.tensor_tensor(act_t[:, u, :], l, sig[:, u, :], ALU.mult).then_inc(a_r, 1)

                def output(j, u, q, fresh=False):
                    e = dve.value_load(r.tile_expert[0:1, bass.ds(j, 1)], min_val=0, max_val=NE)
                    if not fresh:
                        dve.wait_ge(sent[u], (j - u) * 8)
                    dve.wait_ge(row_in[q], rows_in(j, q))
                    dve.tensor_copy(yrow[:, u:u + 1], rows[:, q, P:ROW]).then_inc(id_sb, 1)
                    dve.wait_ge(y_ps, j + 1)
                    dve.tensor_tensor(y[:, u, :], Y_BANK[u][:, 0:P], b2[:, e, :], ALU.add).then_inc(y_sb, 1)

                dve.wait_ge(wload, 64)
                gate_part(0, 0)
                value_part(0, 0, fresh=True)
                gate_part(1, 1)
                value_part(1, 1, fresh=True)
                output(0, 0, 0, fresh=True)
                gate_part(2, 0)
                value_part(2, 0)
                output(1, 1, 1, fresh=True)
                with dve.Fori(0, (N - 4) // 4) as i:
                    for n in range(4):
                        j, u = i * 4 + (n + 3), (n + 3) % 2
                        gate_part(j, u)
                        value_part(j, u)
                        output(j - 1, 1 - u, (n + 2) % 4)
                gate_part(N - 1, 1)
                value_part(N - 1, 1)
                output(N - 2, 0, (N - 2) % 4)
                output(N - 1, 1, (N - 1) % 4)

            @blk.gpsimd
            def _(pool):
                with pool.Fori(0, N // 2) as i:
                    for u in (0, 1):
                        pool.wait_ge(id_sb, i * 2 + (u + 1))
                        pool.wait_ge(y_sb, i * 2 + (u + 1))
                        pool.sem_inc(begun, 1)
                        pool.indirect_dma_start(yg, bass.IndirectOffsetOnAxis(yrow[:, u:u + 1], 0), y[:, u, :], None,
                                                bounds_check=r.choices * NB * P - 1, oob_is_err=False)\
                            .then_inc(sent[u], 16)
                for u in (0, 1):
                    pool.wait_ge(sent[u], N // 2 * 16)


DIRECT = (
    "L0_ffn_alpha", "L0_ffn_b1", "L0_ffn_b2", "L0_ffn_gate_b", "L0_ffn_gate_w", "L0_ffn_w1", "L0_ffn_w2",
    "L0_xattn_Wk", "L0_xattn_Wo", "L0_xattn_Wq", "L0_xattn_Wv", "L0_xattn_bk", "L0_xattn_bo", "L0_xattn_bq",
    "L0_xattn_bv", "L1_ffn_gate_b", "g_ffn", "g_xattn", "x",
)


def layout(inputs):
    import numpy as np
    arrays = {name: inputs[name] for name in DIRECT}
    arrays["ctx_T"] = np.ascontiguousarray(inputs["ctx_768"].transpose(2, 0, 1))

    def get(name):
        return inputs["L1_xattn_" + name]

    def side_by_side(w):
        return w.T.reshape(-1, P, w.shape[0]).transpose(1, 0, 2).reshape(P, -1)
    d2v = np.pad(get("W_d2v"), ((0, 0), (0, P - CC)))
    arrays["bit_weights"] = np.ascontiguousarray(np.concatenate(
        [side_by_side(w) for w in (d2v, get("W_img"), get("W_txt"), get("W_att0"), get("W_att1"), get("W_f1"),
                                   get("W_f2"))], axis=1))
    twice = [np.tile(get(n), 2) for n in ("b_att0", "b_att1")]
    arrays["bit_bias"] = np.ascontiguousarray(np.stack(
        [get("b_d2v"), get("b_img"), get("b_txt")] + twice + list(get("b_f1").reshape(4, P)), axis=1))
    arrays["bit_rowbias"] = np.stack(twice + [get("b_f2")])

    def with_shared(name):
        return np.concatenate([inputs["L1_ffn_" + name], inputs["L1_ffn_s" + name][None]])

    def even_odd(w):
        return np.concatenate([w[:, 0::2], w[:, 1::2]], axis=1)
    w13 = np.concatenate([even_odd(with_shared("w1")), even_odd(with_shared("w3"))], axis=1)
    arrays["w13"] = np.ascontiguousarray(w13.transpose(2, 0, 1))
    arrays["b13"] = np.ascontiguousarray(np.concatenate([even_odd(with_shared("b1")), even_odd(with_shared("b3"))],
                                                        axis=1))
    arrays["w2s"] = np.ascontiguousarray(with_shared("w2").transpose(2, 0, 1))
    arrays["b2s"] = with_shared("b2")
    arrays["gate_w_T"] = np.ascontiguousarray(inputs["L1_ffn_gate_w"].T)
    return arrays


def kernel(**inputs):
    import numpy as np
    from concourse import bacc
    from concourse.bass_utils import run_bass_kernel_spmd

    arrays = {"in_" + name: np.ascontiguousarray(a)
              for name, a in layout({name: np.asarray(a) for name, a in inputs.items()}).items()}
    nc = bacc.Bacc("TRN2", target_bir_lowering=False, num_devices=1)
    A = {name[3:]: nc.dram_tensor(name, a.shape, mybir.dt.from_np(a.dtype), kind="ExternalInput").ap()
         for name, a in arrays.items()}
    out = nc.dram_tensor("out", (NB, P, P), F32, kind="ExternalOutput").ap()
    build(nc, A, out)
    result = run_bass_kernel_spmd(nc, [arrays], core_ids=[0])
    return result.results[0]["out"]
```

```python
from contextlib import ExitStack

import concourse.bass as bass
from concourse import mybir

F32 = mybir.dt.float32
BF16 = mybir.dt.bfloat16
I32 = mybir.dt.int32
U32 = mybir.dt.uint32
ALU = mybir.AluOpType
ACT = mybir.ActivationFunctionType
AX = mybir.AxisListType
RED = bass.bass_isa.ReduceOp

P = 128
NB = 32
CC = 96
NH = 16
DH = P // NH
VW = 32
CLAMP = 10000.0
LN_EPS = 1e-5
SCALE = DH ** -0.5
NE = 8
TOPK = 2
FF = 512
TILES = 72
ROW = P + 2
ROUND = 1.5 * 2.0 ** 23


class Chain:

    def __init__(self, eng, sem, start=0):
        self.eng, self.sem, self.start, self.n = eng, sem, start, 0

    def mark(self, ins):
        self.n += 1
        ins.then_inc(self.sem, 1)
        return self.n

    def need(self, n):
        self.eng.wait_ge(self.sem, self.start + n)

    def link(self, ins):
        self.need(self.mark(ins))


def semaphores(nc, stack, names):
    handles = [nc.alloc_semaphore(name=n) for n in names]
    stack.callback(nc.all_engine_barrier)
    stack.callback(nc.clear_and_free_semaphores, handles)
    return handles


def spread(ap, shape, dim):
    return ap.unsqueeze(dim).broadcast_to(shape)


def ln_statistics(dve, link, st, mean, rstd, work, var_ready, std_ready, done):
    me, mo, ve, vo = st[:, :, 1], st[:, :, 4], st[:, :, 2], st[:, :, 5]
    link(dve.tensor_tensor(mean[:, :], me, mo, ALU.add))
    link(dve.tensor_tensor(work[:, 0, :], me, mo, ALU.subtract))
    link(dve.tensor_scalar(mean[:, :], mean[:, :], 0.5, None, ALU.mult))
    link(dve.tensor_tensor(work[:, 1, :], ve, vo, ALU.add))
    link(dve.tensor_tensor(work[:, 0, :], work[:, 0, :], work[:, 0, :], ALU.mult))
    dve.scalar_tensor_tensor(work[:, 2, :], work[:, 0, :], P / 4.0, work[:, 1, :], ALU.mult, ALU.add)\
       .then_inc(var_ready, 1)
    dve.wait_ge(std_ready, 1)
    dve.reciprocal(rstd[:, :], work[:, 3, :]).then_inc(done, 1)


def build(nc, A, out):
    with ExitStack() as ctx:
        def sb(stack, name, shape, dt=F32):
            return stack.enter_context(nc.sbuf_tensor(name, shape, dt))

        def sems(stack, names):
            return semaphores(nc, stack, names.split())

        score_banks = [ctx.enter_context(nc.psum_tensor(f"banks{i}", [P, 1024], F32)) for i in (0, 2)]
        ps = [b[:, j * 512:j * 512 + 512] for b in score_banks for j in (0, 1)]
        ps += [ctx.enter_context(nc.psum_tensor(f"bank{i}", [P, 512], F32)) for i in range(4, 8)]
        X = sb(ctx, "X", [P, NB, P])
        ident = sb(ctx, "ident", [P, P])
        stats = sb(ctx, "stats", [P, NB, 6])
        mean = sb(ctx, "mean", [P, NB])
        rstd = sb(ctx, "rstd", [P, NB])
        lnwork = sb(ctx, "lnwork", [P, 4, NB])
        gates = sb(ctx, "gates", [P, 4])
        epsc = sb(ctx, "epsc", [P, 1])
        CT = sb(ctx, "CT", [CC, NB, P])
        expsum = sb(ctx, "expsum", [P, 2 * NB])

        xg = [nc.dram_tensor(f"xg{n}", (TILES * P, ROW), F32).ap() for n in (0, 1)]
        yg = [nc.dram_tensor(f"yg{n}", (TOPK * NB * P, P), F32).ap() for n in (0, 1)]
        VROWS = 8
        NBIAS = NE * (FF + P) + (NE + 1) * (FF + P)
        bsplit = nc.dram_tensor("bsplit", (3, NBIAS), BF16).ap()

        with ExitStack() as a:
            vacant = sb(a, "vacant", [P, VROWS, ROW])
            bias_in = sb(a, "bias_in", [P, NBIAS // P])
            bias_rest = sb(a, "bias_rest", [P, NBIAS // P])
            bias_parts = sb(a, "bias_parts", [P, 3, NBIAS // P], BF16)
            wq = sb(a, "wq", [P, P]); wk = sb(a, "wk", [CC, P]); wv = sb(a, "wv", [CC, P])
            bq = sb(a, "bq", [P, 1]); bk = sb(a, "bk", [P, 1]); bqs = sb(a, "bqs", [P, 1])
            bv = sb(a, "bv", [P, P])
            headmask = sb(a, "headmask", [P, NH])
            graw = sb(a, "graw", [P, 4])
            cv = sb(a, "cv", [CC, 2, P])
            xn = sb(a, "xn", [P, 2, P])
            xT = sb(a, "xT", [P, 2, P])
            qT = sb(a, "qT", [P, 2, P])
            kT = sb(a, "kT", [P, 2, P])
            kx = sb(a, "kx", [P, 2, NH, P])
            V = sb(a, "V", [P, 2, NH, VW])
            mx = sb(a, "mx", [P, 2, 8])
            D = sb(a, "D", [P, 2, 8, P])
            E = sb(a, "E", [P, 4, 8, P])
            PT = sb(a, "PT", [P, 4, 4 * P])
            oT = sb(a, "oT", [P, 2, 4, P])
            rl = sb(a, "rl", [P, 2, NH])
            O = sb(a, "O", [P, 2, P])
            OF = sb(a, "OF", [P, 2, P])
            wo = sb(a, "wo", [P, P]); bo = sb(a, "bo", [P, P])
            bog = sb(a, "bog", [P, P])
            y = sb(a, "y", [P, P])

            loaded = sems(a, "loaded0 loaded1 loaded2 loaded3")
            (bias_loaded, bias_kept, ctx_loaded, vacant_set, vacated, gload, zeroed, made, chain_p, chain_v,
             var_r, std_r, stat_done, prep) = sems(
                a, "bias_loaded bias_kept ctx_loaded vacant_set vacated gload zeroed made chain_p "
                   "chain_v var_r std_r stat_done prep")
            with nc.Block() as blk:
                @blk.sync
                def _(sp):
                    for n in range(4):
                        sp.dma_start(X[:, n * 8:n * 8 + 8, :], A["x_T"][:, n * 8:n * 8 + 8, :]).then_inc(loaded[n], 16)
                    sp.dma_start(CT[:, :, :], A["ctx_T"]).then_inc(ctx_loaded, 16)
                    sp.dma_start(bias_in[:, :], A["biases"]).then_inc(bias_loaded, 16)
                    for n in range(4):
                        sp.wait_ge(loaded[n], 16)
                    sp.wait_ge(ctx_loaded, 16)
                    sp.wait_ge(bias_loaded, 16)
                    sp.wait_ge(gload, 16 * 10)

                @blk.scalar
                def _(act):
                    for dst, src in ((wq[:, :], A["L0_xattn_Wq"]), (wk[:, :], A["L0_xattn_Wk"]),
                                     (wv[:, :], A["L0_xattn_Wv"]),
                                     (bq[:, :], A["L0_xattn_bq"].unsqueeze(1)),
                                     (bk[:, :], A["L0_xattn_bk"].unsqueeze(1)),
                                     (bv[:, :], A["L0_xattn_bv"].partition_broadcast(P)),
                                     (wo[:, :], A["L0_xattn_Wo"]),
                                     (bo[:, :], A["L0_xattn_bo"].partition_broadcast(P)),
                                     (graw[:, 0:2], A["g_xattn"].partition_broadcast(P)),
                                     (graw[:, 2:4], A["g_ffn"].partition_broadcast(P))):
                        act.dma_start(dst, src).then_inc(gload, 16)
                    act.wait_ge(gload, 16 * 10)
                    act.activation(gates[:, :], graw[:, :], ACT.Tanh).then_inc(prep, 1)
                    act.activation(bqs[:, :], bq[:, :], ACT.Copy, scale=SCALE).then_inc(prep, 1)
                    act.wait_ge(var_r, 1)
                    act.wait_ge(zeroed, 1)
                    act.activation(lnwork[:, 3, :], lnwork[:, 2, :], ACT.Sqrt, bias=epsc[:, :], scale=1.0 / P)\
                       .then_inc(std_r, 1)

                @blk.gpsimd
                def _(pool):
                    c = Chain(pool, chain_p)
                    pool.memset(epsc[:, :], LN_EPS).then_inc(zeroed, 1)
                    pool.memset(vacant[:, :, 0:P], 0.0).then_inc(vacant_set, 1)
                    pool.memset(vacant[:, :, P:ROW], 2.0 * TOPK * NB * P).then_inc(vacant_set, 1)
                    c.link(pool.memset(ident[:, :], 0.0))
                    c.link(pool.memset(headmask[:, :], 1.0))
                    c.link(pool.affine_select(out=ident[:, :], in_=ident[:, :], compare_op=ALU.not_equal,
                                              fill=1.0, base=0, pattern=[[-1, P]], channel_multiplier=1))
                    c.link(pool.affine_select(out=headmask[:, :], in_=headmask[:, :], compare_op=ALU.is_ge,
                                              fill=0.0, base=0, pattern=[[-DH, NH]], channel_multiplier=1))
                    c.link(pool.affine_select(out=headmask[:, :], in_=headmask[:, :], compare_op=ALU.is_ge,
                                              fill=0.0, base=DH - 1, pattern=[[DH, NH]], channel_multiplier=-1))
                    c.link(pool.memset(V[:, :, :, :], 0.0))
                    c.link(pool.memset(V[:, :, :, DH:DH + 1], 1.0))

                @blk.vector
                def _(dve):
                    for n in range(4):
                        dve.wait_ge(loaded[n], 16)
                        for b in range(n * 8, n * 8 + 8):
                            dve.bn_stats(stats[:, b, :], X[:, b, :]).then_inc(made, 1)
                    dve.wait_ge(made, NB)
                    c = Chain(dve, chain_v)
                    ln_statistics(dve, c.link, stats, mean, rstd, lnwork, var_r, std_r, stat_done)
                    dve.wait_ge(bias_loaded, 16)
                    split_biases(c, nc, dve, bias_in, bias_parts, bias_rest)

            (cv_in0, cv_in1, xn_made, inputs_ps, xT_sb, qk_ps, v_ps, q_sb, k_sb, kx_made0, kx_made1, v_sb, scored,
             chain_s, shifted, expd, capped, pT_ps, pT_sb, pv_ps, o_sb, back_ps, normed, of_ps, of_sb, y_ps, y_sb, bog_made, capping) = sems(
                a, "cv_in0 cv_in1 xn_made inputs_ps xT_sb qk_ps v_ps q_sb k_sb kx_made0 kx_made1 v_sb scored "
                   "chain_s shifted expd capped pT_ps pT_sb pv_ps o_sb back_ps normed of_ps of_sb y_ps y_sb bog_made capping")
            cv_in = (cv_in0, cv_in1)
            kx_made = (kx_made0, kx_made1)
            S = ((ps[0], ps[1]), (ps[2], ps[3]))
            BACK_BANK, IN_BANK = ps[4], ps[5]
            GROUP_BANK = (IN_BANK, BACK_BANK, IN_BANK, BACK_BANK)
            OPS, QKV = ps[6], ps[7]

            def links_before(t, k):
                scores, backs, sums = min(k, NB) * 4, max(k - 3, 0), max(k - 4, 0) * 2
                return t * 7 - 11 if k == INNER else scores + backs + sums

            INNER = 4

            def steps(eng, step):
                for t in range(INNER):
                    step(t, t % 2, t)
                with eng.Fori(0, (NB - 8) // 2) as i:
                    for n in (0, 1):
                        step(i * 2 + (INNER + n), n, INNER)
                for t in range(INNER + NB - 8, NB + 4):
                    step(t, t % 2, t)

            def spread_keys(eng, b, u, h, k):
                eng.wait_ge(k_sb, b + 1)
                if k >= 1:
                    eng.wait_ge(scored, b * 2 - 2)
                eng.tensor_tensor(kx[:, u, 8 * h:8 * h + 8, :], spread(kT[:, u, :], [P, 8, P], 1),
                                  spread(headmask[:, 8 * h:8 * h + 8], [P, 8, P], 2), ALU.mult)\
                   .then_inc(kx_made[h], 1)

            def has_scores(k): return k < NB
            def has_values(k): return 2 <= k <= NB + 1
            def has_back(k): return 3 <= k <= NB + 2
            def has_sum(k): return k >= 4
            def has_v(k): return 1 <= k <= NB
            def has_project(k): return k < NB - 2

            with nc.Block() as blk:
                @blk.sync
                def _(sp):
                    for k in range(3):
                        sp.dma_start(bsplit[k:k + 1, :].rearrange("k (p c) -> p (k c)", p=P), bias_parts[:, k, :])\
                          .then_inc(bias_kept, 16)
                    sp.dma_start(cv[:, 0, :], A["ctx_T"][:, 0, :]).then_inc(cv_in[0], 16)
                    sp.dma_start(cv[:, 1, :], A["ctx_T"][:, 1, :]).then_inc(cv_in[1], 16)

                    def context(i):
                        for u in (0, 1):
                            sp.wait_ge(v_ps, i * 2 + (u - 1))
                            sp.dma_start(cv[:, u, :], A["ctx_T"][:, i * 2 + u, :]).then_inc(cv_in[u], 16)
                    with sp.Fori(1, TILES // VROWS + 1) as i:
                        context(i)
                        for x in xg:
                            sp.dma_start(x.rearrange("(p j v) c -> p j v c", p=P, v=VROWS)[:, i - 1, :, :],
                                         vacant[:, :, :]).then_inc(vacated, 16)
                    with sp.Fori(TILES // VROWS + 1, NB // 2) as i:
                        context(i)
                    sp.wait_ge(vacated, 32 * (TILES // VROWS))
                    sp.wait_ge(bias_kept, 48)

                @blk.tensor
                def _(pe):
                    def turn_inputs(b, u):
                        pe.wait_ge(xn_made, b + 1)
                        pe.transpose(IN_BANK[:, 0:P], xn[:, u, :], ident[:, :]).then_inc(inputs_ps, 1)

                    def project(b, u):
                        pe.wait_ge(xT_sb, b + 1)
                        pe.matmul(QKV[:, 0:P], wq[:, :], xT[:, u, :], start=True, stop=True)
                        pe.matmul(QKV[:, P:2 * P], wk[:, :], CT[:, b, :], start=True, stop=True).then_inc(qk_ps, 1)

                    def score(b, u, h, k):
                        pe.wait_ge(kx_made[h], b + 1)
                        pe.wait_ge(q_sb, b + 1)
                        if k >= 1:
                            pe.wait_ge(shifted, b * 2 + (h - 1))
                        for j in (0, 1):
                            mm = pe.matmul(S[h][j][:, :], qT[:, u, :],
                                           kx[:, u, 8 * h + 4 * j:8 * h + 4 * j + 4, :], start=True, stop=True)
                        mm.then_inc(scored, 1)

                    def turn_exps(b, u, g):
                        for r in range(4):
                            mm = pe.transpose(GROUP_BANK[g][:, r * P:(r + 1) * P],
                                              E[:, 2 * u + g // 2, 4 * (g % 2) + r, :], ident[:, :])
                        mm.then_inc(pT_ps, 1)

                    def apply_values(b, u, g):
                        pe.wait_ge(pT_sb, b * 4 + (g + 1))
                        for r in range(4):
                            mm = pe.matmul(OPS[VW * r:VW * (r + 1), g * P:(g + 1) * P], V[:, u, 4 * g + r, :],
                                           PT[:, g, r * P:(r + 1) * P], start=True, stop=True)
                        mm.then_inc(pv_ps, 1)

                    def turn_back(b, u):
                        pe.wait_ge(o_sb, b + 1)
                        for g in range(4):
                            mm = pe.transpose(BACK_BANK[:, g * P:(g + 1) * P], oT[:, u, g, :], ident[:, :])
                        mm.then_inc(back_ps, 1)

                    turn_inputs(0, 0)
                    project(0, 0)
                    turn_inputs(1, 1)
                    pe.wait_ge(q_sb, 1)
                    pe.wait_ge(k_sb, 1)
                    project(1, 1)

                    def step(t, u, k):
                        b, w = t - 2, 1 - u
                        if has_scores(k):
                            score(t, u, 0, k)
                        if has_back(k):
                            pe.wait_ge(pT_sb, b * 4)
                            turn_back(t - 3, w)
                        if has_scores(k):
                            score(t, u, 1, k)
                        if has_values(k):
                            pe.wait_ge(capped, b * 2 + 1)
                            if k >= 3:
                                pe.wait_ge(pT_sb, b * 4)
                            else:
                                pe.wait_ge(xT_sb, 4)
                            turn_exps(b, u, 0)
                        if has_v(k):
                            pe.wait_ge(q_sb, t + 2 if k < NB - 1 else NB)
                            pe.wait_ge(k_sb, t + 2 if k < NB - 1 else NB)
                        if has_sum(k):
                            pe.wait_ge(y_sb, t - 4)
                        if has_v(k):
                            pe.wait_ge(cv_in[w], (t - 1) * 8 + (16 - 8 * w))
                            pe.matmul(QKV[:, 2 * P:3 * P], cv[:, w, :], wv[:, :], start=True, stop=True)\
                              .then_inc(v_ps, 1)
                        if has_sum(k):
                            pe.wait_ge(normed, t - 3)
                            pe.transpose(QKV[:, 3 * P:4 * P], O[:, u, :], ident[:, :]).then_inc(of_ps, 1)
                        if has_values(k):
                            if k >= 3:
                                pe.wait_ge(normed, b)
                            turn_exps(b, u, 1)
                        if has_project(k):
                            if has_values(k):
                                pe.wait_ge(pT_sb, b * 4 + 1)
                            else:
                                pe.wait_ge(xT_sb, t + 2)
                            turn_inputs(t + 2, u)
                        if has_values(k):
                            if k >= 3:
                                pe.wait_ge(o_sb, b)
                            pe.wait_ge(v_sb, b + 1)
                            apply_values(b, u, 0)
                            pe.wait_ge(capped, b * 2 + 2)
                            if has_project(k):
                                pe.wait_ge(xT_sb, b + 5)
                            else:
                                pe.wait_ge(pT_sb, b * 4 + 1)
                            turn_exps(b, u, 2)
                        if has_sum(k):
                            pe.wait_ge(v_sb, t if k <= NB else NB)
                            pe.wait_ge(of_sb, t - 3)
                            pe.matmul(QKV[:, 3 * P:4 * P], OF[:, u, :], wo[:, :], start=True, stop=True)\
                              .then_inc(y_ps, 1)
                        if has_project(k):
                            if k >= 1:
                                pe.wait_ge(v_sb, t)
                            else:
                                pe.wait_ge(q_sb, 2)
                                pe.wait_ge(k_sb, 2)
                            project(t + 2, u)
                        if has_values(k):
                            apply_values(b, u, 1)
                        if has_values(k):
                            turn_exps(b, u, 3)
                            apply_values(b, u, 2)
                            apply_values(b, u, 3)
                    steps(pe, step)

                @blk.scalar
                def _(act):
                    def inputs(b, u, fresh=False):
                        act.wait_ge(inputs_ps, b + 1)
                        if not fresh:
                            act.wait_ge(qk_ps, b - 1)
                        act.activation(xT[:, u, :], IN_BANK[:, 0:P], ACT.Copy).then_inc(xT_sb, 1)

                    def queries_keys(b, u, fresh=False):
                        act.wait_ge(qk_ps, b + 1)
                        if not fresh:
                            act.wait_ge(scored, b * 2 - 2)
                            act.wait_ge(kx_made[0], b - 1)
                            act.wait_ge(kx_made[1], b - 1)
                        act.activation(qT[:, u, :], QKV[:, 0:P], ACT.Identity, bias=bqs[:, :], scale=SCALE)\
                           .then_inc(q_sb, 1)
                        act.activation(kT[:, u, :], QKV[:, P:2 * P], ACT.Identity, bias=bk[:, :])\
                           .then_inc(k_sb, 1)

                    def exponentials(b, u, h, k):
                        act.wait_ge(shifted, b * 2 + (h + 1))
                        if k >= 2:
                            act.wait_ge(pT_ps, b * 4 + (2 * h - 6))
                        act.activation(E[:, 2 * u + h, :, :], D[:, h, :, :], ACT.Exp,
                                       accum_out=expsum[:, bass.ds(b * 2 + h, 1)]).then_inc(expd, 1)

                    def copy_exps(b, g, k):
                        act.wait_ge(pT_ps, b * 4 + (g + 1))
                        if k >= 3:
                            act.wait_ge(pv_ps, b * 4 + (g - 3))
                        act.activation(PT[:, g, :], GROUP_BANK[g][:, :], ACT.Copy).then_inc(pT_sb, 1)

                    def copy_result(b, u, k):
                        act.wait_ge(pv_ps, b * 4 + 4)
                        if k >= 3:
                            act.wait_ge(back_ps, b - 1)
                        act.activation(oT[:, u, :, :], OPS[:, :].rearrange("p (g q) -> p g q", g=4), ACT.Copy)\
                           .then_inc(o_sb, 1)

                    def copy_attention(b, u, k):
                        act.wait_ge(of_ps, b + 1)
                        act.wait_ge(v_sb, b + 4 if k <= NB else NB)
                        act.activation(OF[:, u, :], QKV[:, 3 * P:4 * P], ACT.Copy).then_inc(of_sb, 1)

                    for b in (0, 1):
                        inputs(b, b, fresh=True)
                        queries_keys(b, b, fresh=True)

                    def step(t, u, k):
                        b, w = t - 2, 1 - u
                        if has_values(k):
                            copy_exps(b, 0, k)
                        if has_values(k):
                            copy_exps(b, 1, k)
                        if has_project(k):
                            inputs(t + 2, u)
                        if has_sum(k):
                            copy_attention(t - 4, u, k)
                        if has_values(k):
                            copy_exps(b, 2, k)
                        if has_project(k):
                            queries_keys(t + 2, u)
                        if has_values(k):
                            copy_exps(b, 3, k)
                            copy_result(b, u, k)
                        if has_scores(k):
                            exponentials(t, u, 0, k)
                        if has_scores(k):
                            exponentials(t, u, 1, k)
                    steps(act, step)

                @blk.gpsimd
                def _(pool):
                    def cap(b, u, h):
                        pool.wait_ge(expd, b * 2 + (h + 1))
                        e = E[:, 2 * u + h, :, :]
                        pool.sem_inc(capping, 1)
                        pool.tensor_scalar(e, e, 1.0, None, ALU.min).then_inc(capped, 1)

                    spread_keys(pool, 0, 0, 1, 0)

                    def step(t, u, k):
                        if k < NB - 1:
                            spread_keys(pool, t + 1, 1 - u, 1, k)
                        if has_scores(k):
                            cap(t, u, 0)
                            cap(t, u, 1)
                    steps(pool, step)

                @blk.vector
                def _(dve):
                    def normalise(b, u, fresh=False):
                        if not fresh:
                            dve.wait_ge(inputs_ps, b - 1)
                        dve.tensor_scalar(xn[:, u, :], X[:, b, :], mean[:, bass.ds(b, 1)],
                                          rstd[:, bass.ds(b, 1)], ALU.subtract, ALU.mult).then_inc(xn_made, 1)

                    by_head = [banks[:, :].rearrange("p (h k) -> p h k", h=8) for banks in score_banks]

                    def maxima(c, b, h):
                        dve.wait_ge(scored, b * 2 + (h + 1))
                        return c.mark(dve.tensor_reduce(mx[:, h, :], by_head[h], AX.X, ALU.max))

                    def clip_maxima(c, maxed):
                        clipped = []
                        for h in (0, 1):
                            c.need(maxed[h])
                            clipped.append(c.mark(dve.tensor_scalar(mx[:, h, :], mx[:, h, :], CLAMP, -CLAMP,
                                                                    ALU.min, ALU.max)))
                        return clipped

                    def shift(c, b, k, clipped):
                        for h in (0, 1):
                            if k >= 1:
                                dve.wait_ge(expd, b * 2 + (h - 1))
                            c.need(clipped[h])
                            dve.scalar_tensor_tensor(D[:, h, :, :], by_head[h], -CLAMP,
                                                     spread(mx[:, h, :], [P, 8, P], 2), ALU.max, ALU.subtract)\
                               .then_inc(shifted, 1)

                    def values(b, u, k):
                        dve.wait_ge(v_ps, b + 1)
                        if has_sum(k):
                            dve.wait_ge(of_ps, b - 2)
                        if k >= 3:
                            dve.wait_ge(pv_ps, b * 4 - 4)
                        dve.tensor_tensor(V[:, u, :, 0:DH], QKV[:, 2 * P:3 * P].rearrange("p (h d) -> p h d", h=NH),
                                          bv[:, :].rearrange("p (h d) -> p h d", h=NH), ALU.add).then_inc(v_sb, 1)

                    def invert(c, b, u):
                        dve.wait_ge(back_ps, b + 1)
                        return c.mark(dve.reciprocal(
                            rl[:, u, :], BACK_BANK[:, :].rearrange("p (h d) -> p h d", d=VW)[:, :, DH]))

                    def divide(c, b, u, k, inverted):
                        if k >= 5 or k == INNER:
                            dve.wait_ge(of_ps, b - 1)
                        c.need(inverted)
                        dve.tensor_tensor(O[:, u, :].rearrange("p (h d) -> p h d", h=NH),
                                          BACK_BANK[:, :].rearrange("p (h d) -> p h d", d=VW)[:, :, 0:DH],
                                          spread(rl[:, u, :], [P, NH, DH], 2), ALU.mult).then_inc(normed, 1)

                    def project(b, k):
                        dve.wait_ge(y_ps, b + 1)
                        dve.wait_ge(k_sb, b + 7 if k < NB - 2 else NB)
                        dve.scalar_tensor_tensor(y[:, :], QKV[:, 3 * P:4 * P], gates[:, 0:1], bog[:, :],
                                                 ALU.mult, ALU.add).then_inc(y_sb, 1)

                    def add(c, b):
                        dve.wait_ge(y_sb, b + 1)
                        xb = X[:, b, :]
                        c.link(dve.tensor_tensor(xb, xb, y[:, :], ALU.add))
                        c.link(dve.bn_stats(stats[:, b, :], xb))

                    dve.tensor_scalar(bog[:, :], bo[:, :], gates[:, 0:1], None, ALU.mult).then_inc(bog_made, 1)
                    dve.wait_ge(bog_made, 1)
                    normalise(0, 0, fresh=True)
                    normalise(1, 1, fresh=True)
                    spread_keys(dve, 0, 0, 0, 0)
                    normalise(2, 0)

                    def step(t, u, k):
                        c = Chain(dve, chain_s, links_before(t, k))
                        if k < NB - 1:
                            spread_keys(dve, t + 1, 1 - u, 0, k)
                        if has_scores(k):
                            maxed = [maxima(c, t, 0)]
                        if has_back(k):
                            inverted = invert(c, t - 3, 1 - u)
                            divide(c, t - 3, 1 - u, k, inverted)
                        if has_scores(k):
                            maxed.append(maxima(c, t, 1))
                            clipped = clip_maxima(c, maxed)
                        if has_v(k):
                            values(t - 1, 1 - u, k)
                        if has_scores(k):
                            shift(c, t, k, clipped)
                        if has_sum(k):
                            project(t - 4, k)
                        if k < NB - 3:
                            normalise(t + 3, 1 - u)
                        if has_sum(k):
                            add(c, t - 4)
                    steps(dve, step)

        nan_guard(nc, A, X, CT, expsum, stats, gates, ps)

        t = dict(nc=nc, A=A, X=X, ident=ident, stats=stats, mean=mean, rstd=rstd, lnwork=lnwork, epsc=epsc,
                 gates=gates, ps=ps)
        tern = ctx.enter_context(ExitStack())
        ternary = Ternary(nc, tern)
        with ExitStack() as a:
            r = Routing(nc, a, "e0", keep_xT=False)
            w = GeluWeights(nc, a, "e0w")
            normalise_and_gate(r, lambda sp: load_gelu(w, bsplit, A, sp), first=True, **t)
            route(r, gate=gates[:, 2:3], first=True, **t)
            ternary_keys(ternary, r, xg[0], CT=CT, **t)
            gelu_experts(r, w, xg[0], yg[0], **t)
            combine(r, yg[0], **t)
        ternary_attention(ternary, CT=CT, **t)
        tern.close()
        with ExitStack() as a:
            r = Routing(nc, a, "e1", keep_xT=True)
            w = SwigluWeights(nc, a, "e1w")
            normalise_and_gate(r, lambda sp: load_swiglu(w, bsplit, A, sp), first=False, **t)
            route(r, gate=gates[:, 3:4], first=False, **t)
            for shared in (True, False):
                swiglu_experts(r, w, nc, ident, ps, X, gates[:, 3:4], xg[1], yg[1], shared)
            combine(r, yg[1], out=out, **t)


def nan_guard(nc, A, X, CT, expsum, stats, gates, ps):
    with ExitStack() as a:
        sb = lambda name, shape, dt=F32: a.enter_context(nc.sbuf_tensor(name, shape, dt))
        sems = lambda names: semaphores(nc, a, names.split())
        nans = sb("nans", [P, 4])
        flag = sb("flag", [P, 1], I32)
        wo = sb("g_wo", [P, P]); wv = sb("g_wv", [CC, P]); bv = sb("g_bv", [P, 1]); bo = sb("g_bo", [P, P])
        ctxsum = sb("ctxsum", [CC, NB])
        vbar = sb("vbar", [P, NB])
        vrep = sb("vrep", [P, P])
        (chain, row_flag, all_flag, flagged, loaded, vbar_ps, vrep_made, y_ps, added, summed) = sems(
            "g_chain row_flag all_flag flagged g_loaded vbar_ps vrep_made g_y_ps added g_summed")

        with nc.Block() as blk:
            @blk.gpsimd
            def _(pool):
                pool.wait_ge(row_flag, 1)
                pool.partition_all_reduce(nans[:, 3:4], nans[:, 2:3], P, RED.max).then_inc(all_flag, 1)

            @blk.sync
            def _(sp):
                sp.wait_ge(flagged, 1)
                with sp.If(sp.value_load(flag[0:1, 0:1], min_val=0, max_val=1) > 0):
                    for dst, src in ((X[:, :, :], A["x_T"]),
                                     (wo[:, :], A["L0_xattn_Wo"]), (wv[:, :], A["L0_xattn_Wv"]),
                                     (bv[:, :], A["L0_xattn_bv"].unsqueeze(1)),
                                     (bo[:, :], A["L0_xattn_bo"].partition_broadcast(P))):
                        sp.dma_start(dst, src).then_inc(loaded, 16)
                sp.end_ifs()

            @blk.tensor
            def _(pe):
                pe.wait_ge(flagged, 1)
                with pe.If(pe.value_load(flag[0:1, 0:1], min_val=0, max_val=1) > 0):
                    pe.wait_ge(loaded, 16 * 5)
                    pe.wait_ge(summed, 1)
                    pe.matmul(ps[0][:, 0:NB], wv[:, :], ctxsum[:, :], start=True, stop=True).then_inc(vbar_ps, 1)
                    with pe.Fori(0, NB) as b:
                        pe.wait_ge(vrep_made, b + 1)
                        pe.wait_ge(added, b + 1)
                        pe.matmul(ps[1][:, 0:P], vrep[:, :], wo[:, :], start=True, stop=True).then_inc(y_ps, 1)
                pe.end_ifs()

            @blk.vector
            def _(dve):
                c = Chain(dve, chain)
                c.link(dve.tensor_reduce(nans[:, 0:1], expsum[:, :], AX.X, ALU.add))
                c.link(dve.tensor_tensor(nans[:, 1:2], nans[:, 0:1], nans[:, 0:1], ALU.is_equal))
                dve.tensor_scalar(nans[:, 2:3], nans[:, 1:2], -1.0, 1.0, ALU.mult, ALU.add).then_inc(row_flag, 1)
                dve.wait_ge(all_flag, 1)
                dve.tensor_copy(flag[:, :], nans[:, 3:4]).then_inc(flagged, 1)
                dve.wait_ge(flagged, 1)
                with dve.If(dve.value_load(flag[0:1, 0:1], min_val=0, max_val=1) > 0):
                    dve.sem_inc(added, 1)
                    dve.tensor_reduce(ctxsum[:, :], CT[:, :, :], AX.X, ALU.add).then_inc(summed, 1)
                    dve.wait_ge(vbar_ps, 1)
                    c.link(dve.tensor_scalar(vbar[:, :], ps[0][:, 0:NB], 1.0 / P, bv[:, :], ALU.mult, ALU.add))
                    c.link(dve.tensor_scalar(bo[:, :], bo[:, :], gates[:, 0:1], None, ALU.mult))
                    with dve.Fori(0, NB) as b:
                        dve.tensor_copy(vrep[:, :], vbar[:, bass.ds(b, 1)].broadcast_to([P, P])).then_inc(vrep_made, 1)
                        l = Chain(dve, chain, b * 3 + c.n)
                        dve.wait_ge(y_ps, b + 1)
                        xb = X[:, b, :]
                        l.link(dve.scalar_tensor_tensor(xb, ps[1][:, 0:P], gates[:, 0:1], xb, ALU.mult, ALU.add))
                        l.link(dve.tensor_tensor(xb, xb, bo[:, :], ALU.add))
                        l.link(dve.bn_stats(stats[:, b, :], xb))
                        dve.sem_inc(added, 1)
                dve.end_ifs()


class Routing:

    def __init__(self, nc, stack, name, keep_xT):
        sb = lambda n, shape, dt=F32: stack.enter_context(nc.sbuf_tensor(f"{name}_{n}", shape, dt))
        self.name = name
        self.logits = sb("logits", [P, NB, NE])
        self.slots = sb("slots", [P, TOPK, NB], U32)
        self.weights = sb("weights", [P, TOPK, NB])
        self.tile_expert = sb("tile_expert", [P, TILES], I32)
        self.rows = sb("rows", [P, TOPK, NB, ROW])
        self.xT = sb("xT", [P, NB, P]) if keep_xT else None


def named(nc, stack, name):
    sb = lambda n, shape, dt=F32: stack.enter_context(nc.sbuf_tensor(f"{name}_{n}", shape, dt))
    sems = lambda names: semaphores(nc, stack, [f"{name}_{n}" for n in names.split()])
    return sb, sems


def route(r, gate, nc, A, X, ident, stats, mean, rstd, lnwork, epsc, gates, ps, first):
    with ExitStack() as a:
        sb, sems = named(nc, a, r.name + "r")
        rev = sb("rev", [P, NE])
        jota = sb("jota", [P, TILES])
        before = sb("before", [P, P], BF16)
        ones = sb("ones", [P, P], BF16)
        extra = sb("extra", [P, NE])
        probs = sb("probs", [P, NB, NE]); choice = sb("choice", [P, NB, NE]); w3 = sb("w3", [P, NB, NE])
        hot = sb("hot", [P, TOPK, NB, NE])
        best = sb("best", [P, 4, NB])
        chosen = sb("chosen", [P, NB, NE], BF16)
        cum = sb("cum", [P, 2, NE, NB])
        each = sb("each", [P, NE, NB])
        small = sb("small", [P, 6, NE])
        cmp = sb("cmp", [P, TILES, NE])
        slotf = sb("slotf", [P, TOPK, NB])
        loaded, made, chain, shifted, expd, chosen_r, counted, pool_chain = sems(
            "loaded made chain shifted expd chosen_r counted pool_chain")
        B3 = [P, NB, NE]
        with nc.Block() as blk:
            @blk.sync
            def _(sp):
                src = A["L0_ffn_alpha"] if first else A["L1_ffn_gate_b"]
                sp.dma_start(extra[:, :], src.partition_broadcast(P)).then_inc(loaded, 16)

            @blk.gpsimd
            def _(pool):
                c = Chain(pool, pool_chain)
                c.link(pool.iota(rev[:, :], pattern=[[-1, NE]], base=NE, channel_multiplier=0,
                                 allow_small_or_imprecise_dtypes=True))
                c.link(pool.iota(jota[:, :], pattern=[[1, TILES]], base=0, channel_multiplier=0,
                                 allow_small_or_imprecise_dtypes=True))
                c.link(pool.memset(ones[:, :], 1.0))
                c.link(pool.memset(before[:, :], 1.0))
                c.link(pool.affine_select(out=before[:, :], in_=before[:, :], compare_op=ALU.is_ge, fill=0.0,
                                          base=-1, pattern=[[1, P]], channel_multiplier=-1))
                pool.sem_inc(made, 1)

            @blk.scalar
            def _(act):
                act.wait_ge(shifted, 1)
                act.activation(probs[:, :, :], probs[:, :, :], ACT.Exp).then_inc(expd, 1)

            @blk.tensor
            def _(pe):
                pe.wait_ge(made, 1)
                pe.wait_ge(chosen_r, 1)
                m = chosen[:, :, :]
                pe.matmul(ps[0][:, 0:NB * NE], before[:, :], m, start=True, stop=True)
                pe.matmul(ps[1][:, 0:NB * NE], ones[:, :], m, start=True, stop=True).then_inc(counted, 1)

            @blk.vector
            def _(dve):
                c = Chain(dve, chain)
                tt, ts = dve.tensor_tensor, dve.tensor_scalar
                L = c.link
                m = best[:, 0, :]
                L(dve.tensor_reduce(m, r.logits[:, :, :], AX.X, ALU.max))
                tt(probs[:, :, :], r.logits[:, :, :], spread(m, B3, 2), ALU.subtract).then_inc(shifted, 1)
                dve.wait_ge(expd, 1)
                L(dve.tensor_reduce(m, probs[:, :, :], AX.X, ALU.add))
                L(dve.reciprocal(m, m))
                L(tt(probs[:, :, :], probs[:, :, :], spread(m, B3, 2), ALU.mult))
                dve.wait_ge(loaded, 16)
                dve.wait_ge(made, 1)
                ranked = probs[:, :, :]
                if not first:
                    ranked = choice[:, :, :]
                    L(tt(ranked, probs[:, :, :], spread(extra[:, :], B3, 1), ALU.add))
                for k in range(TOPK):
                    h = hot[:, k, :, :]
                    if k:
                        L(dve.scalar_tensor_tensor(choice[:, :, :], hot[:, 0, :, :], -3.0e38, ranked,
                                                   ALU.mult, ALU.add))
                        ranked = choice[:, :, :]
                    L(dve.tensor_reduce(m, ranked, AX.X, ALU.max))
                    L(tt(w3[:, :, :], ranked, spread(m, B3, 2), ALU.is_equal))
                    L(tt(w3[:, :, :], w3[:, :, :], spread(rev[:, :], B3, 1), ALU.mult))
                    L(dve.tensor_reduce(best[:, 1, :], w3[:, :, :], AX.X, ALU.max))
                    L(tt(h, spread(rev[:, :], B3, 1), spread(best[:, 1, :], B3, 2), ALU.is_equal))
                tt(chosen[:, :, :], hot[:, 0, :, :], hot[:, 1, :, :], ALU.add).then_inc(chosen_r, 1)
                for k in range(TOPK):
                    L(tt(w3[:, :, :], hot[:, k, :, :], probs[:, :, :], ALU.mult))
                    L(dve.tensor_reduce(r.weights[:, k, :], w3[:, :, :], AX.X, ALU.add))
                if first:
                    L(tt(best[:, 2, :], r.weights[:, 0, :], r.weights[:, 1, :], ALU.add))
                    L(dve.reciprocal(best[:, 2, :], best[:, 2, :]))
                    for k in range(TOPK):
                        L(tt(r.weights[:, k, :], r.weights[:, k, :], best[:, 2, :], ALU.mult))
                        L(tt(w3[:, :, :], hot[:, k, :, :], spread(extra[:, :], B3, 1), ALU.mult))
                        L(dve.tensor_reduce(best[:, 3, :], w3[:, :, :], AX.X, ALU.add))
                        L(tt(r.weights[:, k, :], r.weights[:, k, :], best[:, 3, :], ALU.mult))
                for k in range(TOPK):
                    c.mark(ts(r.rows[:, k, :, P + 1], r.weights[:, k, :], gate, None, ALU.mult))
                dve.wait_ge(counted, 1)
                L(dve.tensor_copy(each[:, :, :], ps[1][:, 0:NB * NE].rearrange("p (b e) -> p e b", e=NE)))
                sums, dst, d = each[:, :, :], 0, 1
                while d < NB:
                    c.mark(dve.tensor_copy(cum[:, dst, :, 0:d], sums[:, :, 0:d]))
                    L(tt(cum[:, dst, :, d:NB], sums[:, :, d:NB], sums[:, :, 0:NB - d], ALU.add))
                    sums, src, dst, d = cum[:, dst, :, :], dst, 1 - dst, 2 * d
                ntile, end, start = small[:, 0, :], small[:, 1, :], small[:, 2, :]
                L(ts(ntile, cum[:, src, :, NB - 1], (P - 1) / 2.0, 1.0 / P, ALU.add, ALU.mult))
                L(ts(ntile, ntile, ROUND, -ROUND, ALU.add, ALU.add))
                L(dve.tensor_copy(end, ntile))
                for d in (1, 2, 4):
                    L(dve.tensor_copy(small[:, 3, :], end))
                    L(tt(small[:, 1, d:NE], small[:, 3, d:NE], small[:, 3, 0:NE - d], ALU.add))
                L(tt(start, end, ntile, ALU.subtract))
                L(tt(cum[:, dst, :, :], cum[:, src, :, :], each[:, :, :], ALU.subtract))
                L(dve.scalar_tensor_tensor(cum[:, dst, :, :], spread(start, [P, NE, NB], 2), float(P),
                                           cum[:, dst, :, :], ALU.mult, ALU.add))
                L(tt(w3[:, :, :], ps[0][:, 0:NB * NE].rearrange("p (b e) -> p b e", e=NE),
                     cum[:, dst, :, :].rearrange("p e b -> p b e"), ALU.add))
                for k in range(TOPK):
                    L(tt(choice[:, :, :], hot[:, k, :, :], w3[:, :, :], ALU.mult))
                    L(dve.tensor_reduce(slotf[:, k, :], choice[:, :, :], AX.X, ALU.add))
                L(dve.tensor_copy(r.slots[:, :, :], slotf[:, :, :]))
                C3 = [P, TILES, NE]
                L(tt(cmp[:, :, :], spread(jota[:, :], C3, 2), spread(end, C3, 1), ALU.is_ge))
                L(dve.tensor_reduce(jota[:, :], cmp[:, :, :], AX.X, ALU.add))
                L(ts(r.tile_expert[:, :], jota[:, :], float(NE - 1), None, ALU.min))


BIT_WEIGHTS = (("d2v", CC * P, 0, P), ("img", P * P, P, 2 * P), ("txt", P * P, 2 * P, 3 * P),
               ("att0", P * P // 2, 3 * P, 7 * P // 2), ("att1", P * P // 2, 7 * P // 2, 4 * P),
               ("f1", 2 * P * FF, 4 * P, 12 * P), ("f2", FF * P, 12 * P, 16 * P))
D2V, IMG_W, TXT, ATT0, ATT1, F1, F2 = range(7)
CTX_A, VIS_A, IMG_A, XN_A, CAT_A, HID_A = range(6)
QMAX = 127.0
GB = 4
G = NB // GB
GW = GB * P


class Ternary:

    def __init__(self, nc, stack):
        sb, _ = named(nc, stack, "t")
        self.qW = sb("qW", [P, 16 * P], BF16)
        self.katt = sb("katt", [P, 2, 2, P // 2], BF16)
        self.bias = sb("bias", [P, 9])
        self.rowbias = sb("rowbias", [P, 3, P])
        self.wsc = sb("wsc", [P, 7])
        self.amax = sb("amax", [P, 6]); self.gm = sb("gm", [1, 6])
        self.isc = sb("isc", [P, 6]); self.inv = sb("inv", [P, 6])
        self.osc = sb("osc", [P, 7])
        self.imgq = sb("imgq", [P, NB, P], BF16)
        self.K = [sb("K0", [P, NB, P]), sb("K1", [P, NB, P])]
        self.avg = sb("avg", [P, NB])
        self.ones = sb("ones", [P, P])


class LargestOfAll:

    def __init__(self, nc, stack, name, k, bank, ident):
        _, sems = named(nc, stack, name)
        self.amax_r, self.turned, self.one, self.spread, self.done = sems("amax_r turned one spread done")
        self.k, self.bank, self.ident = k, bank, ident

    def tensor(self, pe, a, n=1):
        k = self.k
        pe.wait_ge(self.amax_r, n)
        pe.transpose(self.bank[0:1, 0:P], k.amax[:, a:a + 1], self.ident[:, :]).then_inc(self.turned, 1)
        pe.wait_ge(self.one, n)
        pe.matmul(self.bank[:, P:P + 1], k.ones[0:1, :], k.gm[0:1, a:a + 1], start=True, stop=True)\
          .then_inc(self.spread, 1)

    def vector(self, dve, L, a, layers, n=1):
        k = self.k
        dve.wait_ge(self.turned, n)
        dve.tensor_reduce(k.gm[0:1, a:a + 1], self.bank[0:1, 0:P], AX.X, ALU.max).then_inc(self.one, 1)
        dve.wait_ge(self.spread, n)
        L(dve.tensor_scalar(k.isc[:, a:a + 1], self.bank[:, P:P + 1], 1e-8, 1.0 / QMAX, ALU.max, ALU.mult))
        L(dve.reciprocal(k.inv[:, a:a + 1], k.isc[:, a:a + 1]))
        for w in layers:
            L(dve.tensor_tensor(k.osc[:, w:w + 1], k.isc[:, a:a + 1], k.wsc[:, w:w + 1], ALU.mult))
        dve.sem_inc(self.done, 1)


def ternary_keys(k, r, xg, nc, A, X, CT, ident, stats, mean, rstd, lnwork, epsc, gates, ps):
    with ExitStack() as a:
        sb, sems = named(nc, a, "tk")
        W = sb("W", [P, 16 * P])
        neg = sb("neg", [P, 8 * P])
        wsum = sb("wsum", [P, 7]); thr = sb("thr", [P, 2, 7])
        counts = sb("counts", [P, 7])
        scaled = sb("scaled", [P, 2, GW])
        qin = sb("qin", [P, NB, P], BF16)
        vis = k.K[0]
        img = sb("img", [P, NB, P])
        partmax = sb("partmax", [P, G])
        qW, katt, bias, osc, inv, amax, K, avg, imgq = (k.qW, k.katt, k.bias, k.osc, k.inv, k.amax, k.K, k.avg,
                                                        k.imgq)
        MAX_BANK = ps[7]
        largest_of = LargestOfAll(nc, a, "tkm", k, MAX_BANK, ident)
        (wload, chain, wsum_r, wtot_ps, sent, counts_r, pool_chain, scaled_r, q_r, out_ps, out_r, chunk_max, avg_r) = sems(
            "wload chain wsum_r wtot_ps sent counts_r pool_chain scaled_r q_r out_ps out_r chunk_max avg_r")
        stages = ((CT, CTX_A, D2V, vis, VIS_A, qin), (vis, VIS_A, IMG_W, img, IMG_A, qin),
                  (img, IMG_A, ATT0, K[0], None, imgq), (None, IMG_A, ATT1, K[1], None, imgq))
        with nc.Block() as blk:
            @blk.sync
            def _(sp):
                sp.dma_start(W[:, :], A["bit_weights"]).then_inc(wload, 16)
                sp.dma_start(bias[:, :], A["bit_bias"]).then_inc(wload, 16)
                sp.dma_start(k.rowbias[:, :, :], A["bit_rowbias"].partition_broadcast(P)).then_inc(wload, 16)

            @blk.gpsimd
            def _(pool):
                c = Chain(pool, pool_chain)
                for n, (_, count, _, _) in enumerate(BIT_WEIGHTS):
                    m = c.mark(pool.memset(counts[:, n:n + 1], 1.0 / count))
                c.need(m)
                c.link(pool.memset(k.ones[:, :], 1.0))
                pool.sem_inc(counts_r, 1)
                scatter_rows(r, xg, pool, sent)

            @blk.scalar
            def _(act):
                for n, (src, ain, w, dst, aout, q) in enumerate(stages):
                    act.wait_ge(largest_of.done, min(n, 2) + 1)
                    K0 = CC if n == 0 else P

                    def scale(g, u, wait, base):
                        if wait:
                            act.wait_ge(q_r, base + (g - 1))
                        act.activation(scaled[0:K0, u, :], src[:, bass.ds(g * GB, GB), :], ACT.Copy,
                                       scale=inv[0:K0, ain:ain + 1]).then_inc(scaled_r, 1)

                    def output(g, u, n=n, dst=dst, w=w):
                        act.wait_ge(out_ps, g + (n * G + 1))
                        act.activation(dst[:, bass.ds(g * GB, GB), :], ps[u][:, :], ACT.Identity,
                                       bias=bias[:, w:w + 1], scale=osc[:, w:w + 1]).then_inc(out_r, 1)

                    if src is not None:
                        base = n * G
                        scale(0, 0, False, base)
                        scale(1, 1, False, base)
                        with act.Fori(0, (G - 2) // 2) as i:
                            for u in (0, 1):
                                output(i * 2 + u, u)
                                scale(i * 2 + (u + 2), u, True, base)
                        output(G - 2, 0)
                        output(G - 1, 1)
                    else:
                        with act.Fori(0, G // 2) as i:
                            for u in (0, 1):
                                output(i * 2 + u, u)

            @blk.tensor
            def _(pe):
                pe.wait_ge(counts_r, 1)
                pe.wait_ge(wsum_r, 1)
                pe.matmul(ps[6][:, 0:7], k.ones[:, :], wsum[:, :], start=True, stop=True)\
                  .then_inc(wtot_ps, 1)
                largest_of.tensor(pe, CTX_A, 1)
                for n, (src, ain, w, dst, aout, q) in enumerate(stages):
                    K0 = CC if n == 0 else P
                    lhs = katt[:, n - 2, :, :] if n >= 2 else qW[0:K0, BIT_WEIGHTS[w][2]:BIT_WEIGHTS[w][3]]
                    with pe.Fori(0, G // 2) as i:
                        for u in (0, 1):
                            g = i * 2 + u
                            if n < 3:
                                pe.wait_ge(q_r, g + (n * G + 1))
                            if n:
                                pe.wait_ge(out_r, g + (n * G - 1))
                            pe.matmul(ps[u][:, :], lhs, q[0:K0, bass.ds(g * GB, GB), :], start=True, stop=True)\
                              .then_inc(out_ps, 1)
                    if aout is not None:
                        largest_of.tensor(pe, aout, n + 2)

            @blk.vector
            def _(dve):
                c = Chain(dve, chain)
                L = c.link
                L(dve.memset(amax[:, :], 0.0))
                dve.tensor_reduce(amax[0:CC, CTX_A:CTX_A + 1], CT[:, :, :], AX.XY, ALU.max,
                                  apply_absolute_value=True).then_inc(largest_of.amax_r, 1)
                dve.wait_ge(wload, 48)
                dve.wait_ge(counts_r, 1)
                for n, (_, _, c0, c1) in enumerate(BIT_WEIGHTS):
                    m = c.mark(dve.tensor_reduce(wsum[:, n:n + 1], W[:, c0:c1], AX.X, ALU.add,
                                                 apply_absolute_value=True))
                c.need(m)
                dve.sem_inc(wsum_r, 1)
                dve.wait_ge(wtot_ps, 1)
                L(dve.tensor_tensor(k.wsc[:, :], ps[6][:, 0:7], counts[:, :], ALU.mult))
                L(dve.tensor_scalar(k.wsc[:, :], k.wsc[:, :], 1e-5, None, ALU.max))
                c.mark(dve.tensor_scalar(thr[:, 0, :], k.wsc[:, :], 0.5, None, ALU.mult))
                L(dve.tensor_scalar(thr[:, 1, :], k.wsc[:, :], -0.5, None, ALU.mult))
                for n, (_, _, c0, c1) in enumerate(BIT_WEIGHTS):
                    L(dve.tensor_scalar(neg[:, 0:c1 - c0], W[:, c0:c1], thr[:, 1, n:n + 1], None, ALU.is_lt))
                    L(dve.scalar_tensor_tensor(qW[:, c0:c1], W[:, c0:c1], thr[:, 0, n:n + 1], neg[:, 0:c1 - c0],
                                               ALU.is_gt, ALU.subtract))
                L(dve.tensor_copy(katt[:, :, :, :], spread(
                    qW[:, 3 * P:4 * P].rearrange("p (a f) -> p a f", a=2), [P, 2, 2, P // 2], 2)))
                largest_of.vector(dve, L, CTX_A, (D2V,), 1)
                for n, (src, ain, w, dst, aout, q) in enumerate(stages):
                    K0 = CC if n == 0 else P

                    def rounded(g, u, n=n, q=q, K0=K0):
                        dve.wait_ge(scaled_r, g + (n * G + 1))
                        dve.tensor_scalar(q[0:K0, bass.ds(g * GB, GB), :],
                                          scaled[0:K0, u, :].rearrange("p (b q) -> p b q", q=P), ROUND, -ROUND,
                                          ALU.add, ALU.add).then_inc(q_r, 1)

                    def largest(g, n=n, dst=dst):
                        dve.wait_ge(out_r, g + (n * G + 1))
                        dve.tensor_reduce(partmax[:, bass.ds(g, 1)], dst[:, bass.ds(g * GB, GB), :], AX.XY,
                                          ALU.max, apply_absolute_value=True).then_inc(chunk_max, 1)

                    if src is None:
                        continue
                    rounded(0, 0)
                    rounded(1, 1)
                    with dve.Fori(0, (G - 2) // 2) as i:
                        for u in (0, 1):
                            if aout is not None:
                                largest(i * 2 + u)
                            rounded(i * 2 + (u + 2), u)
                    if aout is not None:
                        largest(G - 2)
                        largest(G - 1)
                        dve.wait_ge(chunk_max, (n + 1) * G)
                        dve.tensor_reduce(amax[:, aout:aout + 1], partmax[:, 0:G], AX.X, ALU.max)\
                           .then_inc(largest_of.amax_r, 1)
                        largest_of.vector(dve, L, aout, (IMG_W,) if aout == VIS_A else (ATT0, ATT1), n + 2)
                    if n == 2:
                        dve.tensor_reduce(avg[:, :], img[:, :, :], AX.X, ALU.add).then_inc(avg_r, 1)
                        dve.wait_ge(avg_r, 1)
                        L(dve.tensor_scalar(avg[:, :], avg[:, :], 1.0 / P, None, ALU.mult))

def ternary_attention(k, nc, A, X, CT, ident, stats, mean, rstd, lnwork, epsc, gates, ps):
    with ExitStack() as a:
        sb, sems = named(nc, a, "t")
        qW, katt, bias, rowbias, osc, inv, amax, K, avg, imgq = (
            k.qW, k.katt, k.bias, k.rowbias, k.osc, k.inv, k.amax, k.K, k.avg, k.imgq)
        largest_of = LargestOfAll(nc, a, "tm", k, ps[7], ident)
        partmax = sb("partmax", [P, 4 * G])
        hsc = sb("hsc", [P, 1]); hbias = sb("hbias", [P, 4])
        hraw = sb("hraw", [P, 4])
        gf2 = sb("gf2", [P, 1]); gb2 = sb("gb2", [P, P])
        identb = sb("identb", [P, P], BF16)
        scaled = sb("scaled", [P, 2, GW])
        qin = sb("qin", [P, NB, P], BF16)
        fused = sb("fused", [P, NB, P]); xn = sb("xn", [P, NB, P])
        avgq = sb("avgq", [P, NB], BF16)

        with ExitStack() as s:
            ssb, ssems = named(nc, s, "tx")
            scaled_r, q_r, xn_r, turned, qT_r, out_ps, out_r, chain, var_r, std_r, stat_done, identb_r = ssems(
                "scaled_r q_r xn_r turned qT_r out_ps out_r chain var_r std_r stat_done identb_r")
            xq = ssb("xq", [P, 2, GW], BF16)
            with nc.Block() as blk:
                @blk.gpsimd
                def _(pool):
                    pool.memset(identb[:, :], 0.0).then_inc(identb_r, 1)
                    pool.wait_ge(identb_r, 1)
                    pool.affine_select(out=identb[:, :], in_=identb[:, :], compare_op=ALU.not_equal, fill=1.0,
                                       base=0, pattern=[[-1, P]], channel_multiplier=1).then_inc(identb_r, 1)

                @blk.scalar
                def _(act):
                    act.wait_ge(var_r, 1)
                    act.activation(lnwork[:, 3, :], lnwork[:, 2, :], ACT.Sqrt, bias=epsc[:, :], scale=1.0 / P)\
                       .then_inc(std_r, 1)
                    act.wait_ge(largest_of.done, 1)

                    def scale(g, u, fresh=False):
                        if not fresh:
                            act.wait_ge(q_r, g - 1)
                        act.activation(scaled[:, u, :], xn[:, bass.ds(g * GB, GB), :], ACT.Copy,
                                       scale=inv[:, XN_A:XN_A + 1]).then_inc(scaled_r, 1)

                    def output(g, u):
                        act.wait_ge(out_ps, g + 1)
                        act.activation(fused[:, bass.ds(g * GB, GB), :], ps[4 + u][:, :], ACT.Identity,
                                       bias=bias[:, TXT:TXT + 1], scale=osc[:, TXT:TXT + 1]).then_inc(out_r, 1)
                    scale(0, 0, fresh=True)
                    scale(1, 1, fresh=True)
                    with act.Fori(0, (G - 2) // 2) as i:
                        for u in (0, 1):
                            scale(i * 2 + (u + 2), u)
                            output(i * 2 + u, u)
                    output(G - 2, 0)
                    output(G - 1, 1)

                @blk.tensor
                def _(pe):
                    pe.wait_ge(identb_r, 2)
                    largest_of.tensor(pe, XN_A, 1)
                    pe.sem_inc(turned, 2)
                    pe.sem_inc(qT_r, 2)
                    pe.sem_inc(out_r, 2)

                    def turn(g, u):
                        pe.wait_ge(q_r, g + 1)
                        pe.wait_ge(qT_r, g + 1)
                        for j in range(GB):
                            mm = pe.matmul(ps[u][:, j * P:(j + 1) * P], xq[:, u, j * P:(j + 1) * P],
                                           identb[:, :], start=True, stop=True)
                        mm.then_inc(turned, 1)

                    def product(g, u):
                        pe.wait_ge(qT_r, g + 3)
                        pe.wait_ge(out_r, g + 1)
                        pe.matmul(ps[4 + u][:, :], qW[:, 2 * P:3 * P], qin[:, bass.ds(g * GB, GB), :],
                                  start=True, stop=True).then_inc(out_ps, 1)
                    turn(0, 0)
                    turn(1, 1)
                    with pe.Fori(0, (G - 2) // 2) as i:
                        for u in (0, 1):
                            product(i * 2 + u, u)
                            turn(i * 2 + (u + 2), u)
                    product(G - 2, 0)
                    product(G - 1, 1)

                @blk.vector
                def _(dve):
                    c = Chain(dve, chain)
                    ln_statistics(dve, c.link, stats, mean, rstd, lnwork, var_r, std_r, stat_done)
                    dve.wait_ge(stat_done, 1)
                    with dve.Fori(0, NB // 8) as i:
                        for j in range(8):
                            b = i * 8 + j
                            dve.tensor_scalar(xn[:, b, :], X[:, b, :], mean[:, bass.ds(b, 1)],
                                              rstd[:, bass.ds(b, 1)], ALU.subtract, ALU.mult).then_inc(xn_r, 1)
                    dve.wait_ge(xn_r, NB)
                    dve.tensor_reduce(amax[:, XN_A:XN_A + 1], xn[:, :, :], AX.XY, ALU.max,
                                      apply_absolute_value=True).then_inc(largest_of.amax_r, 1)
                    largest_of.vector(dve, c.link, XN_A, (TXT,), 1)

                    def quantise(g, u):
                        dve.wait_ge(scaled_r, g + 1)
                        dve.wait_ge(turned, g + 1)
                        dve.tensor_scalar(xq[:, u, :], scaled[:, u, :], ROUND, -ROUND, ALU.add, ALU.add)\
                           .then_inc(q_r, 1)

                    def copy(g, u):
                        dve.wait_ge(turned, g + 3)
                        dve.tensor_copy(qin[:, bass.ds(g * GB, GB), :],
                                        ps[u][:, :].rearrange("p (b q) -> p b q", q=P)).then_inc(qT_r, 1)
                    quantise(0, 0)
                    quantise(1, 1)
                    with dve.Fori(0, (G - 2) // 2) as i:
                        for u in (0, 1):
                            copy(i * 2 + u, u)
                            quantise(i * 2 + (u + 2), u)
                    copy(G - 2, 0)
                    copy(G - 1, 1)

        with ExitStack() as s:
            ssb, ssems = named(nc, s, "ta")
            fg = [ssb("fg0", [P, 2, GW]), ssb("fg1", [P, 2, GW])]
            ktok = [ssb("ktok0", [P, 2, GW]), ssb("ktok1", [P, 2, GW])]
            mx = ssb("mx", [P, 2, GB]); nm = ssb("nm", [P, 2, GB])
            E = ssb("E", [P, 2, GW]); esum = ssb("esum", [P, 2, GB]); rl = ssb("rl", [P, 2, GB])
            PT = ssb("PT", [P, 2, GW])
            each = ssems("f_in " + " ".join(f"{n}0 {n}1" for n in
                                            "kt_ps kt_r s_ps m_r e_r n_r t_ps t_r o_ps f_r ach".split()))
            f_in = each[0]
            kt_ps, kt_r, s_ps, m_r, e_r, n_r, t_ps, t_r, o_ps, f_r, ach = [
                each[n:n + 2] for n in range(1, len(each), 2)]
            ISQ = P ** -0.5
            KT_BANK = (ps[0], ps[1])
            S_BANK, T_BANK, O_BANK = (ps[2], ps[3]), (ps[4], ps[5]), (ps[6], ps[7])

            def rounds(eng, step):
                for g in (0, 1):
                    step(g, g % 2, g)
                with eng.Fori(0, (G - 4) // 2) as i:
                    for n in (0, 1):
                        step(i * 2 + (2 + n), n, None)
                for g in (G - 2, G - 1, G):
                    step(g, g % 2, g)

            def has(k, back):
                return k is None or 0 <= k - back < G

            with nc.Block() as blk:
                @blk.tensor
                def _(pe):
                    def keys(o, g, u, k):
                        if later(k, -1 if o == 0 else 0, 1):
                            pe.wait_ge(kt_r[o], g)
                        for j in range(GB):
                            mm = pe.matmul(KT_BANK[o][:, j * P:(j + 1) * P],
                                           imgq[:, bass.ds(g * GB + j, 1), :], katt[:, o, :, :],
                                           start=True, stop=True)
                        mm.then_inc(kt_ps[o], 1)

                    def score(o, g, u, k):
                        pe.wait_ge(f_in if o == 0 else f_r[0], g + 1)
                        if later(k, -1 if o == 0 else 0, 1):
                            pe.wait_ge(e_r[o], g * GB)
                        for j in range(GB):
                            mm = pe.matmul(S_BANK[o][:, j * P:(j + 1) * P], fg[o][:, u, j * P:(j + 1) * P],
                                           K[o][:, bass.ds(g * GB + j, 1), :], start=True, stop=True)
                        mm.then_inc(s_ps[o], 1)

                    def turn(o, g, u, k):
                        pe.wait_ge(n_r[o], g + 1)
                        if later(k, o, 1):
                            pe.wait_ge(t_r[o], g)
                        for j in range(GB):
                            mm = pe.transpose(T_BANK[o][:, j * P:(j + 1) * P], E[:, o, j * P:(j + 1) * P], ident[:, :])
                        mm.then_inc(t_ps[o], 1)

                    def apply(o, g, u, k):
                        pe.wait_ge(t_r[o], g + 1)
                        pe.wait_ge(kt_r[o], g + 1)
                        if later(k, o, 1):
                            pe.wait_ge(f_r[o], g)
                        for j in range(GB):
                            mm = pe.matmul(O_BANK[o][:, j * P:(j + 1) * P], ktok[o][:, u, j * P:(j + 1) * P],
                                           PT[:, o, j * P:(j + 1) * P], start=True, stop=True)
                        mm.then_inc(o_ps[o], 1)

                    def step(g, u, k):
                        w = 1 - u
                        if has(k, 0):
                            turn(0, g, u, k)
                        if has(k, -1):
                            score(0, g + 1, w, k)
                            keys(0, g + 1, w, k)
                        if has(k, 1):
                            turn(1, g - 1, w, k)
                        if has(k, 0):
                            apply(0, g, u, k)
                            keys(1, g, u, k)
                        if has(k, 1):
                            apply(1, g - 1, w, k)
                        if has(k, 0):
                            score(1, g, u, k)
                    keys(0, 0, 0, -1)
                    score(0, 0, 0, -1)
                    rounds(pe, step)

                @blk.scalar
                def _(act):
                    def exps(o, g, u, k):
                        act.wait_ge(m_r[o], g + 1)
                        if later(k, -1 if o == 0 else 0, 1):
                            act.wait_ge(t_ps[o], g)
                        for j in range(GB):
                            act.activation(E[:, o, j * P:(j + 1) * P], S_BANK[o][:, j * P:(j + 1) * P], ACT.Exp,
                                           bias=nm[:, o, j:j + 1], scale=ISQ,
                                           accum_out=esum[:, o, j:j + 1]).then_inc(e_r[o], 1)

                    def copy(o, g, u, k):
                        act.wait_ge(t_ps[o], g + 1)
                        if later(k, o, 1):
                            act.wait_ge(o_ps[o], g)
                        act.activation(PT[:, o, :], T_BANK[o][:, :], ACT.Copy).then_inc(t_r[o], 1)

                    def step(g, u, k):
                        if has(k, 0):
                            copy(0, g, u, k)
                        if has(k, 1):
                            copy(1, g - 1, 1 - u, k)
                        if has(k, -1):
                            exps(0, g + 1, 1 - u, k)
                        if has(k, 0):
                            exps(1, g, u, k)
                    exps(0, 0, 0, -1)
                    rounds(act, step)

                @blk.vector
                def _(dve):
                    def fetch(g, u, k):
                        if later(k, -2, 2):
                            dve.wait_ge(o_ps[0], g - 1)
                            dve.wait_ge(f_r[0], g - 1)
                        dve.tensor_copy(fg[0][:, u, :].rearrange("p (b q) -> p b q", q=P),
                                        fused[:, bass.ds(g * GB, GB), :]).then_inc(f_in, 1)

                    def keys(o, g, u, k):
                        dve.wait_ge(kt_ps[o], g + 1)
                        if later(k, -1 if o == 0 else 0, 2):
                            dve.wait_ge(o_ps[o], g - 1)
                        dve.scalar_tensor_tensor(
                            ktok[o][:, u, :].rearrange("p (b f) -> p b f", f=P),
                            KT_BANK[o][:, :].rearrange("p (b f) -> p b f", f=P), osc[:, ATT0 + o:ATT0 + o + 1],
                            spread(rowbias[:, o, :], [P, GB, P], 1), ALU.mult, ALU.add).then_inc(kt_r[o], 1)

                    def maximum(o, g, u):
                        dve.wait_ge(s_ps[o], g + 1)
                        c = Chain(dve, ach[o], g * 2)
                        c.link(dve.tensor_reduce(mx[:, o, :], S_BANK[o][:, :].rearrange("p (b k) -> p b k", k=P),
                                                 AX.X, ALU.max))
                        dve.tensor_scalar(nm[:, o, :], mx[:, o, :], -ISQ, None, ALU.mult).then_inc(m_r[o], 1)

                    def normalise(o, g, u):
                        dve.wait_ge(e_r[o], g * GB + GB)
                        c = Chain(dve, ach[o], g * 2 + 1)
                        c.link(dve.reciprocal(rl[:, o, :], esum[:, o, :]))
                        e = E[:, o, :].rearrange("p (b k) -> p b k", k=P)
                        dve.scalar_tensor_tensor(e, e, 0.1, spread(rl[:, o, :], [P, GB, P], 2),
                                                 ALU.mult, ALU.mult).then_inc(n_r[o], 1)

                    def add(o, g, u, k):
                        dve.wait_ge(o_ps[o], g + 1)
                        if o == 0 and later(k, 0, 2):
                            dve.wait_ge(f_r[1], g - 1)
                        shape = "p (b q) -> p b q"
                        to = fg[1][:, u, :].rearrange(shape, q=P) if o == 0 else fused[:, bass.ds(g * GB, GB), :]
                        dve.tensor_tensor(to, fg[o][:, u, :].rearrange(shape, q=P),
                                          O_BANK[o][:, :].rearrange(shape, q=P), ALU.add).then_inc(f_r[o], 1)

                    def step(g, u, k):
                        w = 1 - u
                        if has(k, -1):
                            maximum(0, g + 1, w)
                            keys(0, g + 1, w, k)
                        if has(k, 0):
                            add(0, g, u, k)
                        if has(k, -2):
                            fetch(g + 2, u, k)
                        if has(k, 1):
                            add(1, g - 1, w, k)
                        if has(k, 0):
                            keys(1, g, u, k)
                            maximum(1, g, u)
                        if has(k, -1):
                            normalise(0, g + 1, w)
                        if has(k, 0):
                            normalise(1, g, u)
                    fetch(0, 0, -2)
                    fetch(1, 1, -1)
                    maximum(0, 0, 0)
                    keys(0, 0, 0, -1)
                    normalise(0, 0, 0)
                    rounds(dve, step)

        with ExitStack() as s:
            ssb, ssems = named(nc, s, "tf")
            hin = ssb("hin", [P, 4, GW])
            hq = ssb("hq", [P, 2, 4, GW], BF16)
            (chain2, chunk_max, scaled_r, q_r, avg_r, h_ps, h_max, hs_r, h2_ps, h2_r, hq_r, y_ps, y_r, xb_r, gb2_r, biased) = ssems(
                "chain2 chunk_max scaled_r q_r avg_r h_ps h_max hs_r h2_ps h2_r hq_r y_ps y_r xb_r gb2_r biased")

            def hidden_product(pe, bank, c, g):
                pe.matmul(bank[:, :], qW[:, 4 * P + c * P:5 * P + c * P], qin[:, bass.ds(g * GB, GB), :],
                          start=True, stop=False)
                return pe.matmul(bank[:, :], qW[:, 8 * P + c * P:9 * P + c * P],
                                 spread(avgq[:, bass.ds(g * GB, GB)], [P, GB, P], 2), start=False, stop=True)

            with nc.Block() as blk:
                @blk.gpsimd
                def _(pool):
                    pool.wait_ge(gb2_r, 1)
                    pool.tensor_tensor(X[:, :, :], X[:, :, :], spread(gb2[:, :], [P, NB, P], 1), ALU.add)\
                        .then_inc(biased, 1)

                @blk.tensor
                def _(pe):
                    largest_of.tensor(pe, CAT_A, 2)
                    pe.sem_inc(h_max, 8)
                    with pe.Fori(0, G // 2) as i:
                        for n in (0, 1):
                            g = i * 2 + n
                            pe.wait_ge(q_r, g + 1)
                            pe.wait_ge(avg_r, 1)
                            for c in range(4):
                                pe.wait_ge(h_max, g * 4 + (c + 1))
                                hidden_product(pe, ps[4 * n + c], c, g).then_inc(h_ps, 1)
                    largest_of.tensor(pe, HID_A, 3)
                    pe.wait_ge(hs_r, 1)
                    def hidden(g, u):
                        for c in range(4):
                            pe.wait_ge(h2_r, g * 4 + (c + 1))
                            hidden_product(pe, ps[c], c, g).then_inc(h2_ps, 1)

                    def output(g, u):
                        pe.wait_ge(hq_r, g * 4 + 8)
                        pe.wait_ge(y_r, g * 4 + 1)
                        for j in range(GB):
                            for c in range(4):
                                mm = pe.matmul(ps[6 + u][:, j * P:(j + 1) * P], hq[:, u, c, j * P:(j + 1) * P],
                                               qW[:, (12 + c) * P:(13 + c) * P], start=(c == 0), stop=(c == 3))
                        mm.then_inc(y_ps, 1)
                    pe.sem_inc(h2_r, 4)
                    pe.sem_inc(y_r, 8)
                    hidden(0, 0)
                    hidden(1, 1)
                    with pe.Fori(0, (G - 2) // 2) as i:
                        for n in (0, 1):
                            output(i * 2 + n, n)
                            hidden(i * 2 + (n + 2), n)
                    output(G - 2, 0)
                    output(G - 1, 1)

                @blk.scalar
                def _(act):
                    act.wait_ge(largest_of.done, 2)

                    def scale(g, u, fresh=False):
                        if not fresh:
                            act.wait_ge(q_r, g - 1)
                        act.activation(scaled[:, u, :], fused[:, bass.ds(g * GB, GB), :], ACT.Copy,
                                       scale=inv[:, CAT_A:CAT_A + 1]).then_inc(scaled_r, 1)
                    scale(0, 0, fresh=True)
                    scale(1, 1, fresh=True)
                    with act.Fori(0, (G - 2) // 2) as i:
                        for u in (0, 1):
                            scale(i * 2 + (u + 2), u)
                    act.wait_ge(hs_r, 1)
                    with act.Fori(0, G) as g:
                        for c in range(4):
                            act.wait_ge(h2_ps, g * 4 + (c + 1))
                            act.wait_ge(hq_r, g * 4 + (c + 1))
                            act.activation(hin[:, c, :], ps[c][:, :], ACT.Relu, bias=hbias[:, c:c + 1],
                                           scale=hsc[:, :]).then_inc(h2_r, 1)

                @blk.vector
                def _(dve):
                    c = Chain(dve, chain2)
                    L = c.link
                    L(dve.tensor_reduce(partmax[:, 0:1], fused[:, :, :], AX.XY, ALU.max, apply_absolute_value=True))
                    L(dve.tensor_reduce(partmax[:, 1:2], avg[:, :], AX.X, ALU.max, apply_absolute_value=True))
                    dve.tensor_reduce(amax[:, CAT_A:CAT_A + 1], partmax[:, 0:2], AX.X, ALU.max)\
                       .then_inc(largest_of.amax_r, 1)
                    largest_of.vector(dve, L, CAT_A, (F1,), 2)
                    L(dve.tensor_scalar(avg[:, :], avg[:, :], inv[:, CAT_A:CAT_A + 1], None, ALU.mult))
                    dve.tensor_scalar(avgq[:, :], avg[:, :], ROUND, -ROUND, ALU.add, ALU.add).then_inc(avg_r, 1)
                    dve.tensor_scalar(gb2[:, :], rowbias[:, 2, :], gates[:, 1:2], None, ALU.mult).then_inc(gb2_r, 1)
                    def quantise(g, u):
                        dve.wait_ge(scaled_r, g + 1)
                        dve.tensor_scalar(qin[:, bass.ds(g * GB, GB), :],
                                          scaled[:, u, :].rearrange("p (b q) -> p b q", q=P), ROUND, -ROUND,
                                          ALU.add, ALU.add).then_inc(q_r, 1)

                    def maxima(g, u):
                        for c in range(4):
                            dve.wait_ge(h_ps, g * 4 + (c + 1))
                            dve.tensor_reduce(partmax[:, bass.ds(g + c * G, 1)], ps[4 * u + c][:, :], AX.X,
                                              ALU.max).then_inc(h_max, 1)
                    quantise(0, 0)
                    quantise(1, 1)
                    with dve.Fori(0, (G - 2) // 2) as i:
                        for u in (0, 1):
                            maxima(i * 2 + u, u)
                            quantise(i * 2 + (u + 2), u)
                    maxima(G - 2, 0)
                    maxima(G - 1, 1)
                    dve.wait_ge(h_max, 8 + 4 * G)
                    L(dve.tensor_reduce(hraw[:, :], partmax[:, :].rearrange("p (c g) -> p c g", c=4), AX.X, ALU.max))
                    L(dve.scalar_tensor_tensor(hraw[:, :], hraw[:, :], osc[:, F1:F1 + 1], bias[:, 5:9],
                                               ALU.mult, ALU.add))
                    L(dve.tensor_scalar(hraw[:, :], hraw[:, :], 0.0, None, ALU.max))
                    dve.tensor_reduce(amax[:, HID_A:HID_A + 1], hraw[:, :], AX.X, ALU.max)\
                       .then_inc(largest_of.amax_r, 1)
                    largest_of.vector(dve, L, HID_A, (F2,), 3)
                    L(dve.tensor_tensor(hsc[:, :], osc[:, F1:F1 + 1], inv[:, HID_A:HID_A + 1], ALU.mult))
                    L(dve.tensor_scalar(hbias[:, :], bias[:, 5:9], inv[:, HID_A:HID_A + 1], None, ALU.mult))
                    L(dve.tensor_tensor(gf2[:, :], osc[:, F2:F2 + 1], gates[:, 1:2], ALU.mult))
                    dve.sem_inc(hs_r, 1)

                    dve.sem_inc(hq_r, 4)
                    dve.wait_ge(biased, 1)

                    def rounded(g, u):
                        for k in range(4):
                            dve.wait_ge(h2_r, g * 4 + (k + 5))
                            if k == 0 and (not isinstance(g, int) or g > 1):
                                dve.wait_ge(y_ps, g - 1)
                            dve.tensor_scalar(hq[:, u, k, :], hin[:, k, :], ROUND, -ROUND, ALU.add, ALU.add)\
                               .then_inc(hq_r, 1)

                    def add(g, u):
                        dve.wait_ge(y_ps, g + 1)
                        xb = X[:, bass.ds(g * GB, GB), :]
                        l = Chain(dve, xb_r, g)
                        l.link(dve.scalar_tensor_tensor(xb, ps[6 + u][:, :].rearrange("p (b f) -> p b f", f=P),
                                                        gf2[:, :], xb, ALU.mult, ALU.add))
                        for j in range(GB):
                            dve.bn_stats(stats[:, bass.ds(g * GB + j, 1), :], X[:, bass.ds(g * GB + j, 1), :])\
                               .then_inc(y_r, 1)
                    rounded(0, 0)
                    rounded(1, 1)
                    with dve.Fori(0, (G - 2) // 2) as i:
                        for n in (0, 1):
                            add(i * 2 + n, n)
                            rounded(i * 2 + (n + 2), n)
                    add(G - 2, 0)
                    add(G - 1, 1)
                    dve.wait_ge(y_r, 8 + NB)


def split_biases(c, nc, dve, b, parts, rest):
    for k in range(3):
        src = b if k == 0 else rest
        c.link(dve.tensor_copy(parts[:, k, :], src[:, :]))
        if k < 2:
            c.link(dve.tensor_tensor(rest[:, :], src[:, :], parts[:, k, :], ALU.subtract))


def normalise_and_gate(r, load_experts, nc, A, X, ident, stats, mean, rstd, lnwork, epsc, gates, ps, first):
    with ExitStack() as a:
        sb, sems = named(nc, a, r.name + "g")
        gw = sb("gw", [P, NE]); gb = sb("gb", [P, NE])
        xn = sb("xn", [P, 2, GW]); xT = sb("xT", [P, 2, GW])
        chain, loaded, var_r, std_r, stat_done, xn_made, xT_ps, xT_sb, gated, row_r, ids = sems(
            "chain loaded var_r std_r stat_done xn_made xT_ps xT_sb gated row_r ids")
        X_BANK = (ps[4], ps[5])
        with nc.Block() as blk:
            @blk.sync
            def _(sp):
                sp.dma_start(gw[:, :], A["L0_ffn_gate_w"] if first else A["gate_w_T"]).then_inc(loaded, 16)
                if first:
                    sp.dma_start(gb[:, :], A["L0_ffn_gate_b"].partition_broadcast(P)).then_inc(loaded, 16)
                load_experts(sp)

            @blk.gpsimd
            def _(pool):
                for k in range(TOPK):
                    pool.iota(r.rows[:, k, :, P], pattern=[[1, NB]], base=k * NB, channel_multiplier=TOPK * NB,
                              allow_small_or_imprecise_dtypes=True).then_inc(ids, 1)

            @blk.vector
            def _(dve):
                c = Chain(dve, chain)
                ln_statistics(dve, c.link, stats, mean, rstd, lnwork, var_r, std_r, stat_done)
                dve.wait_ge(stat_done, 1)

                def normalise(g, u, fresh=False):
                    if not fresh:
                        dve.wait_ge(row_r, g - 1)
                        dve.wait_ge(xT_ps, g - 1)
                    for j in range(GB):
                        dve.tensor_scalar(xn[:, u, j * P:(j + 1) * P], X[:, g * GB + j, :],
                                          mean[:, bass.ds(g * GB + j, 1)], rstd[:, bass.ds(g * GB + j, 1)],
                                          ALU.subtract, ALU.mult).then_inc(xn_made, 1)
                    dve.wait_ge(xn_made, g * GB + GB)
                    dve.tensor_copy(r.rows[:, 1, bass.ds(g * GB, GB), 0:P],
                                    xn[:, u, :].rearrange("p (b f) -> p b f", f=P))
                normalise(0, 0, fresh=True)
                normalise(1, 1, fresh=True)
                with dve.Fori(0, (G - 2) // 2) as i:
                    for u in (0, 1):
                        normalise(i * 2 + (u + 2), u)
                dve.wait_ge(loaded, 32 if first else 16)
                dve.wait_ge(gated, G)
                lg = ps[7][:, 0:NB * NE].rearrange("p (b e) -> p b e", e=NE)
                if first:
                    c.link(dve.tensor_tensor(r.logits[:, :, :], lg, spread(gb[:, :], [P, NB, NE], 1), ALU.add))
                else:
                    c.link(dve.tensor_copy(r.logits[:, :, :], lg))

            @blk.scalar
            def _(act):
                act.wait_ge(var_r, 1)
                act.activation(lnwork[:, 3, :], lnwork[:, 2, :], ACT.Sqrt, bias=epsc[:, :], scale=1.0 / P)\
                   .then_inc(std_r, 1)

                def group(g, u, fresh=False):
                    act.wait_ge(xT_ps, g + 1)
                    if not fresh:
                        act.wait_ge(gated, g - 1)
                    act.activation(xT[:, u, :], X_BANK[u][:, :], ACT.Copy).then_inc(xT_sb, 1)
                    if r.xT is not None:
                        act.activation(r.xT[:, bass.ds(g * GB, GB), :], X_BANK[u][:, :], ACT.Copy).then_inc(xT_sb, 1)
                    act.wait_ge(xn_made, g * GB + GB)
                    act.activation(r.rows[:, 0, bass.ds(g * GB, GB), 0:P],
                                   xn[:, u, :].rearrange("p (b f) -> p b f", f=P), ACT.Copy).then_inc(row_r, 1)
                group(0, 0, fresh=True)
                group(1, 1, fresh=True)
                with act.Fori(0, (G - 2) // 2) as i:
                    for u in (0, 1):
                        group(i * 2 + (u + 2), u)

            @blk.tensor
            def _(pe):
                per = 2 if r.xT is not None else 1

                def turn(g, u, fresh=False):
                    pe.wait_ge(xn_made, g * GB + GB)
                    if not fresh:
                        pe.wait_ge(xT_sb, g * per - per)
                    for j in range(GB):
                        mm = pe.transpose(X_BANK[u][:, j * P:(j + 1) * P], xn[:, u, j * P:(j + 1) * P], ident[:, :])
                    mm.then_inc(xT_ps, 1)

                def gate(g, u):
                    pe.wait_ge(xT_sb, g * per + per)
                    for j in range(GB):
                        mm = pe.matmul(ps[7][:, bass.ds(g * (GB * NE) + j * NE, NE)], xT[:, u, j * P:(j + 1) * P],
                                       gw[:, :], start=True, stop=True)
                    mm.then_inc(gated, 1)
                pe.wait_ge(loaded, 32 if first else 16)
                turn(0, 0, fresh=True)
                turn(1, 1, fresh=True)
                with pe.Fori(0, (G - 2) // 2) as i:
                    for u in (0, 1):
                        gate(i * 2 + u, u)
                        turn(i * 2 + (u + 2), u)
                gate(G - 2, 0)
                gate(G - 1, 1)


def scatter_rows(r, xg, pool, sent):
    for b in range(NB):
        for k in range(TOPK):
            pool.indirect_dma_start(xg, bass.IndirectOffsetOnAxis(r.slots[:, k, b:b + 1], 0), r.rows[:, k, b, :],
                                    None, bounds_check=TILES * P - 1).then_inc(sent, 16)
    pool.wait_ge(sent, 16 * TOPK * NB)


AHEAD = 8
PEEL = 8


def expert_steps(eng, tiles, step):
    for t in range(PEEL):
        step(t, t % AHEAD, t)
    with eng.Fori(0, (tiles - PEEL) // AHEAD - 1) as i:
        for n in range(AHEAD):
            step(i * AHEAD + (n + PEEL), n, None)
    for t in range(tiles - AHEAD, tiles + 5):
        step(t, t % AHEAD, t)


def live(k, back, tiles):
    return k is None or 0 <= k - back < tiles


def later(k, back, n):
    return k is None or k - back >= n


class ExpertOfTile:

    def __init__(self, pe, name, tile_expert):
        self.pe, self.tile_expert = pe, tile_expert
        self.registers = [pe.alloc_register(f"{name}{q}") for q in range(AHEAD)]

    def load(self, j, q):
        self.pe.reg_load(self.registers[q], self.tile_expert[0:1, bass.ds(j, 1)])

    def of(self, q):
        return self.pe.snap(self.registers[q % AHEAD], min_val=0, max_val=NE - 1)

    def free(self):
        for reg in self.registers:
            self.pe.free_register(reg)


def rows_in(j, q):
    return (j - q) * (16 // AHEAD) + 16


def load_rows(sp, xg, rows, row_in, xT_ps, id_sb):
    with sp.Fori(1, TILES // AHEAD) as i:
        for q in range(AHEAD):
            sp.wait_ge(xT_ps, i * AHEAD + (q - AHEAD + 1))
            sp.wait_ge(id_sb, i * AHEAD + (q - AHEAD + 1))
            sp.dma_start(rows[:, q, :], xg[bass.ds(i * (AHEAD * P) + q * P, P), :]).then_inc(row_in[q], 16)


def send_outputs(pool, yg, y, yrow, y_sb, id_sb, begun, sent):
    with pool.Fori(0, TILES // AHEAD) as i:
        for n in range(AHEAD):
            pool.wait_ge(id_sb, i * AHEAD + (n + 1))
            pool.wait_ge(y_sb, i * AHEAD + (n + 1))
            pool.sem_inc(begun, 1)
            pool.indirect_dma_start(yg, bass.IndirectOffsetOnAxis(yrow[:, n:n + 1], 0), y[:, n % 4, :], None,
                                    bounds_check=TOPK * NB * P - 1, oob_is_err=False).then_inc(sent[n % 4], 16)
    for v in range(4):
        pool.wait_ge(sent[v], TILES // 4 * 16)


def take_ids(dve, j, q, k, rows, yrow, weight, row_in, sent, id_sb):
    dve.wait_ge(row_in[q], rows_in(j, q))
    if later(k, -1, 8):
        dve.wait_ge(sent[q % 4], (j - q % 4) * 4 - 16)
    dve.tensor_copy(weight[:, q:q + 1], rows[:, q, P + 1:ROW])
    dve.tensor_copy(yrow[:, q:q + 1], rows[:, q, P:P + 1]).then_inc(id_sb, 1)


class GeluWeights:

    def __init__(self, nc, stack, name):
        sb, sems = named(nc, stack, name)
        self.w1 = sb("w1", [P, NE, FF])
        self.w2 = sb("w2", [P, NE, FF // P, P])
        self.b1 = sb("b1", [3, NE, FF], BF16)
        self.b2 = sb("b2", [3, NE, P], BF16)
        self.loaded, = sems("loaded")


def load_gelu(w, biases, A, eng):
    eng.dma_start(w.w1[:, :, :], A["L0_ffn_w1"].rearrange("e d f -> d e f")).then_inc(w.loaded, 16)
    eng.dma_start(w.w2[:, :, :, :], A["L0_ffn_w2"].rearrange("e (c i) d -> i e c d", i=P)).then_inc(w.loaded, 16)
    eng.dma_start(w.b1[:, :, :], biases[:, 0:NE * FF].rearrange("k (e f) -> k e f", e=NE)).then_inc(w.loaded, 16)
    eng.dma_start(w.b2[:, :, :], biases[:, NE * FF:NE * (FF + P)].rearrange("k (e f) -> k e f", e=NE))\
       .then_inc(w.loaded, 16)


def gelu_experts(r, w, xg, yg, nc, A, X, ident, stats, mean, rstd, lnwork, epsc, gates, ps):
    with ExitStack() as a:
        sb, sems = named(nc, a, r.name + "x")
        NC = FF // P
        w1, w2, b1, b2 = w.w1, w.w2, w.b1, w.b2
        ones = sb("ones", [3, P], BF16)
        rows = sb("rows", [P, AHEAD, ROW])
        xT = sb("xT", [P, 2, P])
        g = sb("g", [P, 2, FF]); gT = sb("gT", [P, 2, FF])
        y = sb("y", [P, 4, P]); yrow = sb("yrow", [P, AHEAD], U32); weight = sb("weight", [P, AHEAD])
        ones_r, xT_ps, xT_sb, h_ps, g_sb, gT_ps, gT_sb, y_ps, y_sb, id_sb, begun = sems(
            "ones_r xT_ps xT_sb h_ps g_sb gT_ps gT_sb y_ps y_sb id_sb begun")
        row_in = sems(" ".join(f"row_in{q}" for q in range(AHEAD)))
        sent = sems("sent0 sent1 sent2 sent3")
        X_BANK, H_BANK, GT_BANK, Y_BANK = (ps[0], ps[1]), (ps[2], ps[3]), (ps[4], ps[5]), (ps[6], ps[7])
        with nc.Block() as blk:
            @blk.sync
            def _(sp):
                for q in range(AHEAD):
                    sp.dma_start(rows[:, q, :], xg[q * P:(q + 1) * P, :]).then_inc(row_in[q], 16)
                load_rows(sp, xg, rows, row_in, xT_ps, id_sb)

            @blk.scalar
            def _(act):
                def gelu(j, u, k):
                    act.wait_ge(h_ps, j + 1)
                    if later(k, 0, 2):
                        act.wait_ge(gT_ps, j - 1)
                    act.activation(g[:, u, :], H_BANK[u][:, :], ACT.Gelu).then_inc(g_sb, 1)

                def output(j, u, q, k):
                    v = q % 4
                    act.wait_ge(y_ps, j + 1)
                    act.wait_ge(id_sb, j + 1)
                    if later(k, 2, 4):
                        act.wait_ge(sent[v], (j - v) * 4)
                    act.activation(y[:, v, :], Y_BANK[u][:, 0:P], ACT.Copy, scale=weight[:, q:q + 1])\
                       .then_inc(y_sb, 1)

                def step(t, n, k):
                    if live(k, 0, TILES):
                        gelu(t, n % 2, k)
                    if live(k, 2, TILES):
                        output(t - 2, n % 2, (n - 2) % AHEAD, k)
                expert_steps(act, TILES, step)

            @blk.tensor
            def _(pe):
                expert = ExpertOfTile(pe, r.name + "expert", r.tile_expert)

                def turn(j, u, q, k):
                    pe.wait_ge(row_in[q], rows_in(j, q))
                    if later(k, -1, 2):
                        pe.wait_ge(xT_sb, j - 1)
                    pe.transpose(X_BANK[u][:, 0:P], rows[:, q, 0:P], ident[:, :]).then_inc(xT_ps, 1)

                def first_product(j, u, k, e):
                    if later(k, 0, 2):
                        pe.wait_ge(g_sb, j - 1)
                    pe.matmul(H_BANK[u][:, :], ones[:, :], b1[:, e, :], start=True, stop=False)
                    pe.wait_ge(xT_sb, j + 1)
                    pe.matmul(H_BANK[u][:, :], xT[:, u, :], w1[:, e, :], start=False, stop=True).then_inc(h_ps, 1)

                def turn_hidden(j, u, k):
                    pe.wait_ge(g_sb, j + 1)
                    if later(k, 1, 2):
                        pe.wait_ge(gT_sb, j - 1)
                    for c in range(NC):
                        mm = pe.transpose(GT_BANK[u][:, c * P:(c + 1) * P], g[:, u, c * P:(c + 1) * P], ident[:, :])
                    mm.then_inc(gT_ps, 1)

                def second_product(j, u, k, e):
                    if later(k, 2, 2):
                        pe.wait_ge(y_sb, j - 1)
                    pe.matmul(Y_BANK[u][:, 0:P], ones[:, :], b2[:, e, :], start=True, stop=False)
                    pe.wait_ge(gT_sb, j + 1)
                    for c in range(NC):
                        mm = pe.matmul(Y_BANK[u][:, 0:P], gT[:, u, c * P:(c + 1) * P], w2[:, e, c, :],
                                       start=False, stop=(c == NC - 1))
                    mm.then_inc(y_ps, 1)

                def step(t, n, k):
                    u = n % 2
                    if live(k, -1, TILES):
                        turn(t + 1, 1 - u, (n + 1) % AHEAD, k)
                    if live(k, 0, TILES):
                        first_product(t, u, k, expert.of(n))
                    if live(k, -1, TILES):
                        expert.load(t + 1, (n + 1) % AHEAD)
                    if live(k, 1, TILES):
                        turn_hidden(t - 1, 1 - u, k)
                    if live(k, 2, TILES):
                        second_product(t - 2, u, k, expert.of(n - 2))
                turn(0, 0, 0, -1)
                expert.load(0, 0)
                pe.wait_ge(w.loaded, 64)
                pe.wait_ge(ones_r, 1)
                expert_steps(pe, TILES, step)
                expert.free()

            @blk.vector
            def _(dve):
                def input_copy(j, u, k):
                    dve.wait_ge(xT_ps, j + 1)
                    if later(k, -1, 2):
                        dve.wait_ge(h_ps, j - 1)
                    dve.tensor_copy(xT[:, u, :], X_BANK[u][:, 0:P]).then_inc(xT_sb, 1)

                def hidden_copy(j, u, k):
                    dve.wait_ge(gT_ps, j + 1)
                    if later(k, 1, 2):
                        dve.wait_ge(y_ps, j - 1)
                    dve.tensor_copy(gT[:, u, :], GT_BANK[u][:, :]).then_inc(gT_sb, 1)

                def step(t, n, k):
                    u = n % 2
                    if live(k, -1, TILES):
                        input_copy(t + 1, 1 - u, k)
                        take_ids(dve, t + 1, (n + 1) % AHEAD, k, rows, yrow, weight, row_in, sent, id_sb)
                    if live(k, 1, TILES):
                        hidden_copy(t - 1, 1 - u, k)
                dve.memset(ones[:, :], 1.0).then_inc(ones_r, 1)
                input_copy(0, 0, -1)
                take_ids(dve, 0, 0, -1, rows, yrow, weight, row_in, sent, id_sb)
                expert_steps(dve, TILES, step)

            @blk.gpsimd
            def _(pool):
                send_outputs(pool, yg, y, yrow, y_sb, id_sb, begun, sent)


ALPHA = 1.702
LIMIT = 7.0


class SwigluWeights:

    def __init__(self, nc, stack, name):
        sb, sems = named(nc, stack, name)
        self.w13 = sb("w13", [P, NE + 1, FF])
        self.w2 = sb("w2", [P, NE + 1, P])
        self.b13 = sb("b13", [3, NE + 1, FF], BF16)
        self.b2 = sb("b2", [3, NE + 1, P], BF16)
        self.ones = sb("ones", [3, P], BF16)
        self.loaded, = sems("loaded")


def load_swiglu(w, biases, A, eng):
    eng.dma_start(w.w13[:, :, :], A["w13"]).then_inc(w.loaded, 16)
    eng.dma_start(w.w2[:, :, :], A["w2s"]).then_inc(w.loaded, 16)
    first = NE * (FF + P)
    second = first + (NE + 1) * FF
    eng.dma_start(w.b13[:, :, :], biases[:, first:second].rearrange("k (e f) -> k e f", f=FF)).then_inc(w.loaded, 16)
    eng.dma_start(w.b2[:, :, :], biases[:, second:second + (NE + 1) * P].rearrange("k (e f) -> k e f", f=P))\
       .then_inc(w.loaded, 16)


def swiglu_experts(r, w, nc, ident, ps, X, gate, xg, yg, shared):
    N = NB if shared else TILES
    with ExitStack() as a:
        sb, sems = named(nc, a, r.name + ("h" if shared else "x"))
        rows = sb("rows", [P, AHEAD, ROW]) if not shared else None
        xT = sb("xT", [P, 2, P])
        prod = sb("prod", [P, 2, 2 * P]); sig = sb("sig", [P, 2, P]); h1 = sb("h1", [P, 2, 2 * P])
        act_t = sb("act", [P, 2, P]); aT = sb("aT", [P, 2, P])
        y = sb("y", [P, 4, P]); yrow = sb("yrow", [P, AHEAD], U32); weight = sb("weight", [P, AHEAD])
        ones_r, xT_ps, xT_sb, h_ps, h1_r, g_r, sig_r, a_r, aT_ps, aT_sb, y_ps, y_sb, id_sb, chain, begun = sems(
            "ones_r xT_ps xT_sb h_ps h1_r g_r sig_r a_r aT_ps aT_sb y_ps y_sb id_sb chain begun")
        row_in = sems(" ".join(f"row_in{q}" for q in range(AHEAD)))
        sent = sems("sent0 sent1 sent2 sent3")
        X_BANK, H_BANK, AT_BANK, Y_BANK = (ps[0], ps[1]), (ps[2], ps[3]), (ps[4], ps[5]), (ps[6], ps[7])
        with nc.Block() as blk:
            @blk.sync
            def _(sp):
                if not shared:
                    for q in range(AHEAD):
                        sp.dma_start(rows[:, q, :], xg[q * P:(q + 1) * P, :]).then_inc(row_in[q], 16)
                    load_rows(sp, xg, rows, row_in, xT_ps, id_sb)

            @blk.scalar
            def _(act):
                def turned(j, u, k):
                    if shared:
                        if later(k, -1, 2):
                            act.wait_ge(h_ps, j - 1)
                        act.activation(xT[:, u, :], r.xT[:, j, :], ACT.Copy).then_inc(xT_sb, 1)
                        return
                    act.wait_ge(xT_ps, j + 1)
                    if later(k, -1, 2):
                        act.wait_ge(h_ps, j - 1)
                    act.activation(xT[:, u, :], X_BANK[u][:, 0:P], ACT.Copy).then_inc(xT_sb, 1)

                def sigmoid(j, u, k):
                    act.wait_ge(g_r, j + 1)
                    if later(k, 1, 2):
                        act.wait_ge(a_r, j - 1)
                    act.activation(sig[:, u, :], prod[:, u, 0:P], ACT.Sigmoid, scale=ALPHA).then_inc(sig_r, 1)

                def hidden(j, u, k):
                    act.wait_ge(aT_ps, j + 1)
                    if later(k, 3, 2):
                        act.wait_ge(y_ps, j - 1)
                    act.activation(aT[:, u, :], AT_BANK[u][:, 0:P], ACT.Copy).then_inc(aT_sb, 1)

                def first_layer(j, u, k):
                    act.wait_ge(h_ps, j + 1)
                    if later(k, 1, 2):
                        act.wait_ge(g_r, j - 1)
                    act.activation(h1[:, u, :], H_BANK[u][:, 0:2 * P], ACT.Copy).then_inc(h1_r, 1)

                def output(j, u, q, k):
                    v = q % 4
                    act.wait_ge(y_ps, j + 1)
                    act.wait_ge(id_sb, j + 1)
                    if later(k, 4, 4):
                        act.wait_ge(sent[v], (j - v) * 4)
                    act.activation(y[:, v, :], Y_BANK[u][:, 0:P], ACT.Copy, scale=weight[:, q:q + 1])\
                       .then_inc(y_sb, 1)

                def step(t, n, k):
                    u = n % 2
                    if live(k, 1, N):
                        first_layer(t - 1, 1 - u, k)
                    if live(k, 3, N):
                        hidden(t - 3, 1 - u, k)
                    if live(k, -1, N):
                        turned(t + 1, 1 - u, k)
                    if live(k, 1, N):
                        sigmoid(t - 1, 1 - u, k)
                    if live(k, 4, N) and not shared:
                        output(t - 4, u, (n - 4) % AHEAD, k)
                turned(0, 0, -1)
                expert_steps(act, N, step)

            @blk.tensor
            def _(pe):
                expert = None if shared else ExpertOfTile(pe, r.name + "expert", r.tile_expert)

                def expert_of(q):
                    return NE if shared else expert.of(q)

                def turn(j, u, q, k):
                    pe.wait_ge(row_in[q], rows_in(j, q))
                    if later(k, -1, 2):
                        pe.wait_ge(xT_sb, j - 1)
                    pe.transpose(X_BANK[u][:, 0:P], rows[:, q, 0:P], ident[:, :]).then_inc(xT_ps, 1)

                def first_product(j, u, k, e):
                    if later(k, 0, 2):
                        pe.wait_ge(g_r, j - 1)
                    pe.matmul(H_BANK[u][:, :], w.ones[:, :], w.b13[:, e, :], start=True, stop=False)
                    pe.wait_ge(xT_sb, j + 1)
                    pe.matmul(H_BANK[u][:, :], xT[:, u, :], w.w13[:, e, :], start=False, stop=True).then_inc(h_ps, 1)

                def turn_hidden(j, u, k):
                    pe.wait_ge(a_r, j + 1)
                    if later(k, 3, 2):
                        pe.wait_ge(aT_sb, j - 1)
                    pe.transpose(AT_BANK[u][:, 0:P], act_t[:, u, :], ident[:, :]).then_inc(aT_ps, 1)

                def second_product(j, u, k, e):
                    if later(k, 3, 2):
                        pe.wait_ge(y_sb, j - 1)
                    pe.matmul(Y_BANK[u][:, 0:P], w.ones[:, :], w.b2[:, e, :], start=True, stop=False)
                    pe.wait_ge(aT_sb, j + 1)
                    pe.matmul(Y_BANK[u][:, 0:P], aT[:, u, :], w.w2[:, e, :], start=False, stop=True).then_inc(y_ps, 1)

                def step(t, n, k):
                    u = n % 2
                    if live(k, 3, N):
                        turn_hidden(t - 3, 1 - u, k)
                    if live(k, -1, N) and not shared:
                        turn(t + 1, 1 - u, (n + 1) % AHEAD, k)
                    if live(k, -1, N) and not shared:
                        expert.load(t + 1, (n + 1) % AHEAD)
                    if live(k, 0, N):
                        first_product(t, u, k, expert_of(n))
                    if live(k, 3, N):
                        second_product(t - 3, 1 - u, k, expert_of(n - 3))
                if shared:
                    pe.wait_ge(w.loaded, 64)
                    pe.wait_ge(ones_r, 1)
                else:
                    turn(0, 0, 0, -1)
                    expert.load(0, 0)
                expert_steps(pe, N, step)
                if not shared:
                    expert.free()

            @blk.vector
            def _(dve):
                def product(j, u):
                    c = Chain(dve, chain, j * 3)
                    dve.wait_ge(h1_r, j + 1)
                    return c, c.mark(dve.tensor_tensor(prod[:, u, :], h1[:, u, :], H_BANK[u][:, 2 * P:4 * P],
                                                       ALU.mult))

                def gate_values(c, made, j, u):
                    g, l = prod[:, u, 0:P], prod[:, u, P:2 * P]
                    c.need(made)
                    dve.tensor_scalar(g, g, LIMIT, None, ALU.min).then_inc(g_r, 1)
                    c.link(dve.tensor_scalar(l, l, LIMIT, -LIMIT, ALU.min, ALU.max))
                    dve.wait_ge(g_r, j + 1)
                    c.mark(dve.scalar_tensor_tensor(l, l, 1.0, g, ALU.add, ALU.mult))

                def activate(j, u, k):
                    dve.wait_ge(sig_r, j + 1)
                    dve.wait_ge(chain, j * 3 + 3)
                    if later(k, 2, 2):
                        dve.wait_ge(aT_ps, j - 1)
                    dve.tensor_tensor(act_t[:, u, :], prod[:, u, P:2 * P], sig[:, u, :], ALU.mult).then_inc(a_r, 1)

                def add(j, u):
                    dve.wait_ge(y_ps, j + 1)
                    dve.scalar_tensor_tensor(X[:, j, :], Y_BANK[u][:, 0:P], gate, X[:, j, :], ALU.mult, ALU.add)\
                       .then_inc(y_sb, 1)

                def step(t, n, k):
                    u = n % 2
                    if live(k, -1, N) and not shared:
                        take_ids(dve, t + 1, (n + 1) % AHEAD, k, rows, yrow, weight, row_in, sent, id_sb)
                    if live(k, 1, N):
                        c, made = product(t - 1, 1 - u)
                    if live(k, 2, N):
                        activate(t - 2, u, k)
                    if live(k, 4, N) and shared:
                        add(t - 4, u)
                    if live(k, 1, N):
                        gate_values(c, made, t - 1, 1 - u)
                if shared:
                    dve.memset(w.ones[:, :], 1.0).then_inc(ones_r, 1)
                else:
                    take_ids(dve, 0, 0, -1, rows, yrow, weight, row_in, sent, id_sb)
                expert_steps(dve, N, step)

            @blk.gpsimd
            def _(pool):
                if shared:
                    scatter_rows(r, xg, pool, sent[0])
                else:
                    send_outputs(pool, yg, y, yrow, y_sb, id_sb, begun, sent)


def combine(r, yg, nc, A, X, ident, stats, mean, rstd, lnwork, epsc, gates, ps, out=None):
    W = 8
    with ExitStack() as a:
        sb, sems = named(nc, a, r.name + "c")
        y = sb("y", [P, NB // W, TOPK, W, P])
        chain, stored, y_ready = sems("chain stored y_ready")
        y_in = sems(" ".join(f"y_in{n}" for n in range(NB // W)))
        with nc.Block() as blk:
            @blk.sync
            def _(sp):
                places = yg.rearrange("(p k b) f -> p k b f", k=TOPK, b=NB)
                for n in range(NB // W):
                    sp.dma_start(y[:, n, :, :, :], places[:, :, n * W:(n + 1) * W, :]).then_inc(y_in[n], 16)
                for n in range(NB // W):
                    sp.wait_ge(y_in[n], 16)
                    sp.sem_inc(y_ready, 1)
                if out is not None:
                    for n in range(NB // W):
                        sp.wait_ge(chain, (n + 1) * TOPK)
                        sp.dma_start(out[:, n * W:(n + 1) * W, :], X[:, n * W:(n + 1) * W, :]).then_inc(stored, 16)
                    sp.wait_ge(stored, 16 * (NB // W))

            @blk.vector
            def _(dve):
                with dve.Fori(0, NB // W) as n:
                    dve.wait_ge(y_ready, n + 1)
                    c = Chain(dve, chain, n * TOPK)
                    for k in range(TOPK):
                        xs = X[:, bass.ds(n * W, W), :]
                        c.link(dve.tensor_tensor(xs, xs, y[:, bass.ds(n, 1), k, :, :].squeeze(1), ALU.add))
                    if out is None:
                        for j in range(W):
                            dve.bn_stats(stats[:, n * W + j, :], X[:, n * W + j, :])


DIRECT = (
    "L0_ffn_alpha", "L0_ffn_gate_b", "L0_ffn_gate_w", "L0_ffn_w1", "L0_ffn_w2", "L0_xattn_Wk", "L0_xattn_Wo",
    "L0_xattn_Wq", "L0_xattn_Wv", "L0_xattn_bk", "L0_xattn_bo", "L0_xattn_bq", "L0_xattn_bv", "L1_ffn_gate_b",
    "g_ffn", "g_xattn",
)


def layout(inputs):
    import numpy as np
    arrays = {name: inputs[name] for name in DIRECT}
    arrays["ctx_T"] = np.ascontiguousarray(inputs["ctx_768"].transpose(2, 0, 1))

    def get(name):
        return inputs["L1_xattn_" + name]

    def side_by_side(w):
        return w.T.reshape(-1, P, w.shape[0]).transpose(1, 0, 2).reshape(P, -1)
    d2v = np.pad(get("W_d2v"), ((0, 0), (0, P - CC)))
    arrays["bit_weights"] = np.ascontiguousarray(np.concatenate(
        [side_by_side(w) for w in (d2v, get("W_img"), get("W_txt"), get("W_att0"), get("W_att1"), get("W_f1"),
                                   get("W_f2"))], axis=1))
    twice = [np.tile(get(n), 2) for n in ("b_att0", "b_att1")]
    arrays["bit_bias"] = np.ascontiguousarray(np.stack(
        [get("b_d2v"), get("b_img"), get("b_txt")] + twice + list(get("b_f1").reshape(4, P)), axis=1))
    arrays["bit_rowbias"] = np.stack(twice + [get("b_f2")])

    def with_shared(name):
        return np.concatenate([inputs["L1_ffn_" + name], inputs["L1_ffn_s" + name][None]])

    def even_odd(w):
        return np.concatenate([w[:, 0::2], w[:, 1::2]], axis=1)
    w13 = np.concatenate([even_odd(with_shared("w1")), even_odd(with_shared("w3"))], axis=1)
    arrays["w13"] = np.ascontiguousarray(w13.transpose(2, 0, 1))
    b13 = np.concatenate([even_odd(with_shared("b1")), even_odd(with_shared("b3"))], axis=1)
    arrays["w2s"] = np.ascontiguousarray(with_shared("w2").transpose(2, 0, 1))
    arrays["x_T"] = np.ascontiguousarray(inputs["x"].transpose(1, 0, 2))
    arrays["biases"] = np.ascontiguousarray(np.concatenate(
        [inputs["L0_ffn_b1"].ravel(), inputs["L0_ffn_b2"].ravel(), b13.ravel(),
         with_shared("b2").ravel()]).reshape(P, -1))
    arrays["gate_w_T"] = np.ascontiguousarray(inputs["L1_ffn_gate_w"].T)
    return arrays


def kernel(**inputs):
    import numpy as np
    from concourse import bacc
    from concourse.bass_utils import run_bass_kernel_spmd

    arrays = {"in_" + name: np.ascontiguousarray(a)
              for name, a in layout({name: np.asarray(a) for name, a in inputs.items()}).items()}
    nc = bacc.Bacc("TRN2", target_bir_lowering=False, num_devices=1)
    A = {name[3:]: nc.dram_tensor(name, a.shape, mybir.dt.from_np(a.dtype), kind="ExternalInput").ap()
         for name, a in arrays.items()}
    out = nc.dram_tensor("out", (P, NB, P), F32, kind="ExternalOutput").ap()
    build(nc, A, out)
    result = run_bass_kernel_spmd(nc, [arrays], core_ids=[0])
    return np.ascontiguousarray(result.results[0]["out"].transpose(1, 0, 2))
```
